# Optimizing a Trainium2 kernel written in Bass

```python
import numpy as np
import jax
import jax.numpy as jnp

def _softmax(x, axis=-1):
    return jax.nn.softmax(x, axis=axis)

def _gelu(x):
    return jax.nn.gelu(x, approximate=True)

def _silu(x):
    return jax.nn.silu(x)

def _sigmoid(x):
    return jax.nn.sigmoid(x)

def _layernorm(x, axis=-1, eps=1e-05):
    m = jnp.mean(x, axis=axis, keepdims=True)
    v = jnp.var(x, axis=axis, keepdims=True)
    return (x - m) / jnp.sqrt(v + eps)

def _scatter_add(tgt, idx, src, axis=0):
    return tgt.at[idx].add(src)

def _segment_sum(src, seg, n):
    return jax.ops.segment_sum(src, seg, n)
kernel_name = 'mk_decoder_preln_d1_seqx_r8_e14f62'

def setup_inputs(seed: int=0):
    np.random.seed(seed)
    _w = jnp.asarray

    def _rec_inputs():
        import jax
        import jax.numpy as jnp
        _rk = jax.random.key(seed)
        x = -0.0002928 + 1 * jax.random.normal(jax.random.fold_in(_rk, 1), (16, 256, 128), jnp.float32)
        _lenS = 256 - jax.random.randint(jax.random.fold_in(_rk, 7), (16,), 0, max(1, 256 // 4) + 1, jnp.int32)
        _lenS2 = 64 - jax.random.randint(jax.random.fold_in(_rk, 8), (16,), 0, max(1, 64 // 4) + 1, jnp.int32)
        _ctx_768P = jax.random.normal(jax.random.fold_in(_rk, 11), (16, 16, 96), jnp.float32)
        _ctx_768c = jax.random.dirichlet(jax.random.fold_in(_rk, 511), 0.3 * jnp.ones((16,), jnp.float32), (16, 64))
        _ctx_768t = jnp.einsum('bsk,bkd->bsd', _ctx_768c, _ctx_768P)
        _ctx_768t = _ctx_768t * jax.lax.rsqrt(jnp.mean(jnp.square(_ctx_768t)) + 1e-12) * 0.953939
        ctx_768 = 2.09791e-05 + 1.00001 * (_ctx_768t + 0.3 * jax.random.normal(jax.random.fold_in(_rk, 611), (16, 64, 96), jnp.float32))
        return (x, ctx_768)
    x, ctx_768 = _rec_inputs()

    def _L0_attn_setup():
        import jax, jax.numpy as jnp
        import numpy as np
        import math
        B, L, D = (2, 512, 128)
        H, DK, DV = (4, 32, 32)
        CHUNK = 32
        PROB_FLOOR = 0.02

        def _l2norm(x, eps=1e-06):
            return x * jax.lax.rsqrt(jnp.sum(x * x, -1, keepdims=True) + eps)

        def _silu(x):
            return x * jax.nn.sigmoid(x)

        def _short_conv(x, w):
            K = w.shape[-1]
            xp = jnp.pad(x, ((0, 0), (K - 1, 0), (0, 0)))
            y = sum((xp[:, j:j + x.shape[1], :] * w[:, j] for j in range(K)))
            return _silu(y)

        def _fir_conv(x, filt):
            b, l, h, d = x.shape
            K = filt.shape[-1]
            xf = jnp.pad(x.reshape(b, l, h * d).transpose(0, 2, 1), ((0, 0), (0, 0), (K - 1, 0)))
            w = filt.reshape(h * d, 1, K)
            y = jax.lax.conv_general_dilated(xf, w, (1,), 'VALID', dimension_numbers=('NCH', 'OIH', 'NCH'), feature_group_count=h * d)
            return y.transpose(0, 2, 1).reshape(b, l, h, d)

        def _delta_rule_chunkwise(q, k, v, beta, chunk=CHUNK):
            b, h, Lq, dk = q.shape
            dv = v.shape[-1]
            n = Lq // chunk
            q = _l2norm(q)
            k = _l2norm(k)
            v = v * beta[..., None]
            kb = k * beta[..., None]
            rs = lambda t: t.reshape(b, h, n, chunk, t.shape[-1])
            qc, kc, vc, kbc = (rs(q), rs(k), rs(v), rs(kb))
            strict_lower = jnp.tril(jnp.ones((chunk, chunk), bool), -1)
            M = jnp.where(strict_lower, jnp.einsum('bhncd,bhnmd->bhncm', kbc, kc), 0.0)
            eye = jnp.eye(chunk, dtype=q.dtype)
            T = jax.scipy.linalg.solve_triangular(eye + M, jnp.broadcast_to(eye, M.shape), lower=True, unit_diagonal=True)
            u = T @ vc
            w = T @ kbc
            incl_lower = jnp.tril(jnp.ones((chunk, chunk), bool), 0)

            def step(S, xs):
                q_i, k_i, u_i, w_i = xs
                attn = jnp.where(incl_lower, q_i @ k_i.swapaxes(-1, -2), 0.0)
                u_adj = u_i - w_i @ S
                out_i = q_i @ S + attn @ u_adj
                S = S + k_i.swapaxes(-1, -2) @ u_adj
                return (S, out_i)
            S0 = jnp.zeros((b, h, dk, dv), q.dtype)
            xs = tuple((jnp.moveaxis(t, 2, 0) for t in (qc, kc, u, w)))
            S, out = jax.lax.scan(step, S0, xs)
            out = jnp.moveaxis(out, 0, 2).reshape(b, h, Lq, dv)
            return (out, S)

        def _rmsnorm(x, w, eps=1e-05):
            return x * jax.lax.rsqrt(jnp.mean(x * x, -1, keepdims=True) + eps) * w

        def _per_head_stats(x):
            mean = jnp.mean(x, -1, keepdims=True)
            var = jnp.var(x, -1, keepdims=True)
            am = jnp.mean(jnp.abs(x), -1, keepdims=True)
            l2 = jnp.sqrt(jnp.sum(x * x, -1, keepdims=True))
            return jnp.concatenate([mean, var, am, l2], -1)

        def _forward(hidden_states, q_w, k_w, v_w, b_w, q_cw, k_cw, v_cw, fir_short_w, fir_long_w, mlp1_w, mlp1_b, mlp2_w, mlp2_b, logit_temp, conv_res_logit, norm_w, o_w):
            b, l, _ = hidden_states.shape
            q_in = _short_conv(hidden_states @ q_w.T, q_cw)
            k_in = _short_conv(hidden_states @ k_w.T, k_cw)
            v_in = _short_conv(hidden_states @ v_w.T, v_cw)
            q = q_in.reshape(b, l, H, DK)
            k = k_in.reshape(b, l, H, DK)
            v_direct = v_in.reshape(b, l, H, DV)
            beta = jnp.maximum(jax.nn.sigmoid(hidden_states @ b_w.T), 1e-06)
            delta_out, _S = _delta_rule_chunkwise(q.transpose(0, 2, 1, 3), k.transpose(0, 2, 1, 3), v_direct.transpose(0, 2, 1, 3), beta.transpose(0, 2, 1))
            delta_out = delta_out.transpose(0, 2, 1, 3)
            local_short = _fir_conv(v_direct, fir_short_w)
            local_long = _fir_conv(v_direct, fir_long_w)
            stats = jnp.concatenate([_per_head_stats(local_short), _per_head_stats(local_long), _per_head_stats(delta_out), _per_head_stats(v_direct)], -1)
            hs_exp = jnp.broadcast_to(hidden_states[:, :, None, :], (b, l, H, hidden_states.shape[-1]))
            gate_in = jnp.concatenate([hs_exp, stats], -1)
            h1 = jax.nn.gelu(gate_in @ mlp1_w.T + mlp1_b)
            logits = h1 @ mlp2_w.T + mlp2_b
            temp = jax.nn.softplus(logit_temp)
            p = jax.nn.softmax(logits / temp, -1)
            p = jnp.maximum(p, PROB_FLOOR)
            p = p / jnp.sum(p, -1, keepdims=True)
            o = p[..., 0:1] * local_short + p[..., 1:2] * local_long + p[..., 2:3] * delta_out + p[..., 3:4] * v_direct
            o = o + jax.nn.sigmoid(conv_res_logit)[None, None, :, None] * local_short
            o = _rmsnorm(o, norm_w)
            o = o.reshape(b, l, H * DV) @ o_w.T
            return o
        key = jax.random.key(seed)
        ks = jax.random.split(key, 16)
        s = 0.02
        hidden_gate = D * 2 // 2
        gate_in_dim = D + 16
        inp = {'hidden_states': jax.random.normal(ks[0], (B, L, D), jnp.float32), 'q_w': jax.random.normal(ks[1], (D, D), jnp.float32) * s, 'k_w': jax.random.normal(ks[2], (D, D), jnp.float32) * s, 'v_w': jax.random.normal(ks[3], (D, D), jnp.float32) * s, 'b_w': jax.random.normal(ks[4], (H, D), jnp.float32) * s, 'q_cw': jax.random.normal(ks[5], (D, 4), jnp.float32) * s, 'k_cw': jax.random.normal(ks[6], (D, 4), jnp.float32) * s, 'v_cw': jax.random.normal(ks[7], (D, 4), jnp.float32) * s, 'fir_short_w': jax.random.normal(ks[8], (H, DV, 5), jnp.float32) * s, 'fir_long_w': jax.random.normal(ks[9], (H, DV, 64), jnp.float32) * s, 'mlp1_w': jax.random.normal(ks[10], (hidden_gate, gate_in_dim), jnp.float32) * s, 'mlp1_b': jnp.zeros((hidden_gate,), jnp.float32), 'mlp2_w': jax.random.normal(ks[11], (4, hidden_gate), jnp.float32) * s, 'mlp2_b': jnp.array([-0.5, -0.5, 1.0, 3.0], jnp.float32), 'logit_temp': jnp.full((1,), math.log(math.expm1(0.7)), jnp.float32), 'conv_res_logit': jnp.full((H,), -2.0, jnp.float32), 'norm_w': jnp.ones((DV,), jnp.float32), 'o_w': jax.random.normal(ks[12], (D, D), jnp.float32) * s}
        return inp
    _L0_attn_all = _L0_attn_setup()
    _L0_attn_in = {k: v for k, v in _L0_attn_all.items() if k in ('q_w', 'k_w', 'v_w', 'b_w', 'q_cw', 'k_cw', 'v_cw', 'fir_short_w', 'fir_long_w', 'mlp1_w', 'mlp1_b', 'mlp2_w', 'mlp2_b', 'logit_temp', 'conv_res_logit', 'norm_w', 'o_w')}
    del _L0_attn_all

    def _L0_xattn_setup():
        import jax, jax.numpy as jnp
        import numpy as np
        N_HEADS = 16
        D_HEAD = 64
        key = jax.random.key(seed)
        ks = jax.random.split(key, 7)
        B, SQ, SKV = (2, 256, 256)
        D_MODEL, D_COND, D_ATTN = (128, 96, N_HEADS * D_HEAD)
        return {'x': jax.random.normal(ks[0], (B, SQ, D_MODEL), jnp.float32), 'cond': jax.random.normal(ks[1], (B, SKV, D_COND), jnp.float32), 'w_q': jax.random.normal(ks[2], (D_MODEL, D_ATTN), jnp.float32) * D_MODEL ** (-0.5), 'w_k': jax.random.normal(ks[3], (D_COND, D_ATTN), jnp.float32) * D_COND ** (-0.5), 'w_v': jax.random.normal(ks[4], (D_COND, D_ATTN), jnp.float32) * D_COND ** (-0.5), 'w_out': jax.random.normal(ks[5], (D_ATTN, D_MODEL), jnp.float32) * D_ATTN ** (-0.5), 'b_out': jnp.zeros((D_MODEL,), jnp.float32)}
    _L0_xattn_all = _L0_xattn_setup()
    _L0_xattn_in = {k: v for k, v in _L0_xattn_all.items() if k in ('w_q', 'w_k', 'w_v', 'w_out', 'b_out')}
    del _L0_xattn_all

    def _L0_ffn_setup():
        import jax, jax.numpy as jnp
        import numpy as np
        B, S, D, E, F, TOP_K = (4, 256, 128, 8, 512, 2)
        key = jax.random.key(seed)
        k0, k1, k2, k3 = jax.random.split(key, 4)
        init = lambda k, shape, fan: (jax.random.normal(k, shape, jnp.float32) / np.sqrt(fan)).astype(jnp.float32)
        return {'x': jax.random.normal(k0, (B, S, D), jnp.float32), 'gate_w': init(k1, (D, E), D), 'w1': init(k2, (E, D, F), D), 'b1': jnp.zeros((E, F), jnp.float32), 'w2': init(k3, (E, F, D), F), 'b2': jnp.zeros((E, D), jnp.float32)}
    _L0_ffn_all = _L0_ffn_setup()
    _L0_ffn_in = {k: v for k, v in _L0_ffn_all.items() if k in ('gate_w', 'w1', 'b1', 'w2', 'b2')}
    del _L0_ffn_all
    return {'x': x, 'ctx_768': ctx_768, 'L0_attn_q_w': _L0_attn_in['q_w'], 'L0_attn_k_w': _L0_attn_in['k_w'], 'L0_attn_v_w': _L0_attn_in['v_w'], 'L0_attn_b_w': _L0_attn_in['b_w'], 'L0_attn_q_cw': _L0_attn_in['q_cw'], 'L0_attn_k_cw': _L0_attn_in['k_cw'], 'L0_attn_v_cw': _L0_attn_in['v_cw'], 'L0_attn_fir_short_w': _L0_attn_in['fir_short_w'], 'L0_attn_fir_long_w': _L0_attn_in['fir_long_w'], 'L0_attn_mlp1_w': _L0_attn_in['mlp1_w'], 'L0_attn_mlp1_b': _L0_attn_in['mlp1_b'], 'L0_attn_mlp2_w': _L0_attn_in['mlp2_w'], 'L0_attn_mlp2_b': _L0_attn_in['mlp2_b'], 'L0_attn_logit_temp': _L0_attn_in['logit_temp'], 'L0_attn_conv_res_logit': _L0_attn_in['conv_res_logit'], 'L0_attn_norm_w': _L0_attn_in['norm_w'], 'L0_attn_o_w': _L0_attn_in['o_w'], 'L0_xattn_w_q': _L0_xattn_in['w_q'], 'L0_xattn_w_k': _L0_xattn_in['w_k'], 'L0_xattn_w_v': _L0_xattn_in['w_v'], 'L0_xattn_w_out': _L0_xattn_in['w_out'], 'L0_xattn_b_out': _L0_xattn_in['b_out'], 'L0_ffn_gate_w': _L0_ffn_in['gate_w'], 'L0_ffn_w1': _L0_ffn_in['w1'], 'L0_ffn_b1': _L0_ffn_in['b1'], 'L0_ffn_w2': _L0_ffn_in['w2'], 'L0_ffn_b2': _L0_ffn_in['b2']}

def reference(x, ctx_768, L0_attn_q_w, L0_attn_k_w, L0_attn_v_w, L0_attn_b_w, L0_attn_q_cw, L0_attn_k_cw, L0_attn_v_cw, L0_attn_fir_short_w, L0_attn_fir_long_w, L0_attn_mlp1_w, L0_attn_mlp1_b, L0_attn_mlp2_w, L0_attn_mlp2_b, L0_attn_logit_temp, L0_attn_conv_res_logit, L0_attn_norm_w, L0_attn_o_w, L0_xattn_w_q, L0_xattn_w_k, L0_xattn_w_v, L0_xattn_w_out, L0_xattn_b_out, L0_ffn_gate_w, L0_ffn_w1, L0_ffn_b1, L0_ffn_w2, L0_ffn_b2):
    import jax
    import jax.numpy as jnp

    def _L0_attn_ref(hidden_states, q_w, k_w, v_w, b_w, q_cw, k_cw, v_cw, fir_short_w, fir_long_w, mlp1_w, mlp1_b, mlp2_w, mlp2_b, logit_temp, conv_res_logit, norm_w, o_w):
        import jax, jax.numpy as jnp
        import numpy as np
        import math
        B, L, D = (2, 512, 128)
        H, DK, DV = (4, 32, 32)
        CHUNK = 32
        PROB_FLOOR = 0.02

        def _l2norm(x, eps=1e-06):
            return x * jax.lax.rsqrt(jnp.sum(x * x, -1, keepdims=True) + eps)

        def _silu(x):
            return x * jax.nn.sigmoid(x)

        def _short_conv(x, w):
            K = w.shape[-1]
            xp = jnp.pad(x, ((0, 0), (K - 1, 0), (0, 0)))
            y = sum((xp[:, j:j + x.shape[1], :] * w[:, j] for j in range(K)))
            return _silu(y)

        def _fir_conv(x, filt):
            b, l, h, d = x.shape
            K = filt.shape[-1]
            xf = jnp.pad(x.reshape(b, l, h * d).transpose(0, 2, 1), ((0, 0), (0, 0), (K - 1, 0)))
            w = filt.reshape(h * d, 1, K)
            y = jax.lax.conv_general_dilated(xf, w, (1,), 'VALID', dimension_numbers=('NCH', 'OIH', 'NCH'), feature_group_count=h * d)
            return y.transpose(0, 2, 1).reshape(b, l, h, d)

        def _delta_rule_chunkwise(q, k, v, beta, chunk=CHUNK):
            b, h, Lq, dk = q.shape
            dv = v.shape[-1]
            n = Lq // chunk
            q = _l2norm(q)
            k = _l2norm(k)
            v = v * beta[..., None]
            kb = k * beta[..., None]
            rs = lambda t: t.reshape(b, h, n, chunk, t.shape[-1])
            qc, kc, vc, kbc = (rs(q), rs(k), rs(v), rs(kb))
            strict_lower = jnp.tril(jnp.ones((chunk, chunk), bool), -1)
            M = jnp.where(strict_lower, jnp.einsum('bhncd,bhnmd->bhncm', kbc, kc), 0.0)
            eye = jnp.eye(chunk, dtype=q.dtype)
            T = jax.scipy.linalg.solve_triangular(eye + M, jnp.broadcast_to(eye, M.shape), lower=True, unit_diagonal=True)
            u = T @ vc
            w = T @ kbc
            incl_lower = jnp.tril(jnp.ones((chunk, chunk), bool), 0)

            def step(S, xs):
                q_i, k_i, u_i, w_i = xs
                attn = jnp.where(incl_lower, q_i @ k_i.swapaxes(-1, -2), 0.0)
                u_adj = u_i - w_i @ S
                out_i = q_i @ S + attn @ u_adj
                S = S + k_i.swapaxes(-1, -2) @ u_adj
                return (S, out_i)
            S0 = jnp.zeros((b, h, dk, dv), q.dtype)
            xs = tuple((jnp.moveaxis(t, 2, 0) for t in (qc, kc, u, w)))
            S, out = jax.lax.scan(step, S0, xs)
            out = jnp.moveaxis(out, 0, 2).reshape(b, h, Lq, dv)
            return (out, S)

        def _rmsnorm(x, w, eps=1e-05):
            return x * jax.lax.rsqrt(jnp.mean(x * x, -1, keepdims=True) + eps) * w

        def _per_head_stats(x):
            mean = jnp.mean(x, -1, keepdims=True)
            var = jnp.var(x, -1, keepdims=True)
            am = jnp.mean(jnp.abs(x), -1, keepdims=True)
            l2 = jnp.sqrt(jnp.sum(x * x, -1, keepdims=True))
            return jnp.concatenate([mean, var, am, l2], -1)

        def _forward(hidden_states, q_w, k_w, v_w, b_w, q_cw, k_cw, v_cw, fir_short_w, fir_long_w, mlp1_w, mlp1_b, mlp2_w, mlp2_b, logit_temp, conv_res_logit, norm_w, o_w):
            b, l, _ = hidden_states.shape
            q_in = _short_conv(hidden_states @ q_w.T, q_cw)
            k_in = _short_conv(hidden_states @ k_w.T, k_cw)
            v_in = _short_conv(hidden_states @ v_w.T, v_cw)
            q = q_in.reshape(b, l, H, DK)
            k = k_in.reshape(b, l, H, DK)
            v_direct = v_in.reshape(b, l, H, DV)
            beta = jnp.maximum(jax.nn.sigmoid(hidden_states @ b_w.T), 1e-06)
            delta_out, _S = _delta_rule_chunkwise(q.transpose(0, 2, 1, 3), k.transpose(0, 2, 1, 3), v_direct.transpose(0, 2, 1, 3), beta.transpose(0, 2, 1))
            delta_out = delta_out.transpose(0, 2, 1, 3)
            local_short = _fir_conv(v_direct, fir_short_w)
            local_long = _fir_conv(v_direct, fir_long_w)
            stats = jnp.concatenate([_per_head_stats(local_short), _per_head_stats(local_long), _per_head_stats(delta_out), _per_head_stats(v_direct)], -1)
            hs_exp = jnp.broadcast_to(hidden_states[:, :, None, :], (b, l, H, hidden_states.shape[-1]))
            gate_in = jnp.concatenate([hs_exp, stats], -1)
            h1 = jax.nn.gelu(gate_in @ mlp1_w.T + mlp1_b)
            logits = h1 @ mlp2_w.T + mlp2_b
            temp = jax.nn.softplus(logit_temp)
            p = jax.nn.softmax(logits / temp, -1)
            p = jnp.maximum(p, PROB_FLOOR)
            p = p / jnp.sum(p, -1, keepdims=True)
            o = p[..., 0:1] * local_short + p[..., 1:2] * local_long + p[..., 2:3] * delta_out + p[..., 3:4] * v_direct
            o = o + jax.nn.sigmoid(conv_res_logit)[None, None, :, None] * local_short
            o = _rmsnorm(o, norm_w)
            o = o.reshape(b, l, H * DV) @ o_w.T
            return o
        return _forward(hidden_states, q_w, k_w, v_w, b_w, q_cw, k_cw, v_cw, fir_short_w, fir_long_w, mlp1_w, mlp1_b, mlp2_w, mlp2_b, logit_temp, conv_res_logit, norm_w, o_w)

    def _L0_xattn_ref(x, cond, w_q, w_k, w_v, w_out, b_out):
        import jax, jax.numpy as jnp
        import numpy as np
        N_HEADS = 16
        D_HEAD = 64
        B, SQ, _ = x.shape
        SKV = cond.shape[1]
        scale = D_HEAD ** (-0.5)
        q = (x @ w_q).reshape(B, SQ, N_HEADS, D_HEAD)
        k = (cond @ w_k).reshape(B, SKV, N_HEADS, D_HEAD)
        v = (cond @ w_v).reshape(B, SKV, N_HEADS, D_HEAD)
        attn = jnp.einsum('bqhd,bkhd->bhqk', q, k) * scale
        attn = jax.nn.softmax(attn, axis=-1)
        out = jnp.einsum('bhqk,bkhd->bqhd', attn, v).reshape(B, SQ, N_HEADS * D_HEAD)
        return out @ w_out + b_out

    def _L0_ffn_ref(x, gate_w, w1, b1, w2, b2):
        import jax, jax.numpy as jnp
        import numpy as np
        B, S, D, E, F, TOP_K = (4, 256, 128, 8, 512, 2)
        b, s, d = x.shape
        e = gate_w.shape[1]
        xf = x.reshape(-1, d)
        t = xf.shape[0]
        logits = xf @ gate_w
        top_w, top_idx = jax.lax.top_k(logits, TOP_K)
        top_w = jax.nn.softmax(top_w.astype(jnp.float32), axis=-1).astype(x.dtype)
        combine = jnp.zeros((t, e), x.dtype).at[jnp.arange(t)[:, None], top_idx].add(top_w)
        h = jax.nn.gelu(jnp.einsum('td,edf->tef', xf, w1) + b1, approximate=False)
        y = jnp.einsum('tef,efd->ted', h, w2) + b2
        out = jnp.einsum('ted,te->td', y, combine)
        return out.reshape(b, s, d)
    x = x + _L0_attn_ref(_layernorm(x, axis=-1), L0_attn_q_w, L0_attn_k_w, L0_attn_v_w, L0_attn_b_w, L0_attn_q_cw, L0_attn_k_cw, L0_attn_v_cw, L0_attn_fir_short_w, L0_attn_fir_long_w, L0_attn_mlp1_w, L0_attn_mlp1_b, L0_attn_mlp2_w, L0_attn_mlp2_b, L0_attn_logit_temp, L0_attn_conv_res_logit, L0_attn_norm_w, L0_attn_o_w)
    x = x + _L0_xattn_ref(_layernorm(x, axis=-1), ctx_768, L0_xattn_w_q, L0_xattn_w_k, L0_xattn_w_v, L0_xattn_w_out, L0_xattn_b_out)
    x = x + _L0_ffn_ref(_layernorm(x, axis=-1), L0_ffn_gate_w, L0_ffn_w1, L0_ffn_b1, L0_ffn_w2, L0_ffn_b2)
    return x

_drawn_inputs = setup_inputs


def setup_inputs(seed=0):
    import zlib

    import numpy as np

    out = dict(_drawn_inputs(seed))
    spreads = {'L0_attn_mlp1_b': (0.0, 0.8),
     'L0_attn_conv_res_logit': (-2.0, 0.6),
     'L0_attn_norm_w': (1.0, 0.2),
     'L0_xattn_b_out': (0.0, 0.1),
     'L0_ffn_b1': (0.0, 0.1),
     'L0_ffn_b2': (0.0, 0.1)}
    factors = {'L0_attn_q_w': 2.986,
     'L0_attn_k_w': 3.166,
     'L0_attn_b_w': 7.749,
     'L0_attn_q_cw': 2.968,
     'L0_attn_k_cw': 2.842,
     'L0_attn_fir_short_w': 8.0,
     'L0_attn_fir_long_w': 8.0,
     'L0_attn_mlp1_w': 8.0,
     'L0_attn_mlp2_w': 8.0}
    for name, (base, spread) in spreads.items():
        noise = np.random.default_rng([zlib.crc32(name.encode()), seed]).standard_normal(out[name].shape)
        drawn = base * np.exp(spread * noise) if base else spread * noise
        out[name] = jnp.asarray(drawn.astype(out[name].dtype))
    for name, factor in factors.items():
        out[name] = (out[name] * factor).astype(out[name].dtype)
    return out
```

```python
from contextlib import ExitStack, contextmanager

import concourse.bass as bass
from concourse import mybir

F32 = mybir.dt.float32
F16 = mybir.dt.float16
I32 = mybir.dt.int32
ALU = mybir.AluOpType
ACT = mybir.ActivationFunctionType
AX = mybir.AxisListType

P = 128
B, L, D = 16, 256, 128
TILES = B * L // P
H, DH = 4, 32
C = 32
CT = P // C
NCH = L // C
TAPS = 4
PAD = TAPS - 1
FS, FL = 5, 64
XH, XD, SKV, DC = 16, 64, 64, 96
E, F = 8, 512
FT = F // P
BLOCKS = (2 * B * L + E * (P - 1)) // P

FG = 16

W_SCALE = 1024.0
V_SCALE = 64.0
ST_SCALE = 64.0


def wait_apart(eng, sem, value, passed):
    eng.wait_ge(sem, value)
    eng.sem_inc(passed, 1)


class Chain:

    def __init__(self, eng, sem):
        self.eng, self.sem, self.base, self.k = eng, sem, 0, 0

    def __call__(self, ins):
        self.k += 1
        return ins.then_inc(self.sem, 1)

    def settle(self):
        self.eng.wait_ge(self.sem, self.base + self.k)

    def settle_apart(self, passed):
        wait_apart(self.eng, self.sem, self.base + self.k, passed)

    @contextmanager
    def loop(self, n, per):
        start = self.base + self.k
        with self.eng.Fori(0, n) as i:
            self.base, self.k = i * per + start, 0
            yield i
            assert self.k == per, f"{self.k} steps a turn"
        self.base, self.k = start + n * per, 0


def product3(out, a, b, start, stop, **kw):
    bass_tensor = kw.pop("pe")
    (ah, al), (bh, bl) = a, b
    bass_tensor.matmul(out, ah, bh, start=start, stop=False, **kw)
    bass_tensor.matmul(out, ah, bl, start=False, stop=False, **kw)
    return bass_tensor.matmul(out, al, bh, start=False, stop=stop, **kw)


class Shared:

    def __init__(self, nc, ctx):
        sb = lambda n, s, d: ctx.enter_context(nc.sbuf_tensor(n, s, d))
        self.x = sb("x_tok", [P, TILES, D], F32)
        self.xt_hi = sb("xt_hi", [P, B + 1, PAD + L + 1], F16)
        self.xt_lo = sb("xt_lo", [P, B + 1, PAD + L + 1], F16)
        self.ident = sb("ident", [P, P], F32)
        self.flip = sb("flip", [P, P], F32)
        self.ident16 = sb("ident16", [P, P], F16)
        self.causal = sb("causal", [P, C], F32)
        self.eps5 = sb("eps5", [P, 1], F32)
        self.eps6 = sb("eps6", [P, 1], F32)
        self.semaphores = []
        self.passed = ctx.enter_context(nc.semaphore("passed"))

    def semaphore(self, nc, name):
        self.semaphores.append(nc.alloc_semaphore(name))
        return self.semaphores[-1]

    def clear_semaphores(self, nc):
        nc.clear_and_free_semaphores(self.semaphores)
        nc.all_engine_barrier()
        self.semaphores = []

    def hold_attention(self, nc, ctx):
        sb = lambda n, s, d: ctx.enter_context(nc.sbuf_tensor(n, s, d))
        self.qk = sb("qk", [P, TILES, 2 * D], F32)
        self.v = sb("v", [P, TILES, D], F32)
        self.qk_norm = sb("qk_norm", [P, TILES, 2 * H], F32)
        self.beta = sb("beta", [P, TILES, H], F32)
        self.delta = sb("delta", [P, TILES, D], F32)

    def hold_fir(self, nc, ctx):
        sb = lambda n, s, d: ctx.enter_context(nc.sbuf_tensor(n, s, d))
        self.short = sb("short", [P, TILES, D], F32)
        self.long = sb("long", [P, TILES, D], F32)


def norm_and_transpose(nc, g, stage="ln1"):
    with ExitStack() as ctx:
        sb = lambda n, s, d: ctx.enter_context(nc.sbuf_tensor(n, s, d))
        sem = lambda n: g.semaphore(nc, n)
        stats = sb(f"{stage}_stats", [P, TILES, 6], F32)
        mean_var = sb(f"{stage}_mean_var", [P, TILES, 2], F32)
        rstd = sb(f"{stage}_rstd", [P, TILES], F32)
        xn = sb(f"{stage}_xn", [P, 2, 2, D], F32)
        pt = [ctx.enter_context(nc.psum_tensor(f"{stage}_pt{k}", [P, 2 * P], F32)) for k in range(2)]
        dve_steps, var_ready, root_ready = sem(f"{stage}_dve_steps"), sem(f"{stage}_var_ready"), sem(f"{stage}_root_ready")
        normed, turned, hi_ready, lo_ready = sem(f"{stage}_normed"), sem(f"{stage}_turned"), sem(f"{stage}_hi_ready"), sem(f"{stage}_lo_ready")
        block = ctx.enter_context(nc.Block())

        @block.vector
        def _(dve):
            step = Chain(dve, dve_steps)
            with step.loop(TILES // 4, 4) as t:
                for k in range(4):
                    step(nc.vector.bn_stats(stats[:, t * 4 + k, :], g.x[:, t * 4 + k, :]))
            step.settle()
            for t in range(TILES):
                step(nc.vector.bn_aggr(mean_var[:, t, :], stats[:, t, :]))
            step(nc.vector.memset(g.eps5[:], 1e-5))
            nc.vector.memset(g.eps6[:], 1e-6).then_inc(var_ready, 1)
            dve.wait_ge(root_ready, 1)
            step(nc.vector.reciprocal(rstd[:], rstd[:]))
            step.settle()
            dve.sem_inc(lo_ready, 2)
            with dve.Fori(0, B // 2) as t:
                for k in range(2):
                    dve.wait_ge(turned, t * 2 + k + 1)
                    for half in range(2):
                        tile = t * 4 + k * 2 + half
                        last = nc.vector.tensor_scalar(xn[:, k, half, :], g.x[:, tile, :], mean_var[:, tile, 0:1],
                                                       rstd[:, bass.ds(tile, 1)], ALU.subtract, ALU.mult)
                    last.then_inc(normed, 1)
                for k in range(2):
                    dve.wait_ge(hi_ready, t * 2 + k + 1)
                    nc.vector.tensor_tensor(g.xt_lo[:, t * 2 + k, PAD:PAD + L], pt[k][:],
                                            g.xt_hi[:, t * 2 + k, PAD:PAD + L], ALU.subtract).then_inc(lo_ready, 1)

        @block.tensor
        def _(pe):
            pe.sem_inc(turned, 2)
            with pe.Fori(0, B // 2) as t:
                for k in range(2):
                    pe.wait_ge(normed, t * 2 + k + 1)
                    pe.wait_ge(lo_ready, t * 2 + k + 1)
                    for half in range(2):
                        last = nc.tensor.transpose(pt[k][:, half * P:half * P + P], xn[:, k, half, :], g.ident[:])
                    last.then_inc(turned, 1)

        @block.scalar
        def _(act):
            act.wait_ge(var_ready, 1)
            nc.scalar.activation(rstd[:], mean_var[:, :, 1], ACT.Sqrt, bias=g.eps5[:]).then_inc(root_ready, 1)
            with act.Fori(0, B // 2) as t:
                for k in range(2):
                    act.wait_ge(turned, t * 2 + k + 3)
                    nc.scalar.activation(g.xt_hi[:, t * 2 + k, PAD:PAD + L], pt[k][:], ACT.Copy).then_inc(hi_ready, 1)


def load(nc, g, w):
    with ExitStack() as ctx:
        sem = lambda n: g.semaphore(nc, n)
        x_loaded, pool_steps = sem("x_loaded"), sem("const_steps")
        block = ctx.enter_context(nc.Block())

        @block.sync
        def _(sp):
            x_view = w["x"].rearrange("b (h p) d -> p (b h) d", p=P)
            for n in range(4):
                sp.dma_start(g.x[:, 8 * n:8 * n + 8, :], x_view[:, 8 * n:8 * n + 8, :]).then_inc(x_loaded, 16)
            sp.wait_ge(x_loaded, 64)

        @block.gpsimd
        def _(pool):
            step = Chain(pool, pool_steps)
            step(nc.gpsimd.memset(g.ident[:], 0.0))
            step(nc.gpsimd.memset(g.flip[:], 0.0))
            step(nc.gpsimd.memset(g.causal[:], 1.0))
            step(nc.gpsimd.memset(g.xt_hi[:, :, 0:PAD], 0.0))
            step(nc.gpsimd.memset(g.xt_lo[:, :, 0:PAD], 0.0))
            step.settle()
            step(nc.gpsimd.affine_select(out=g.ident[:], in_=g.ident[:], compare_op=ALU.not_equal, fill=1.0,
                                         base=0, pattern=[[-1, P]], channel_multiplier=1))
            step(nc.gpsimd.affine_select(out=g.flip[:], in_=g.flip[:], compare_op=ALU.not_equal, fill=1.0,
                                         base=1 - P, pattern=[[1, P]], channel_multiplier=1))
            for c in range(CT):
                step.settle()
                rows = g.causal[C * c:C * c + C, :]
                step(nc.gpsimd.affine_select(out=rows, in_=rows, compare_op=ALU.is_ge, fill=0.0, base=0,
                                             pattern=[[1, C]], channel_multiplier=-1))
            step.settle()
            step(nc.gpsimd.tensor_scalar(g.ident16[:], g.ident[:], 1.0, None, ALU.mult))
            step.settle()


def project(nc, g, w):
    with ExitStack() as ctx:
        sb = lambda n, s, d: ctx.enter_context(nc.sbuf_tensor(n, s, d))
        sem = lambda n: g.semaphore(nc, n)
        QKV = 3 * D + H
        w_nat = sb("w_nat", [P, 3, D], F32)
        cw = sb("cw", [P, 3, TAPS], F32)
        b_w = sb("b_w_nat", [H, D], F32)
        w_tap = sb("w_tap", [P, TAPS, 3, D], F32)
        b_tap = sb("b_tap", [H, D], F32)
        wc_hi = sb("wc_hi", [P, TAPS, QKV], F16)
        wc_lo = sb("wc_lo", [P, TAPS, QKV], F16)
        square = sb("square", [P, 2, 2 * D], F32)
        pw = [ctx.enter_context(nc.psum_tensor(f"pw{j}", [P, 512], F32)) for j in range(2)]
        pq = [ctx.enter_context(nc.psum_tensor(f"pq{j}", [P, 512], F32)) for j in range(4)]
        loaded, dve_steps = sem("loaded"), sem("dve_steps")
        taps_ready, tap_turned, tap_hi_ready = sem("taps_ready"), sem("tap_turned"), sem("tap_hi_ready")
        weights_ready, qkv_ready, qkv_stored = sem("weights_ready"), sem("qkv_ready"), sem("qkv_stored")
        beta_stored, squared, squares_summed = sem("beta_stored"), sem("squared"), sem("squares_summed")
        root_ready = sem("root_ready")
        block = ctx.enter_context(nc.Block())

        @block.sync
        def _(sp):
            for n, name in enumerate(("q", "k", "v")):
                sp.dma_start(w_nat[:, n, :], w[f"L0_attn_{name}_w"]).then_inc(loaded, 16)
                sp.dma_start(cw[:, n, :], w[f"L0_attn_{name}_cw"]).then_inc(loaded, 16)
            sp.dma_start(b_w[:], w["L0_attn_b_w"]).then_inc(loaded, 16)

        @block.gpsimd
        def _(pool):
            with pool.Fori(0, B) as b:
                for k in range(2):
                    pool.wait_ge(qkv_stored, b * 2 + k + 5)
                    pool.wait_ge(squares_summed, b * 2 + k + 1)
                    qk = g.qk[:, b * 2 + k, :]
                    nc.gpsimd.tensor_tensor(square[:, k, :], qk, qk, ALU.mult).then_inc(squared, 1)

        @block.vector
        def _(dve):
            step = Chain(dve, dve_steps)
            dve.sem_inc(squares_summed, 2)
            dve.wait_ge(loaded, 16 * 7)
            for j in range(TAPS):
                for n in range(3):
                    step(nc.vector.tensor_scalar(w_tap[:, j, n, :], w_nat[:, n, :], cw[:, n, j:j + 1],
                                                 W_SCALE, ALU.mult, ALU.mult))
            nc.vector.tensor_scalar(b_tap[:], b_w[:], W_SCALE, None, ALU.mult).then_inc(taps_ready, 1)
            for j in range(TAPS):
                n = QKV if j == TAPS - 1 else 3 * D
                dve.wait_ge(tap_hi_ready, j + 1)
                nc.vector.tensor_tensor(wc_lo[:, j, 0:n], pw[j % 2][:, 0:n], wc_hi[:, j, 0:n],
                                        ALU.subtract).then_inc(weights_ready, 1)
            with dve.Fori(0, B // 2) as b:
                for k in range(4):
                    dve.wait_ge(qkv_ready, b * 4 + k + 1)
                    nc.vector.tensor_copy(g.beta[:, b * 4 + k, :], pq[k][:, 3 * D:QKV]).then_inc(beta_stored, 1)
                    dve.wait_ge(squared, b * 4 + k + 1)
                    nc.vector.tensor_reduce(g.qk_norm[:, b * 4 + k, :],
                                            square[:, k % 2, :].rearrange("p (h d) -> p h d", d=DH),
                                            AX.X, ALU.add).then_inc(squares_summed, 1)
            dve.wait_ge(root_ready, 2)
            step(nc.vector.reciprocal(g.qk_norm[:], g.qk_norm[:]))
            step(nc.vector.tensor_scalar(g.beta[:], g.beta[:], 1e-6, None, ALU.max))
            step.settle()

        @block.tensor
        def _(pe):
            pe.wait_ge(taps_ready, 1)
            for j in range(TAPS):
                if j >= 2:
                    pe.wait_ge(weights_ready, j - 1)
                for n in range(3):
                    last = nc.tensor.transpose(pw[j % 2][:, n * D:(n + 1) * D], w_tap[:, j, n, :], g.ident[:])
                if j == TAPS - 1:
                    last = nc.tensor.transpose(pw[j % 2][:, 3 * D:QKV], b_tap[:], g.ident[0:H, 0:H])
                last.then_inc(tap_turned, 1)
            pe.wait_ge(weights_ready, TAPS)
            with pe.Fori(0, B // 2) as b:
                for k in range(4):
                    pe.wait_ge(qkv_stored, b * 4 + k + 1)
                    for m, j in enumerate(reversed(range(TAPS))):
                        n = QKV if j == TAPS - 1 else 3 * D
                        at = bass.ds(k % 2 * P + j, P)
                        last = product3(pq[k][:, 0:n], (g.xt_hi[:, b * 2 + k // 2, at], g.xt_lo[:, b * 2 + k // 2, at]),
                                        (wc_hi[:, j, 0:n], wc_lo[:, j, 0:n]), m == 0, m == TAPS - 1, pe=nc.tensor)
                    last.then_inc(qkv_ready, 1)

        @block.scalar
        def _(act):
            for j in range(TAPS):
                n = QKV if j == TAPS - 1 else 3 * D
                act.wait_ge(tap_turned, j + 1)
                nc.scalar.activation(wc_hi[:, j, 0:n], pw[j % 2][:, 0:n], ACT.Copy).then_inc(tap_hi_ready, 1)
            act.sem_inc(qkv_stored, 4)
            with act.Fori(0, B // 2) as b:
                for k in range(4):
                    act.wait_ge(beta_stored, b * 4 + k + 1)
                    nc.scalar.activation(g.qk[:, b * 4 + k, :], pq[k][:, 0:2 * D], ACT.Silu, scale=1 / W_SCALE)
                    nc.scalar.activation(g.v[:, b * 4 + k, :], pq[k][:, 2 * D:3 * D], ACT.Silu,
                                         scale=1 / W_SCALE).then_inc(qkv_stored, 1)
            act.wait_ge(squares_summed, TILES + 2)
            nc.scalar.activation(g.beta[:], g.beta[:], ACT.Sigmoid, scale=1 / W_SCALE).then_inc(root_ready, 1)
            nc.scalar.activation(g.qk_norm[:], g.qk_norm[:], ACT.Sqrt, bias=g.eps6[:]).then_inc(root_ready, 1)


def delta_solve(nc, g, tt, vb, ak, q16):
    with ExitStack() as ctx:
        sb = lambda n, s, d: ctx.enter_context(nc.sbuf_tensor(n, s, d))
        sem = lambda n: g.semaphore(nc, n)
        ps = lambda n: ctx.enter_context(nc.psum_tensor(n, [P, 512], F32))
        W2 = 2 * DH
        negb = sb("negb", [P, TILES, H], F32)
        bv = sb("bv", [P, TILES, H], F32)
        qkn = sb("qkn", [P, 2, 2, 2, D], F32)
        kv = sb("kv", [P, 2, 2 * H, W2], F32)
        kqt = sb("kqt", [P, 2, 2, 2, 2, P], F16)
        at = sb("at", [P, 2, 2 * H, C], F32)
        flat = g.qk[:].rearrange("p t n -> p (t n)")
        ng = flat[:, 0:TILES * H * C].rearrange("p (u s) -> p u s", s=C)
        nu = flat[:, TILES * H * C:].rearrange("p (s m) -> p s m", s=C)
        t_u = flat[:, 0:CT * C * C].rearrange("p (t c j) -> p t c j", c=CT, t=C)
        tmp = sb("fs_tmp", [P, CT * 256], F32)
        bank = [ps(f"dl{n}") for n in range(8)]

        pe_steps = sem("dl_pe_steps")
        betas, normed, scaled, vb_hi, qk_hi = sem("dl_betas"), sem("dl_normed"), sem("dl_scaled"), sem("dl_vb_hi"), sem("dl_qk_hi")
        turned, kqt_hi, kqt_ready, gram_ready = sem("dl_turned"), sem("dl_kqt_hi"), sem("dl_kqt_ready"), sem("dl_gram_ready")
        masked, at_hi, at_stored = sem("dl_masked"), sem("dl_at_hi"), sem("dl_at_stored")
        ng_ready, nu_turned, nu_dve, nu_act = sem("dl_ng_ready"), sem("dl_nu_turned"), sem("dl_nu_dve"), sem("dl_nu_act")
        t_clear, t_one, sub_dve, sub_pool = sem("dl_t_clear"), sem("dl_t_one"), sem("dl_sub_dve"), sem("dl_sub_pool")
        tt_turned, tt_hi, tt_lo = sem("dl_tt_turned"), sem("dl_tt_hi"), sem("dl_tt_lo")
        block = ctx.enter_context(nc.Block())

        @block.vector
        def _(dve):
            step = Chain(dve, sub_dve)
            nc.vector.tensor_scalar(negb[:], g.beta[:], -1.0, None, ALU.mult).then_inc(betas, 1)
            nc.vector.tensor_scalar(bv[:], g.beta[:], V_SCALE, None, ALU.mult).then_inc(betas, 1)
            dve.wait_ge(betas, 2)
            with dve.Fori(0, B // 2) as t:
                for k in range(2):
                    i = t * 2 + k
                    two = bass.ds(i * 2, 2)
                    nc.vector.tensor_tensor(
                        qkn[:, k].rearrange("p t a (h d) -> p (t a h) d", d=DH),
                        g.qk[:, two, :].rearrange("p t (h d) -> p (t h) d", d=DH),
                        g.qk_norm[:, two, :].rearrange("p t h -> p (t h)").unsqueeze(2).to_broadcast([P, 4 * H, DH]),
                        ALU.mult).then_inc(normed, 1)
                for k in range(2):
                    i = t * 2 + k
                    two = bass.ds(i * 2, 2)
                    dve.wait_ge(vb_hi, i + 1)
                    nc.vector.tensor_tensor(
                        vb[:, two, 1].rearrange("p t h w -> p t (h w)"),
                        kv[:, k].rearrange("p (t h) w -> p t (h w)", t=2),
                        vb[:, two, 0].rearrange("p t h w -> p t (h w)"), ALU.subtract)
                    dve.wait_ge(qk_hi, i + 1)
                    nc.vector.tensor_tensor(q16[:, two, 1, :], qkn[:, k, :, 0, :], q16[:, two, 0, :], ALU.subtract)
                    for half in range(2):
                        nc.vector.tensor_tensor(
                            ak[:, i * 2 + half, 1, :, DH:], qkn[:, k, half, 1, :].rearrange("p (h d) -> p h d", d=DH),
                            ak[:, i * 2 + half, 0, :, DH:], ALU.subtract)
                    dve.wait_ge(kqt_hi, i + 1)
                    nc.vector.tensor_tensor(kqt[:, k, 1].rearrange("p t a n -> p (t a n)"), bank[k][:],
                                            kqt[:, k, 0].rearrange("p t a n -> p (t a n)"),
                                            ALU.subtract).then_inc(kqt_ready, 1)
                for k in range(2):
                    i = t * 2 + k
                    two = bass.ds(i * 2, 2)
                    dve.wait_ge(gram_ready, i + 1)
                    gram = bank[2 + k][:].rearrange("p (u a n) -> p u a n", a=2, n=C)
                    nc.vector.tensor_tensor(
                        ng[:, bass.ds(i * 2 * H, 2 * H), :], gram[:, :, 1, :],
                        negb[:, two, :].rearrange("p t h -> p (t h)").unsqueeze(2).to_broadcast([P, 2 * H, C]),
                        ALU.mult)
                    dve.wait_ge(at_stored, i + 1)
                    nc.vector.tensor_tensor(at[:, k], gram[:, :, 0, :],
                                            g.causal[:].unsqueeze(1).to_broadcast([P, 2 * H, C]),
                                            ALU.mult).then_inc(masked, 1)
            for m in range(C // 4):
                if m % 2 == 0:
                    dve.wait_ge(nu_turned, m + 1)
                    nc.vector.tensor_copy(nu[:, 4 * m:4 * m + 4, :], bank[m % 8][:].rearrange("p (s m) -> p s m", s=4)
                                          ).then_inc(nu_dve, 1)
            dve.wait_ge(nu_turned, C // 4)
            nc.vector.memset(t_u[:], 0.0).then_inc(t_clear, 1)
            dve.wait_ge(t_clear, 1)
            for c in range(CT):
                ones = flat[:, c * C:c * C + (C - 1) * (CT * C + 1) + 1:CT * C + 1]
                nc.vector.memset(ones, 1.0).then_inc(t_one, 1)
            dve.wait_ge(nu_dve, C // 8)
            dve.wait_ge(nu_act, C // 8)
            dve.wait_ge(t_one, CT)
            for s in range(C - 1):
                substitute(nc.vector, step, nu, t_u, tmp, s, 0, 3)
            for m in range(C // 4):
                dve.wait_ge(tt_hi, m + 1)
                nc.vector.tensor_tensor(
                    tt[:, :, 1, :].rearrange("p t (h n) -> p t h n", h=H)[:, :, :, 4 * m:4 * m + 4],
                    bank[m % 8][:].rearrange("p (n t h) -> p t h n", n=4, h=H),
                    tt[:, :, 0, :].rearrange("p t (h n) -> p t h n", h=H)[:, :, :, 4 * m:4 * m + 4],
                    ALU.subtract).then_inc(tt_lo, 1)

        @block.gpsimd
        def _(pool):
            step = Chain(pool, sub_pool)
            pool.wait_ge(betas, 2)
            pool.sem_inc(at_stored, 2)
            with pool.Fori(0, B // 2) as t:
                for k in range(2):
                    i = t * 2 + k
                    two = bass.ds(i * 2, 2)
                    pool.wait_ge(normed, i + 1)
                    nc.gpsimd.tensor_tensor(
                        kv[:, k, :, 0:DH], g.v[:, two, :].rearrange("p t (h d) -> p (t h) d", d=DH),
                        bv[:, two, :].rearrange("p t h -> p (t h)").unsqueeze(2).to_broadcast([P, 2 * H, DH]),
                        ALU.mult).then_inc(scaled, 1)
                    for half in range(2):
                        nc.gpsimd.tensor_tensor(
                            kv[:, k, H * half:H * half + H, DH:],
                            qkn[:, k, half, 1, :].rearrange("p (h d) -> p h d", d=DH),
                            negb[:, i * 2 + half, :].unsqueeze(2).to_broadcast([P, H, DH]),
                            ALU.mult).then_inc(scaled, 1)
                for k in range(2):
                    i = t * 2 + k
                    pool.wait_ge(at_hi, i + 1)
                    nc.gpsimd.tensor_tensor(
                        ak[:, bass.ds(i * 2, 2), 1, :, 0:C], at[:, k].rearrange("p (t h) n -> p t h n", t=2),
                        ak[:, bass.ds(i * 2, 2), 0, :, 0:C], ALU.subtract).then_inc(at_stored, 1)
            pool.wait_ge(nu_dve, C // 8)
            pool.wait_ge(nu_act, C // 8)
            pool.wait_ge(t_one, CT)
            for s in range(C - 1):
                substitute(nc.gpsimd, step, nu, t_u, tmp, s, 3, 4)

        @block.scalar
        def _(act):
            with act.Fori(0, B // 2) as t:
                for k in range(2):
                    i = t * 2 + k
                    two = bass.ds(i * 2, 2)
                    act.wait_ge(scaled, i * 3 + 3)
                    nc.scalar.activation(vb[:, two, 0].rearrange("p t h w -> p t (h w)"),
                                         kv[:, k].rearrange("p (t h) w -> p t (h w)", t=2),
                                         ACT.Copy).then_inc(vb_hi, 1)
                    nc.scalar.activation(q16[:, two, 0, :], qkn[:, k, :, 0, :], ACT.Copy)
                    nc.scalar.activation(ak[:, two, 0, :, DH:],
                                         qkn[:, k, :, 1, :].rearrange("p t (h d) -> p t h d", d=DH),
                                         ACT.Copy).then_inc(qk_hi, 1)
                    act.wait_ge(turned, i + 1)
                    nc.scalar.activation(kqt[:, k, 0].rearrange("p t a n -> p (t a n)"), bank[k][:],
                                         ACT.Copy).then_inc(kqt_hi, 1)
                for k in range(2):
                    i = t * 2 + k
                    act.wait_ge(masked, i + 1)
                    nc.scalar.activation(ak[:, bass.ds(i * 2, 2), 0, :, 0:C],
                                         at[:, k].rearrange("p (t h) n -> p t h n", t=2), ACT.Copy).then_inc(at_hi, 1)
            for m in range(C // 4):
                if m % 2 == 1:
                    act.wait_ge(nu_turned, m + 1)
                    nc.scalar.activation(nu[:, 4 * m:4 * m + 4, :], bank[m % 8][:].rearrange("p (s m) -> p s m", s=4),
                                         ACT.Copy).then_inc(nu_act, 1)
            for m in range(C // 4):
                act.wait_ge(tt_turned, m + 1)
                nc.scalar.activation(tt[:, :, 0, :].rearrange("p t (h n) -> p t h n", h=H)[:, :, :, 4 * m:4 * m + 4],
                                     bank[m % 8][:].rearrange("p (n t h) -> p t h n", n=4, h=H),
                                     ACT.Copy).then_inc(tt_hi, 1)

        @block.tensor
        def _(pe):
            step = Chain(pe, pe_steps)
            with step.loop(B // 2, 2 * (H - 1)) as t:
                for k in range(2):
                    i = t * 2 + k
                    pe.wait_ge(normed, i + 1)
                    for half in range(2):
                        for a in range(2):
                            n = (half * 2 + a) * P
                            last = nc.tensor.transpose(bank[k][:, n:n + P], qkn[:, k, half, a, :], g.ident[:])
                    last.then_inc(turned, 1)
                for k in range(2):
                    i = t * 2 + k
                    wait_apart(pe, kqt_ready, i + 1, g.passed)
                    for h in range(H):
                        rows = slice(DH * h, DH * h + DH)
                        for half in range(2):
                            for c in range(CT):
                                toks = slice(C * c, C * c + C)
                                n = (half * H + h) * 2 * C
                                last = product3(bank[2 + k][toks, n:n + 2 * C],
                                                [kqt[rows, k, a, half, 1, toks] for a in range(2)],
                                                [kqt[rows, k, a, half, :, toks] for a in range(2)],
                                                True, True, pe=nc.tensor)
                        if h < H - 1:
                            step(last)
                            step.settle_apart(g.passed)
                    last.then_inc(gram_ready, 1)
            pe.wait_ge(masked, B)
            for m in range(C // 4):
                for s in range(4):
                    last = nc.tensor.transpose(bank[m % 8][:, s * P:s * P + P], ng[:, :, 4 * m + s], g.ident[:])
                last.then_inc(nu_turned, 1)
            pe.wait_ge(sub_dve, 2 * (C - 1))
            pe.wait_ge(sub_pool, 2 * (C - 1))
            for m in range(C // 4):
                for s in range(4):
                    last = nc.tensor.transpose(bank[m % 8][:, s * P:s * P + P], t_u[:, 4 * m + s].rearrange("p c j -> p (c j)"), g.ident[:])
                last.then_inc(tt_turned, 1)


def substitute(engine, step, nu, t_u, tmp, s, c0, c1):
    n, rows, cols = c1 - c0, C - 1 - s, s + 1
    part = tmp[:, c0 * 256:c0 * 256 + n * rows * cols].rearrange("p (t c j) -> p t c j", c=n, t=rows)
    factor = nu[:, s, :].rearrange("p (c t) -> p t c", c=CT)[:, s + 1:C, c0:c1]
    if s:
        step.settle()
    step(engine.tensor_tensor(part, factor.unsqueeze(3).to_broadcast([P, rows, n, cols]),
                              t_u[:, s:s + 1, c0:c1, 0:cols].to_broadcast([P, rows, n, cols]), ALU.mult))
    step.settle()
    below = t_u[:, s + 1:C, c0:c1, 0:cols]
    step(engine.tensor_tensor(below, below, part, ALU.add))


def delta_rule(nc, g):
    with ExitStack() as ctx:
        sb = lambda n, s, d: ctx.enter_context(nc.sbuf_tensor(n, s, d))
        tt = sb("tt", [P, TILES, 2, H * C], F16)
        vb = sb("vb", [P, TILES, 2, H, 2 * DH], F16)
        ak = sb("ak", [P, TILES, 2, H, 2 * DH], F16)
        q16 = g.delta[:].bitcast(F16).rearrange("p t (a n) -> p t a n", a=2)
        delta_solve(nc, g, tt, vb, ak, q16)
        delta_apply(nc, g, tt, vb, ak, q16)


def delta_apply(nc, g, tt, vb, ak, q16):
    with ExitStack() as ctx:
        sb = lambda n, s, d: ctx.enter_context(nc.sbuf_tensor(n, s, d))
        sem = lambda n: g.semaphore(nc, n)
        W2 = 2 * DH
        s_tt = sb("s_tt", [P, 2, 2, H, C], F16)
        s_vb = sb("s_vb", [P, 2, 2, H, W2], F16)
        s_ak = sb("s_ak", [P, 2, 2, H, W2], F16)
        wu = sb("wu", [P, 2, 2, H, W2], F16)
        s_bt = sb("s_bt", [P, 2, CT, 2, W2], F16)
        s_state = sb("s_state", [P, 2, CT, 2, DH], F16)
        move = sb("move", [P, B, 2, DH], F16)
        state = sb("state", [P, B, DH], F32)
        state16 = sb("state16", [P, 2, B, DH], F16)
        bt = g.qk[:].bitcast(F16).rearrange("p t (c a n) -> p (t c) a n", c=CT, a=2)
        ku = tt[:].bitcast(F32).rearrange("p t a n -> p (t a n)").rearrange("p (t n) -> p t n", n=CT * DH)
        states = vb[:].rearrange("p t a h w -> p (t a h w)")[:, 0:B * NCH * 2 * DH].rearrange(
            "p (m a d) -> p m a d", a=2, d=DH)
        bank = [ctx.enter_context(nc.psum_tensor(f"da{n}", [P, 512], F32)) for n in range(8)]
        staged = [sem("da_staged0"), sem("da_staged1")]
        staged_out = [sem("da_staged_out0"), sem("da_staged_out1")]
        wu_ready, wu_hi, wu_lo = sem("da_wu_ready"), sem("da_wu_hi"), sem("da_wu_lo")
        turn_ready, out_ready = sem("da_turn_ready"), sem("da_out_ready")
        bt_hi, bt_lo, ku_stored, part_stored, pe_steps = sem("da_bt_hi"), sem("da_bt_lo"), sem("da_ku_stored"), sem("da_part_stored"), sem("da_pe_steps")
        dve_steps, state_ready = sem("da_dve_steps"), sem("da_state_ready")
        s_hi, s_lo, moved = sem("da_s_hi"), sem("da_s_lo"), sem("da_moved")
        read_out, out_added, states_stored = sem("da_read_out"), sem("da_out_added"), sem("da_states_stored")
        block = ctx.enter_context(nc.Block())

        @block.sync
        def _(sp):
            with sp.Fori(0, TILES // 2) as t:
                for k in range(2):
                    i = t * 2 + k
                    sp.wait_ge(out_ready, i + 1)
                    sp.dma_start(s_tt[:, k], tt[:, i].rearrange("p a (h n) -> p a h n", h=H)).then_inc(staged[k], 16)
                    sp.dma_start(s_vb[:, k], vb[:, i]).then_inc(staged[k], 16)
                    sp.dma_start(s_ak[:, k], ak[:, i]).then_inc(staged[k], 16)
            sp.wait_ge(states_stored, NCH)
            with sp.Fori(0, TILES // 2) as t:
                for k in range(2):
                    i = t * 2 + k
                    sp.wait_ge(read_out, i + 1)
                    sp.dma_start(s_bt[:, k], bt[:, bass.ds(i * CT, CT)]).then_inc(staged_out[k], 16)
                    sp.dma_start(s_state[:, k], states[:, bass.ds(i * CT, CT)]).then_inc(staged_out[k], 16)

        @block.tensor
        def _(pe):
            step = Chain(pe, pe_steps)
            pe.sem_inc(out_ready, 2)
            with step.loop(TILES // 2, 2 * (CT - 1) + 2) as t:
                for k in range(2):
                    wait_apart(pe, staged[k], t * 48 + 48, g.passed)
                    for h in range(H):
                        for c in range(CT):
                            rows = slice(C * c, C * c + C)
                            last = product3(bank[k][rows, h * W2:h * W2 + W2], [s_tt[rows, k, a, h, :] for a in range(2)],
                                            [s_vb[rows, k, a, h, :] for a in range(2)], True, True, pe=nc.tensor)
                    last.then_inc(wu_ready, 1)
                for k in range(2):
                    i = t * 2 + k
                    pe.wait_ge(wu_lo, i + 1)
                    turned = bank[2 + k][:, 0:CT * W2].rearrange("p (c n) -> p c n", c=CT)
                    nc.tensor.matmul(turned[:, :, 0:C], q16[:, i, 0, :], g.ident16[:], start=True, stop=False,
                                     skip_group_check=True)
                    last = nc.tensor.matmul(turned[:, :, 0:C], q16[:, i, 1, :], g.ident16[:], start=False, stop=False,
                                            skip_group_check=True)
                    step(last)
                    step.settle_apart(g.passed)
                    for c in range(CT):
                        rows = slice(C * c, C * c + C)
                        for h in range(H):
                            to = slice(DH * h, DH * h + DH)
                            last = product3(bank[2 + k][to, c * W2:c * W2 + W2],
                                            [wu[rows, k, a, h, DH:] for a in range(2)],
                                            [s_ak[rows, k, a, h, :] for a in range(2)], False, True, pe=nc.tensor,
                                            skip_group_check=True)
                            if h == H - 1 and c == CT - 1:
                                last.then_inc(turn_ready, 1)
                            last = product3(bank[4 + k][to, c * DH:c * DH + DH],
                                            [s_ak[rows, k, a, h, C:] for a in range(2)],
                                            [wu[rows, k, a, h, 0:DH] for a in range(2)], True, True, pe=nc.tensor)
                        if c < CT - 1:
                            step(last)
                            step.settle_apart(g.passed)
                    for h in range(H):
                        for c in range(CT):
                            rows = slice(C * c, C * c + C)
                            last = product3(bank[6 + k][rows, h * DH:h * DH + DH],
                                            [s_ak[rows, k, a, h, 0:C] for a in range(2)],
                                            [wu[rows, k, a, h, 0:DH] for a in range(2)], True, True, pe=nc.tensor)
                    last.then_inc(out_ready, 1)
            with pe.Fori(0, NCH - 1) as n:
                wait_apart(pe, s_lo, n + 1, g.passed)
                for b in range(B):
                    for h in range(H):
                        rows = slice(DH * h, DH * h + DH)
                        last = product3(bank[0][rows, b * DH:b * DH + DH], [move[rows, b, a, :] for a in range(2)],
                                        [state16[rows, a, b, :] for a in range(2)], True, True, pe=nc.tensor)
                last.then_inc(moved, 1)
            pe.sem_inc(read_out, 2)
            with step.loop(TILES // 2, 2 * (H - 1)) as t:
                for k in range(2):
                    i = t * 2 + k
                    pe.wait_ge(staged_out[k], t * 32 + 32)
                    wait_apart(pe, out_added, i + 1, g.passed)
                    for h in range(H):
                        rows = slice(DH * h, DH * h + DH)
                        for c in range(CT):
                            last = product3(bank[1 + k][C * c:C * c + C, h * DH:h * DH + DH],
                                            [s_bt[rows, k, c, a, 0:C] for a in range(2)],
                                            [s_state[rows, k, c, a, :] for a in range(2)], True, True, pe=nc.tensor)
                        if h < H - 1:
                            step(last)
                            step.settle_apart(g.passed)
                    last.then_inc(read_out, 1)

        @block.scalar
        def _(act):
            with act.Fori(0, TILES // 2) as t:
                for k in range(2):
                    act.wait_ge(wu_ready, t * 2 + k + 1)
                    nc.scalar.activation(wu[:, k, 0].rearrange("p h w -> p (h w)"), bank[k][:, 0:H * W2],
                                         ACT.Copy).then_inc(wu_hi, 1)
                for k in range(2):
                    i = t * 2 + k
                    act.wait_ge(out_ready, i + 3)
                    nc.scalar.activation(bt[:, bass.ds(i * CT, CT), 0, :],
                                         bank[2 + k][:, 0:CT * W2].rearrange("p (c n) -> p c n", c=CT),
                                         ACT.Copy).then_inc(bt_hi, 1)
                    nc.scalar.activation(ku[:, i, :], bank[4 + k][:, 0:CT * DH], ACT.Copy).then_inc(ku_stored, 1)
            with act.Fori(0, NCH) as n:
                act.wait_ge(state_ready, n + 1)
                nc.scalar.activation(state16[:, 0], state[:], ACT.Copy).then_inc(s_hi, 1)

        @block.vector
        def _(dve):
            step = Chain(dve, dve_steps)
            with dve.Fori(0, TILES // 2) as t:
                for k in range(2):
                    dve.wait_ge(wu_hi, t * 2 + k + 1)
                    nc.vector.tensor_tensor(wu[:, k, 1].rearrange("p h w -> p (h w)"), bank[k][:, 0:H * W2],
                                            wu[:, k, 0].rearrange("p h w -> p (h w)"),
                                            ALU.subtract).then_inc(wu_lo, 1)
                for k in range(2):
                    i = t * 2 + k
                    dve.wait_ge(out_ready, i + 3)
                    nc.vector.tensor_scalar(g.delta[:, i, :], bank[6 + k][:, 0:H * DH], 1 / V_SCALE, None,
                                            ALU.mult).then_inc(part_stored, 1)
                    dve.wait_ge(bt_hi, i + 1)
                    nc.vector.tensor_tensor(bt[:, bass.ds(i * CT, CT), 1, :],
                                            bank[2 + k][:, 0:CT * W2].rearrange("p (c n) -> p c n", c=CT),
                                            bt[:, bass.ds(i * CT, CT), 0, :], ALU.subtract).then_inc(bt_lo, 1)
            nc.vector.memset(state[:], 0.0).then_inc(state_ready, 1)
            dve.wait_ge(ku_stored, TILES)
            dve.wait_ge(bt_lo, TILES)
            ku_chunk = ku.rearrange("p t (c d) -> p (t c) d", d=DH).rearrange("p (b n) d -> p b n d", n=NCH)
            bt_chunk = bt.rearrange("p (b n) a d -> p b n a d", n=NCH)
            st_chunk = states.rearrange("p (b n) a d -> p b n a d", n=NCH)
            with step.loop(NCH - 1, 2) as n:
                step(nc.vector.tensor_copy(move[:], bt_chunk[:, :, n, :, C:]))
                dve.wait_ge(s_hi, n + 1)
                nc.vector.tensor_tensor(state16[:, 1], state[:], state16[:, 0], ALU.subtract).then_inc(s_lo, 1)
                dve.wait_ge(s_lo, n + 1)
                nc.vector.tensor_copy(st_chunk[:, :, n], state16[:].rearrange("p a b d -> p b a d")
                                      ).then_inc(states_stored, 1)
                step(nc.vector.tensor_tensor(state[:], state[:], ku_chunk[:, :, n, :], ALU.add))
                step.settle()
                dve.wait_ge(moved, n + 1)
                nc.vector.tensor_tensor(state[:], state[:], bank[0][:].rearrange("p (b d) -> p b d", d=DH),
                                        ALU.add).then_inc(state_ready, 1)
            dve.wait_ge(s_hi, NCH)
            nc.vector.tensor_tensor(state16[:, 1], state[:], state16[:, 0], ALU.subtract).then_inc(s_lo, 1)
            dve.wait_ge(s_lo, NCH)
            nc.vector.tensor_copy(st_chunk[:, :, NCH - 1], state16[:].rearrange("p a b d -> p b a d")
                                  ).then_inc(states_stored, 1)
            dve.sem_inc(out_added, 2)
            with dve.Fori(0, TILES // 2) as t:
                for k in range(2):
                    i = t * 2 + k
                    dve.wait_ge(read_out, i + 3)
                    nc.vector.scalar_tensor_tensor(out=g.delta[:, i, :], in0=bank[1 + k][:, 0:H * DH],
                                                   scalar=1 / V_SCALE, in1=g.delta[:, i, :], op0=ALU.mult,
                                                   op1=ALU.add).then_inc(out_added, 1)


def lay_out_fir(weight):
    import numpy as np
    w = np.asarray(weight).reshape(D, -1)
    taps = w.shape[1]
    rows = np.zeros((2 * P + taps + taps % 2, D), w.dtype)
    rows[P - 1:P - 1 + taps] = w[:, ::-1].T
    return np.ascontiguousarray(rows.reshape(-1, D // FG, FG).transpose(1, 0, 2))


def fir(nc, g, w):
    with ExitStack() as ctx:
        sb = lambda n, s, d: ctx.enter_context(nc.sbuf_tensor(n, s, d))
        sem = lambda n: g.semaphore(nc, n)
        kinds = []
        for name, taps in (("short", FS), ("long", FL)):
            rows = w[f"fir_{name}"].shape[1]
            width = P + taps - 1 + (taps - 1) % 2
            kinds.append((name, taps, rows, width))
        n_src = [D * rows // P for _, _, rows, _ in kinds]
        raw = [sb(f"raw_{kind[0]}", [P, n], F32) for kind, n in zip(kinds, n_src)]
        half = [sb(f"half_{kind[0]}", [P, 2, n], F16) for kind, n in zip(kinds, n_src)]
        store = [nc.dram_tensor(f"fir_halves_{kind[0]}", (2, D // FG, kind[2], FG), F16, kind="Internal") for kind in kinds]
        toep = [sb(f"toep_{kind[0]}", [P, 2, 2, kind[3], FG], F16) for kind in kinds]
        v16 = sb("v16", [P, 2, TILES, D], F16)
        bank = [[ctx.enter_context(nc.psum_tensor(f"fir{f}{k}", [P, FG * TILES], F32)) for k in range(2)] for f in range(2)]
        flat_banks = bank[0] + bank[1]
        PART = 4
        PARTS = TILES // PART
        v_turned = sem("fir_v_turned")
        loaded, high, low, stored = sem("fir_loaded"), sem("fir_high"), sem("fir_low"), sem("fir_stored")
        expanded = [[sem(f"fir_expanded{f}{k}") for k in range(2)] for f in range(2)]
        v_high, v_low, product_ready = sem("fir_v_high"), sem("fir_v_low"), sem("fir_product_ready")
        short_stored, long_stored = sem("fir_short_stored"), sem("fir_long_stored")
        block = ctx.enter_context(nc.Block())
        NG = D // FG

        @block.sync
        def _(sp):
            for f, kind in enumerate(kinds):
                src = w[f"fir_{kind[0]}"].rearrange("g u c -> (g u c)").rearrange("(p n) -> p n", p=P)
                sp.dma_start(raw[f][:], src).then_inc(loaded, 16)
            sp.wait_ge(low, 2)
            for f, kind in enumerate(kinds):
                for a in range(2):
                    dst = store[f].ap()[a].rearrange("g u c -> (g u c)").rearrange("(p n) -> p n", p=P)
                    sp.dma_start(dst, half[f][:, a, :]).then_inc(stored, 16)
            sp.wait_ge(stored, 64)
            for n in range(NG):
                if n >= 2:
                    sp.wait_ge(product_ready, n - 1)
                for f, (name, taps, rows, width) in enumerate(kinds):
                    for a in range(2):
                        first = (a * NG + n) * rows * FG
                        src = bass.AP(store[f], first, [[FG, P], [1, width * FG]])
                        sp.dma_start(toep[f][:, n % 2, a].rearrange("p t c -> p (t c)"), src
                                     ).then_inc(expanded[f][n % 2], 16)

        @block.vector
        def _(dve):
            for f in range(2):
                dve.wait_ge(high, f + 1)
                nc.vector.scalar_tensor_tensor(out=half[f][:, 1, :], in0=raw[f][:], scalar=W_SCALE,
                                               in1=half[f][:, 0, :], op0=ALU.mult,
                                               op1=ALU.subtract).then_inc(low, 1)
            for n in range(PARTS):
                at = slice(n * PART, (n + 1) * PART)
                dve.wait_ge(v_high, n + 1)
                nc.vector.scalar_tensor_tensor(out=v16[:, 1, at].rearrange("p t d -> p (t d)"), in0=flat_banks[n % 4][:],
                                               scalar=V_SCALE, in1=v16[:, 0, at].rearrange("p t d -> p (t d)"),
                                               op0=ALU.mult, op1=ALU.subtract).then_inc(v_low, 1)
            dve.sem_inc(short_stored, 2)
            with dve.Fori(0, NG // 2) as t:
                for k in range(2):
                    i = t * 2 + k
                    dve.wait_ge(product_ready, i + 1)
                    nc.vector.tensor_scalar(g.short[:, :, bass.ds(i * FG, FG)],
                                            bank[0][k][:].rearrange("p (c t) -> p t c", c=FG),
                                            1 / (V_SCALE * W_SCALE), None, ALU.mult).then_inc(short_stored, 1)

        @block.scalar
        def _(act):
            act.wait_ge(loaded, 32)
            for f in range(2):
                nc.scalar.activation(half[f][:, 0, :], raw[f][:], ACT.Copy, scale=W_SCALE).then_inc(high, 1)
            for n in range(PARTS):
                at = slice(n * PART, (n + 1) * PART)
                act.wait_ge(v_turned, n + 1)
                nc.scalar.activation(v16[:, 0, at].rearrange("p t d -> p (t d)"), flat_banks[n % 4][:], ACT.Copy,
                                     scale=V_SCALE).then_inc(v_high, 1)
            act.sem_inc(long_stored, 2)
            with act.Fori(0, NG // 2) as t:
                for k in range(2):
                    i = t * 2 + k
                    act.wait_ge(product_ready, i + 1)
                    nc.scalar.activation(g.long[:, :, bass.ds(i * FG, FG)],
                                         bank[1][k][:].rearrange("p (c t) -> p t c", c=FG),
                                         ACT.Copy, scale=1 / (V_SCALE * W_SCALE)).then_inc(long_stored, 1)

        @block.tensor
        def _(pe):
            for n in range(PARTS):
                if n >= 4:
                    pe.wait_ge(v_low, n - 3)
                nc.tensor.matmul(flat_banks[n % 4][:], g.flip[:],
                                 g.v[:, n * PART:(n + 1) * PART].rearrange("p t d -> p (t d)"), start=True, stop=True
                                 ).then_inc(v_turned, 1)
            pe.wait_ge(v_low, PARTS)
            with pe.Fori(0, NG // 2) as t:
                for k in range(2):
                    i = t * 2 + k
                    pe.wait_ge(short_stored, i + 1)
                    pe.wait_ge(long_stored, i + 1)
                    for f, (name, taps, rows, width) in enumerate(kinds):
                        pe.wait_ge(expanded[f][k], t * 32 + 32)
                        for c in range(FG):
                            ch = bass.ds(i * FG + c, 1)
                            own = [v16[:, a, :, ch].rearrange("p t c -> p (t c)") for a in range(2)]
                            before = [v16[:, a, 0:TILES:2, ch].rearrange("p t c -> p (t c)") for a in range(2)]
                            out = bank[f][k][:, c * TILES:(c + 1) * TILES]
                            product3(out, [toep[f][:, k, a, 0:P, c] for a in range(2)], own, True, False,
                                     pe=nc.tensor, skip_group_check=True)
                            n = taps - 1
                            last = product3(out[0:n, 1:TILES:2], [toep[f][:, k, a, P:P + n, c] for a in range(2)],
                                            before, False, True, pe=nc.tensor, skip_group_check=True)
                    last.then_inc(product_ready, 1)


def gate_and_add(nc, g, w):
    U = TILES * H
    paths = (g.short, g.long, g.delta, g.v)
    with ExitStack() as ctx:
        sb = lambda n, s, d: ctx.enter_context(nc.sbuf_tensor(n, s, d))
        sem = lambda n: g.semaphore(nc, n)
        m1 = sb("m1", [P, D + 16], F32)
        m1_pad = sb("m1_pad", [P, H, 2, H, 16], F32)
        m2 = sb("m2", [4, P], F32)
        ow = sb("ow", [P, D], F32)
        nw = sb("nw", [P, 1], F32)
        b1 = sb("b1", [P, 1], F32)
        b2 = sb("b2", [P, 4], F32)
        temp = sb("temp", [P, 4], F32)
        keep = sb("keep", [P, H], F32)
        hs_w = sb("hs_w", [P, 2, P], F16)
        st_w = sb("st_w", [P, 2, H, P], F16)
        m2_w = sb("m2_w", [P, 2, 4], F16)
        o_w = sb("o_w", [P, 2, D], F16)
        o_wf = sb("o_wf", [P, D], F32)
        sq = sb("sq", [P, 2, U // 4, DH], F32)
        raw = sb("st_raw", [P, 3, 4, U], F32)
        stf = sb("stf", [P, TILES, H, 16], F32)
        st16 = sb("st16", [P, TILES, 2, H * 16], F16)
        stt = sb("stt", [P, 2, 2 * P], F16)
        h1 = sb("h1", [P, 2, H, 2 * P], F32)
        h16 = sb("h16", [P, 2, 2, H, 2 * P], F16)
        pr = sb("pr", [P, U, 4], F32)
        ex = sb("ex", [P, U, 4], F32)
        one = sb("one", [P, 2, U], F32)
        on = sb("on", [P, 2, 2, D], F32)
        ot = sb("ot", [P, 2, 2, 2 * P], F16)
        bank = [ctx.enter_context(nc.psum_tensor(f"gt{n}", [P, 512], F32)) for n in range(8)]
        loaded, padded, dve_steps, act_steps, pool_steps = sem("gt_loaded"), sem("gt_padded"), sem("gt_dve_steps"), sem("gt_act_steps"), sem("gt_pool_steps")
        w_turned, w_high, w_low, sq_ready, sq_read = sem("gt_w_turned"), sem("gt_w_high"), sem("gt_w_low"), sem("gt_sq_ready"), sem("gt_sq_read")
        raw_ready, root_ready, st_ready, st16_hi = sem("gt_raw_ready"), sem("gt_root_ready"), sem("gt_st_ready"), sem("gt_st16_hi")
        st16_ready, st_turned, stt_ready, h_ready = sem("gt_st16_ready"), sem("gt_st_turned"), sem("gt_stt_ready"), sem("gt_h_ready")
        gelu_done, h_hi, h_lo, logits_ready = sem("gt_gelu_done"), sem("gt_h_hi"), sem("gt_h_lo"), sem("gt_logits_ready")
        logits_stored, e_in, e_out, p_ready = sem("gt_logits_stored"), sem("gt_e_in"), sem("gt_e_out"), sem("gt_p_ready")
        mixed_dve, mixed_pool, squared, rms_in, rms_out = sem("gt_mixed_dve"), sem("gt_mixed_pool"), sem("gt_squared"), sem("gt_rms_in"), sem("gt_rms_out")
        on_ready, on_turned, ot_hi, ot_lo, out_ready = sem("gt_on_ready"), sem("gt_on_turned"), sem("gt_ot_hi"), sem("gt_ot_lo"), sem("gt_out_ready")
        keep_ready, misc_ready, sq2_ready, sq2_read = sem("gt_keep_ready"), sem("gt_misc_ready"), sem("gt_sq2_ready"), sem("gt_sq2_read")
        added, w_scaled = sem("gt_added"), sem("gt_w_scaled")
        block = ctx.enter_context(nc.Block())
        units = lambda x: x[:].rearrange("p t (h d) -> p (t h) d", d=DH)
        Q = U // 4
        CUT = 88

        turned_weights = (((hs_w[:, 0], hs_w[:, 1]), bank[0][:, 0:P]),
                          ([st_w[:, a].rearrange("p h n -> p (h n)") for a in range(2)], bank[1][:]),
                          ((m2_w[:, 0], m2_w[:, 1]), bank[2][:, 0:4]))

        @block.sync
        def _(sp):
            sp.dma_start(m1[:], w["L0_attn_mlp1_w"]).then_inc(loaded, 16)
            sp.dma_start(m2[:], w["L0_attn_mlp2_w"]).then_inc(loaded, 16)
            sp.dma_start(ow[:], w["L0_attn_o_w"]).then_inc(loaded, 16)
            for h in range(H):
                sp.dma_start(nw[DH * h:DH * h + DH, :], w["L0_attn_norm_w"].unsqueeze(1)).then_inc(loaded, 16)
            sp.dma_start(b1[:], w["L0_attn_mlp1_b"].unsqueeze(1)).then_inc(loaded, 16)
            sp.dma_start(b2[:], w["L0_attn_mlp2_b"].partition_broadcast(P)).then_inc(loaded, 16)
            sp.dma_start(temp[:, 0:1], w["L0_attn_logit_temp"].partition_broadcast(P)).then_inc(loaded, 16)
            sp.dma_start(keep[:], w["L0_attn_conv_res_logit"].partition_broadcast(P)).then_inc(loaded, 16)

        @block.gpsimd
        def _(pool):
            step = Chain(pool, pool_steps)
            step(nc.gpsimd.memset(m1_pad[:], 0.0))
            pool.wait_ge(loaded, 16 * 11)
            step.settle()
            for h in range(H):
                for a in range(2):
                    if h or a:
                        pool.wait_ge(padded, 2 * h + a)
                    nc.gpsimd.tensor_scalar(m1_pad[:, h, a, h, :], m1[:, D:], W_SCALE / ST_SCALE, None,
                                            ALU.mult).then_inc(padded, 1)
            pool.sem_inc(h_lo, 2)
            with pool.Fori(0, B // 2) as t:
                for k in range(2):
                    pool.wait_ge(h_hi, t * 2 + k + 1)
                    nc.gpsimd.tensor_tensor(h16[:, k, 1].rearrange("p h n -> p (h n)"),
                                            h1[:, k].rearrange("p h n -> p (h n)"),
                                            h16[:, k, 0].rearrange("p h n -> p (h n)"), ALU.subtract).then_inc(h_lo, 1)
            pool.wait_ge(p_ready, 1)
            mix(nc.gpsimd, step, [units(x)[:, CUT:] for x in paths], pr[:, CUT:], U - CUT)
            step.settle()
            nc.gpsimd.memset(h1[:, 0, 0, 0:1], 0.0).then_inc(mixed_pool, 1)

        @block.scalar
        def _(act):
            step = Chain(act, act_steps)
            act.wait_ge(loaded, 16 * 11)
            step(nc.scalar.activation(temp[:, 1:2], temp[:, 0:1], ACT.Abs))
            step.settle()
            step(nc.scalar.activation(temp[:, 1:2], temp[:, 1:2], ACT.Exp, scale=-1.0))
            step.settle()
            nc.scalar.activation(temp[:, 1:2], temp[:, 1:2], ACT.Ln, bias=1.0).then_inc(misc_ready, 1)
            nc.scalar.activation(keep[:], keep[:], ACT.Sigmoid).then_inc(keep_ready, 1)
            for n, (dst, src) in enumerate(turned_weights):
                act.wait_ge(w_turned, n + 1)
                nc.scalar.activation(dst[0], src, ACT.Copy).then_inc(w_high, 1)
            for n, x in enumerate(paths):
                for m in range(4):
                    i = 4 * n + m
                    if i >= 2:
                        act.wait_ge(sq_read, i - 1)
                    nc.scalar.activation(sq[:, i % 2], units(x)[:, Q * m:Q * m + Q], ACT.Square).then_inc(sq_ready, 1)
            act.wait_ge(raw_ready, 1)
            nc.scalar.activation(stf[:].rearrange("p t h (x s) -> p (t h) x s", s=4)[:, :, :, 3],
                                 raw[:, 2].rearrange("p x u -> p u x"), ACT.Sqrt,
                                 scale=ST_SCALE * ST_SCALE).then_inc(root_ready, 1)
            act.wait_ge(st_ready, 1)
            nc.scalar.activation(st16[:, :, 0, :], stf[:].rearrange("p t h s -> p t (h s)"), ACT.Copy
                                 ).then_inc(st16_hi, 1)
            with act.Fori(0, B // 2) as t:
                for k in range(2):
                    act.wait_ge(st_turned, t * 2 + k + 1)
                    nc.scalar.activation(stt[:, k], bank[k][:, 0:2 * P], ACT.Copy).then_inc(stt_ready, 1)
                for k in range(2):
                    act.wait_ge(h_ready, t * 2 + k + 1)
                    act.wait_ge(h_lo, t * 2 + k + 1)
                    for n in range(2):
                        last = nc.scalar.activation(h1[:, k, 2 * n:2 * n + 2, :].rearrange("p h n -> p (h n)"),
                                                    bank[2 + 2 * k + n][:], ACT.Gelu_apprx_tanh, bias=b1[:],
                                                    scale=1 / W_SCALE)
                    last.then_inc(gelu_done, 1)
            act.wait_ge(e_in, 1)
            nc.scalar.activation(ex[:], ex[:], ACT.Exp).then_inc(e_out, 1)
            act.wait_ge(mixed_dve, 1)
            act.wait_ge(mixed_pool, 1)
            for m in range(4):
                if m >= 2:
                    act.wait_ge(sq2_read, m - 1)
                nc.scalar.activation(sq[:, m % 2], units(g.short)[:, Q * m:Q * m + Q], ACT.Square
                                     ).then_inc(sq2_ready, 1)
            act.wait_ge(rms_in, 1)
            nc.scalar.activation(one[:, 0], one[:, 0], ACT.Sqrt, bias=g.eps5[:], scale=1 / DH).then_inc(rms_out, 1)
            with act.Fori(0, B // 2) as t:
                for k in range(2):
                    act.wait_ge(on_turned, t * 2 + k + 1)
                    nc.scalar.activation(ot[:, k, 0, :], bank[k][:, 0:2 * P], ACT.Copy).then_inc(ot_hi, 1)

        @block.vector
        def _(dve):
            step = Chain(dve, dve_steps)
            dve.wait_ge(loaded, 16 * 11)
            step(nc.vector.tensor_scalar(m1[:, 0:D], m1[:, 0:D], W_SCALE, None, ALU.mult))
            nc.vector.tensor_scalar(m2[:], m2[:], W_SCALE, None, ALU.mult).then_inc(w_scaled, 1)
            dve.wait_ge(misc_ready, 1)
            step(nc.vector.tensor_scalar(temp[:, 2:3], temp[:, 0:1], 0.0, None, ALU.max))
            step.settle()
            step(nc.vector.tensor_tensor(temp[:, 2:3], temp[:, 2:3], temp[:, 1:2], ALU.add))
            step.settle()
            step(nc.vector.reciprocal(temp[:, 3:4], temp[:, 2:3]))
            step.settle()
            for n, (dst, src) in enumerate(turned_weights):
                dve.wait_ge(w_high, n + 1)
                nc.vector.tensor_tensor(dst[1], src, dst[0], ALU.subtract).then_inc(w_low, 1)
            dve.wait_ge(w_turned, 4)
            step(nc.vector.tensor_scalar(o_wf[:], bank[3][:, 0:D], nw[:], W_SCALE, ALU.mult, ALU.mult))
            step.settle()
            step(nc.vector.tensor_copy(o_w[:, 0], o_wf[:]))
            step.settle()
            nc.vector.tensor_tensor(o_w[:, 1], o_wf[:], o_w[:, 0], ALU.subtract).then_inc(w_low, 1)
            for n, x in enumerate(paths):
                step(nc.vector.tensor_reduce(raw[:, 0, n], units(x), AX.X, ALU.add))
                step(nc.vector.tensor_reduce(raw[:, 1, n], units(x), AX.X, ALU.add, apply_absolute_value=True))
                for m in range(4):
                    i = 4 * n + m
                    dve.wait_ge(sq_ready, i + 1)
                    nc.vector.tensor_reduce(raw[:, 2, n, Q * m:Q * m + Q], sq[:, i % 2], AX.X, ALU.add
                                            ).then_inc(sq_read, 1)
            dve.wait_ge(sq_read, 16)
            stat = lambda s: stf[:].rearrange("p t h (x s) -> p (t h) x s", s=4)[:, :, :, s]
            by_path = lambda n: raw[:, n].rearrange("p x u -> p u x")
            step(nc.vector.tensor_scalar(stat(0), by_path(0), ST_SCALE / DH, None, ALU.mult))
            nc.vector.tensor_scalar(stat(2), by_path(1), ST_SCALE / DH, None, ALU.mult).then_inc(raw_ready, 1)
            dve.wait_ge(root_ready, 1)
            step(nc.vector.scalar_tensor_tensor(out=raw[:, 1].rearrange("p x u -> p (x u)"),
                                                in0=raw[:, 0].rearrange("p x u -> p (x u)"),
                                                scalar=ST_SCALE / DH / DH,
                                                in1=raw[:, 0].rearrange("p x u -> p (x u)"), op0=ALU.mult, op1=ALU.mult))
            step.settle()
            nc.vector.scalar_tensor_tensor(out=stat(1), in0=by_path(2), scalar=ST_SCALE / DH, in1=by_path(1),
                                           op0=ALU.mult, op1=ALU.subtract).then_inc(st_ready, 1)
            dve.wait_ge(st16_hi, 1)
            nc.vector.tensor_tensor(st16[:, :, 1, :], stf[:].rearrange("p t h s -> p t (h s)"), st16[:, :, 0, :],
                                    ALU.subtract).then_inc(st16_ready, 1)
            with dve.Fori(0, B // 2) as t:
                for k in range(2):
                    dve.wait_ge(gelu_done, t * 2 + k + 1)
                    nc.vector.tensor_copy(h16[:, k, 0].rearrange("p h n -> p (h n)"),
                                          h1[:, k].rearrange("p h n -> p (h n)")).then_inc(h_hi, 1)
                for k in range(2):
                    i = t * 2 + k
                    dve.wait_ge(logits_ready, i + 1)
                    nc.vector.tensor_scalar(ex[:, bass.ds(i * 2 * H, 2 * H), :].rearrange("p u n -> p (u n)"),
                                            bank[6 + k][:, 0:2 * H * 4], 1 / W_SCALE, None,
                                            ALU.mult).then_inc(logits_stored, 1)
            dve.wait_ge(logits_stored, B)
            step(nc.vector.tensor_tensor(ex[:], ex[:], b2[:].unsqueeze(1).to_broadcast([P, U, 4]), ALU.add))
            step.settle()
            step(nc.vector.tensor_reduce(one[:, 0], ex[:], AX.X, ALU.max))
            step.settle()
            step(nc.vector.tensor_tensor(ex[:], ex[:], one[:, 0].unsqueeze(2).to_broadcast([P, U, 4]), ALU.subtract))
            step.settle()
            nc.vector.tensor_scalar(ex[:], ex[:], temp[:, 3:4], None, ALU.mult).then_inc(e_in, 1)
            dve.wait_ge(e_out, 1)
            for n in range(2):
                step(nc.vector.tensor_reduce(one[:, n], ex[:], AX.X, ALU.add))
                step.settle()
                step(nc.vector.reciprocal(one[:, n], one[:, n]))
                step.settle()
                step(nc.vector.tensor_tensor(ex[:], ex[:], one[:, n].unsqueeze(2).to_broadcast([P, U, 4]), ALU.mult))
                step.settle()
                if n == 0:
                    step(nc.vector.tensor_scalar(ex[:], ex[:], 0.02, None, ALU.max))
                    step.settle()
            dve.wait_ge(keep_ready, 1)
            step(nc.vector.tensor_tensor(pr[:, :, 0].rearrange("p (t h) -> p t h", h=H),
                                         ex[:, :, 0].rearrange("p (t h) -> p t h", h=H),
                                         keep[:].unsqueeze(1).to_broadcast([P, TILES, H]), ALU.add))
            nc.vector.tensor_copy(pr[:, :, 1:4], ex[:, :, 1:4]).then_inc(p_ready, 1)
            dve.wait_ge(p_ready, 1)
            mix(nc.vector, step, [units(x)[:, 0:CUT] for x in paths], pr[:, 0:CUT], CUT)
            step.settle()
            nc.vector.memset(h1[:, 1, 0, 0:1], 0.0).then_inc(mixed_dve, 1)
            for m in range(4):
                dve.wait_ge(sq2_ready, m + 1)
                nc.vector.tensor_reduce(one[:, 0, Q * m:Q * m + Q], sq[:, m % 2], AX.X, ALU.add).then_inc(sq2_read, 1)
            dve.wait_ge(sq2_read, 4)
            dve.sem_inc(rms_in, 1)
            dve.wait_ge(rms_out, 1)
            step(nc.vector.reciprocal(one[:, 1], one[:, 0]))
            step.settle()
            with dve.Fori(0, B // 2) as t:
                for k in range(2):
                    i = t * 2 + k
                    nc.vector.tensor_tensor(
                        on[:, k].rearrange("p t (h d) -> p (t h) d", d=DH),
                        units(g.short)[:, bass.ds(i * 2 * H, 2 * H), :],
                        one[:, 1, bass.ds(i * 2 * H, 2 * H)].unsqueeze(2).to_broadcast([P, 2 * H, DH]),
                        ALU.mult).then_inc(on_ready, 1)
                for k in range(2):
                    dve.wait_ge(ot_hi, t * 2 + k + 1)
                    nc.vector.tensor_tensor(ot[:, k, 1, :], bank[k][:, 0:2 * P], ot[:, k, 0, :], ALU.subtract
                                            ).then_inc(ot_lo, 1)
                for k in range(2):
                    i = t * 2 + k
                    dve.wait_ge(out_ready, i + 1)
                    xs = g.x[:, bass.ds(i * 2, 2), :].rearrange("p t d -> p (t d)")
                    nc.vector.scalar_tensor_tensor(out=xs, in0=bank[2 + k][:, 0:2 * D], scalar=1 / W_SCALE, in1=xs,
                                                   op0=ALU.mult, op1=ALU.add).then_inc(added, 1)
            dve.wait_ge(added, B)

        @block.tensor
        def _(pe):
            pe.wait_ge(padded, 2 * H)
            pe.wait_ge(w_scaled, 1)
            nc.tensor.transpose(bank[0][:, 0:P], m1[:, 0:D], g.ident[:]).then_inc(w_turned, 1)
            for h in range(H):
                last = nc.tensor.transpose(bank[1][:, h * P:h * P + P],
                                           m1_pad[:, h].rearrange("p a h s -> p (a h s)"), g.ident[:])
            last.then_inc(w_turned, 1)
            nc.tensor.transpose(bank[2][:, 0:4], m2[:], g.ident[0:4, 0:4]).then_inc(w_turned, 1)
            nc.tensor.transpose(bank[3][:, 0:D], ow[:], g.ident[:]).then_inc(w_turned, 1)
            pe.wait_ge(w_low, 4)
            pe.wait_ge(st16_ready, 1)
            with pe.Fori(0, B // 2) as t:
                for k in range(2):
                    i = t * 2 + k
                    for half in range(2):
                        last = nc.tensor.matmul(bank[k][:, half * P:half * P + P],
                                                st16[:, i * 2 + half].rearrange("p a n -> p (a n)"), g.ident16[:],
                                                start=True, stop=True)
                    last.then_inc(st_turned, 1)
                for k in range(2):
                    i = t * 2 + k
                    pe.wait_ge(stt_ready, i + 1)
                    x_t = [x[:, i, PAD:PAD + L] for x in (g.xt_hi, g.xt_lo)]
                    for h in range(H):
                        out = bank[2 + 2 * k + h // 2][:, h % 2 * L:h % 2 * L + L]
                        product3(out, (hs_w[:, 0], hs_w[:, 1]), x_t, True, False, pe=nc.tensor)
                        nc.tensor.matmul(out, st_w[:, 0, h], stt[:, k], start=False, stop=False)
                        last = nc.tensor.matmul(out, st_w[:, 1, h], stt[:, k], start=False, stop=True)
                    last.then_inc(h_ready, 1)
                for k in range(2):
                    i = t * 2 + k
                    pe.wait_ge(h_lo, i + 3)
                    for half in range(2):
                        for h in range(H):
                            n = (half * H + h) * 4
                            last = product3(bank[6 + k][:, n:n + 4],
                                            [h16[:, k, a, h, half * P:half * P + P] for a in range(2)],
                                            (m2_w[:, 0], m2_w[:, 1]), True, True, pe=nc.tensor)
                    last.then_inc(logits_ready, 1)
            with pe.Fori(0, B // 2) as t:
                for k in range(2):
                    pe.wait_ge(on_ready, t * 2 + k + 1)
                    for half in range(2):
                        last = nc.tensor.transpose(bank[k][:, half * P:half * P + P], on[:, k, half], g.ident[:])
                    last.then_inc(on_turned, 1)
                for k in range(2):
                    pe.wait_ge(ot_lo, t * 2 + k + 1)
                    for half in range(2):
                        last = product3(bank[2 + k][:, half * D:half * D + D],
                                        [ot[:, k, a, half * P:half * P + P] for a in range(2)],
                                        (o_w[:, 0], o_w[:, 1]), True, True, pe=nc.tensor)
                    last.then_inc(out_ready, 1)


def mix(engine, step, paths, weights, n):
    for j in range(4):
        step(engine.tensor_tensor(paths[j], paths[j], weights[:, :, j:j + 1].to_broadcast([P, n, DH]), ALU.mult))
    step.settle()
    step(engine.tensor_tensor(paths[0], paths[0], paths[1], ALU.add))
    step(engine.tensor_tensor(paths[2], paths[2], paths[3], ALU.add))
    step.settle()
    step(engine.tensor_tensor(paths[0], paths[0], paths[2], ALU.add))


def cross_attention(nc, g, w):
    XW = XH * XD
    PAIRS = XH // 2
    WS = 64.0
    with ExitStack() as ctx:
        sb = lambda n, s, d: ctx.enter_context(nc.sbuf_tensor(n, s, d))
        sem = lambda n: g.semaphore(nc, n)
        wq = sb("xwq", [P, XW], F32)
        wk = sb("xwk", [DC, XW], F32)
        wv = sb("xwv", [DC, XW], F32)
        wo = sb("xwo", [P, PAIRS, D], F32)
        bo = sb("xbo", [P, D], F32)
        cx = sb("xctx", [P, B // 2, DC], F32)
        wqt = sb("xwqt", [P, 2, PAIRS, D], F16)
        wkt = sb("xwkt", [P, 2, PAIRS, DC], F16)
        wvt = sb("xwvt", [P, 2, PAIRS, DC], F16)
        wo16 = sb("xwo16", [P, 2, PAIRS, D], F16)
        g16 = sb("xg16", [DC, 2, 2, PAIRS, D], F16)
        r16 = sb("xr16", [DC, 2, 2, PAIRS, D], F16)
        ct = sb("xct", [DC, 2, B + 1, SKV], F16)
        ct_now = sb("xct_now", [DC, 2, SKV], F16)
        a16 = sb("xa16", [P, 2, 2, XW], F16)
        vw16 = sb("xvw16", [P, 2, 2, PAIRS * D], F16)
        es = sb("xes", [P, 2, XW], F32)
        mx = sb("xmx", [P, 2, XH], F32)
        rs = sb("xrs", [P, 2, XH], F32)
        pt16 = sb("xpt16", [P, 2, XW], F16)
        prep = ctx.enter_context(nc.psum_tensor("xprep", [P, XW], F32))
        turned = ctx.enter_context(nc.psum_tensor("xturned", [P, XW], F32))
        score = [ctx.enter_context(nc.psum_tensor(f"xscore{k}", [P, XW], F32)) for k in range(2)]
        loaded, w_turned, w_high, w_low = sem("xa_loaded"), sem("xa_w_turned"), sem("xa_w_high"), sem("xa_w_low")
        wo_high, joined, joined_high, joined_low = sem("xa_wo_high"), sem("xa_joined"), sem("xa_joined_high"), sem("xa_joined_low")
        bias_added, ctx_copied, dve_steps = sem("xa_bias_added"), sem("xa_ctx_copied"), sem("xa_dve_steps")
        prep_ready, prep_hi, prep_lo = sem("xa_prep_ready"), sem("xa_prep_hi"), sem("xa_prep_lo")
        scores_ready, shifted, e_ready, recip_ready = sem("xa_scores_ready"), sem("xa_shifted"), sem("xa_e_ready"), sem("xa_recip_ready")
        p_ready, pt_ready, pt_hi, pt_lo = sem("xa_p_ready"), sem("xa_pt_ready"), sem("xa_pt_hi"), sem("xa_pt_lo")
        pv_ready, added, pad_clear = sem("xa_pv_ready"), sem("xa_added"), sem("xa_pad_clear")
        block = ctx.enter_context(nc.Block())
        turns = [(wqt, score[0], P, WS, D), (wkt, score[1], P, WS, DC), (wvt, turned, P, WS, DC), (ct, prep, DC, 1.0, P)]
        joins = [(g16, (score[0], score[1])), (r16, (turned, prep))]

        def turned_view(n):
            dst, src, rows, scale, width = turns[n]
            if n == 3:
                return ([dst[:, a, 0:B].rearrange("p b k -> p (b k)") for a in range(2)], src[0:DC, 0:B * SKV], scale)
            return ([dst[:, a] for a in range(2)], src[:].rearrange("p (j n) -> p j n", n=P)[:, :, 0:width], scale)

        @block.sync
        def _(sp):
            sp.dma_start(wq[:], w["L0_xattn_w_q"]).then_inc(loaded, 16)
            sp.dma_start(wk[:], w["L0_xattn_w_k"]).then_inc(loaded, 16)
            sp.dma_start(wv[:], w["L0_xattn_w_v"]).then_inc(loaded, 16)
            sp.dma_start(cx[:], w["ctx_768"].rearrange("(m c) k d -> (c k) m d", c=2)).then_inc(loaded, 16)
            sp.dma_start(wo[:], w["L0_xattn_w_out"].rearrange("(j p) d -> p j d", p=P)).then_inc(loaded, 16)
            sp.dma_start(bo[:], w["L0_xattn_b_out"].partition_broadcast(P)).then_inc(loaded, 16)

        @block.gpsimd
        def _(pool):
            nc.gpsimd.memset(ct[:, :, B, :], 0.0).then_inc(pad_clear, 1)
            pool.wait_ge(pad_clear, 1)
            nc.gpsimd.memset(g.xt_hi[:, B, :], 0.0).then_inc(pad_clear, 1)
            pool.wait_ge(pad_clear, 2)
            nc.gpsimd.memset(g.xt_lo[:, B, :], 0.0).then_inc(pad_clear, 1)
            pool.wait_ge(pad_clear, 3)
            pool.wait_ge(loaded, 96)
            for n in range(4):
                at = slice(n * TILES // 4, (n + 1) * TILES // 4)
                if n:
                    pool.wait_ge(bias_added, n)
                nc.gpsimd.tensor_tensor(g.x[:, at], g.x[:, at], bo[:].unsqueeze(1).to_broadcast([P, TILES // 4, D]),
                                        ALU.add).then_inc(bias_added, 1)

            def normalise(count, k):
                pool.wait_ge(recip_ready, count)
                p = es[:, k].rearrange("p (h n) -> p h n", n=SKV)
                nc.gpsimd.tensor_tensor(p, p, rs[:, k].unsqueeze(2).to_broadcast([P, XH, SKV]),
                                        ALU.mult).then_inc(p_ready, 1)

            normalise(1, 0)
            with pool.Fori(0, TILES // 4) as i:
                for j in range(4):
                    normalise(i * 4 + j + 2, (j + 1) % 2)

        @block.scalar
        def _(act):
            act.wait_ge(loaded, 96)
            for n in range(4):
                hi, src, scale = turned_view(n)
                act.wait_ge(w_turned, n + 1)
                nc.scalar.activation(hi[0], src, ACT.Copy, scale=scale).then_inc(w_high, 1)
            nc.scalar.activation(wo16[:, 0], wo[:], ACT.Copy, scale=WS).then_inc(wo_high, 1)
            for n, (dst, src) in enumerate(joins):
                for e in range(2):
                    act.wait_ge(joined, 2 * n + e + 1)
                    nc.scalar.activation(dst[:, 0, e].rearrange("p j d -> p (j d)"), src[e][0:DC, :], ACT.Copy,
                                         scale=1 / WS).then_inc(joined_high, 1)

            def prepared(count, dst):
                act.wait_ge(prep_ready, count)
                nc.scalar.activation(dst, prep[:], ACT.Copy).then_inc(prep_hi, 1)

            def exponent(count, k):
                act.wait_ge(shifted, count)
                nc.scalar.activation(es[:, k], es[:, k], ACT.Exp, scale=XD ** -0.5 / WS).then_inc(e_ready, 1)

            prepared(1, a16[:, 0, 0])
            prepared(2, vw16[:, 0, 0])
            exponent(1, 0)
            with act.Fori(0, TILES // 4) as i:
                for j in range(4):
                    prepared(i * 4 + j + 3, (a16, vw16)[j % 2][:, 1 - j // 2, 0])
                    act.wait_ge(pt_ready, i * 4 + j + 1)
                    nc.scalar.activation(pt16[:, 0], turned[:], ACT.Copy).then_inc(pt_hi, 1)
                    exponent(i * 4 + j + 2, (j + 1) % 2)

        @block.vector
        def _(dve):
            step = Chain(dve, dve_steps)
            for n in range(4):
                (hi, lo), src, scale = turned_view(n)
                dve.wait_ge(w_high, n + 1)
                if n < 3:
                    for j in range(PAIRS):
                        last = nc.vector.scalar_tensor_tensor(out=lo[:, j], in0=src[:, j], scalar=scale, in1=hi[:, j],
                                                              op0=ALU.mult, op1=ALU.subtract)
                else:
                    last = nc.vector.tensor_tensor(lo, src, hi, ALU.subtract)
                last.then_inc(w_low, 1)
            dve.wait_ge(wo_high, 1)
            nc.vector.scalar_tensor_tensor(out=wo16[:, 1], in0=wo[:], scalar=WS, in1=wo16[:, 0], op0=ALU.mult,
                                           op1=ALU.subtract).then_inc(w_low, 1)
            for n, (dst, src) in enumerate(joins):
                for e in range(2):
                    dve.wait_ge(joined_high, 2 * n + e + 1)
                    nc.vector.scalar_tensor_tensor(out=dst[:, 1, e].rearrange("p j d -> p (j d)"), in0=src[e][0:DC, :],
                                                   scalar=1 / WS, in1=dst[:, 0, e].rearrange("p j d -> p (j d)"),
                                                   op0=ALU.mult, op1=ALU.subtract).then_inc(joined_low, 1)
            dve.sem_inc(prep_lo, 1)
            dve.sem_inc(pt_lo, 1)
            dve.sem_inc(added, 1)

            def prepared(count, hi, lo):
                dve.wait_ge(prep_hi, count)
                nc.vector.tensor_tensor(lo, prep[:], hi, ALU.subtract).then_inc(prep_lo, 1)

            def shift(count, k):
                s = score[k][:].rearrange("p (h n) -> p h n", n=SKV)
                dve.wait_ge(scores_ready, count)
                step(nc.vector.tensor_reduce(mx[:, k], s, AX.X, ALU.max))
                step.settle()
                nc.vector.tensor_tensor(es[:, k].rearrange("p (h n) -> p h n", n=SKV), s,
                                        mx[:, k].unsqueeze(2).to_broadcast([P, XH, SKV]),
                                        ALU.subtract).then_inc(shifted, 1)

            def total(count, k):
                dve.wait_ge(e_ready, count)
                step(nc.vector.tensor_reduce(mx[:, k], es[:, k].rearrange("p (h n) -> p h n", n=SKV), AX.X, ALU.add))
                step.settle()
                nc.vector.reciprocal(rs[:, k], mx[:, k]).then_inc(recip_ready, 1)

            def copy_ctx(b):
                nc.vector.tensor_copy(ct_now[:], ct[:, :, b, :]).then_inc(ctx_copied, 1)

            dve.wait_ge(w_low, 5)
            copy_ctx(0)
            prepared(1, a16[:, 0, 0], a16[:, 0, 1])
            prepared(2, vw16[:, 0, 0], vw16[:, 0, 1])
            shift(1, 0)
            total(1, 0)
            dve.wait_ge(bias_added, 4)
            dve.wait_ge(pad_clear, 3)
            with step.loop(TILES // 4, 8) as i:
                for j in range(4):
                    if j % 2 == 0:
                        copy_ctx(i * 2 + 1 + j // 2)
                    shift(i * 4 + j + 2, (j + 1) % 2)
                    dst = (a16, vw16)[j % 2][:, 1 - j // 2]
                    prepared(i * 4 + j + 3, dst[:, 0], dst[:, 1])
                    dve.wait_ge(pt_hi, i * 4 + j + 1)
                    nc.vector.tensor_tensor(pt16[:, 1], turned[:], pt16[:, 0], ALU.subtract).then_inc(pt_lo, 1)
                    total(i * 4 + j + 2, (j + 1) % 2)
                    dve.wait_ge(pv_ready, i * 4 + j + 1)
                    xs = g.x[:, i * 4 + j, :]
                    nc.vector.scalar_tensor_tensor(out=xs, in0=score[j % 2][:, 0:D], scalar=1 / WS, in1=xs,
                                                   op0=ALU.mult, op1=ALU.add).then_inc(added, 1)
            dve.wait_ge(added, TILES + 1)

        @block.tensor
        def _(pe):
            pe.wait_ge(loaded, 96)
            for j in range(PAIRS):
                last = nc.tensor.transpose(score[0][:, j * P:j * P + P], wq[:, j * P:j * P + P], g.ident[:])
            last.then_inc(w_turned, 1)
            for src, to in ((wk, score[1]), (wv, turned)):
                for j in range(PAIRS):
                    last = nc.tensor.transpose(to[:, j * P:j * P + DC], src[:, j * P:j * P + P],
                                               g.ident[0:DC, 0:DC])
                last.then_inc(w_turned, 1)
            for m in range(B // 2):
                last = nc.tensor.transpose(prep[0:DC, m * P:m * P + P], cx[:, m], g.ident[:])
            last.then_inc(w_turned, 1)
            pe.wait_ge(w_low, 5)
            for dst, lhs, rhs in ((joins[0][1], wkt, wqt), (joins[1][1], wvt, wo16)):
                for e in range(2):
                    rows = slice(XD * e, XD * e + XD)
                    for j in range(PAIRS):
                        last = product3(dst[e][0:DC, j * D:j * D + D], [lhs[rows, a, j, :] for a in range(2)],
                                        [rhs[rows, a, j, :] for a in range(2)], True, True, pe=nc.tensor)
                    last.then_inc(joined, 1)

            def prepare_a(count, b):
                pe.wait_ge(prep_lo, count)
                for n in range(XH):
                    last = product3(prep[:, n * SKV:n * SKV + SKV], [g16[:, a, n % 2, n // 2, :] for a in range(2)],
                                    [ct[:, a, b, :] for a in range(2)], True, True, pe=nc.tensor)
                last.then_inc(prep_ready, 1)

            def prepare_vw(count, copied):
                pe.wait_ge(prep_lo, count)
                pe.wait_ge(ctx_copied, copied)
                for e in range(2):
                    for n in range(2):
                        cols = slice(n * 512, n * 512 + 512)
                        last = product3(prep[SKV * e:SKV * e + SKV, cols], (ct_now[:, 0], ct_now[:, 1]),
                                        [r16[:, a, e].rearrange("p j d -> p (j d)")[:, cols] for a in range(2)],
                                        True, True, pe=nc.tensor)
                last.then_inc(prep_ready, 1)

            def scores(count, batch, half, k, buf):
                pe.wait_ge(added, count)
                for n in range(2):
                    cols = slice(n * 512, n * 512 + 512)
                    last = product3(score[k][:, cols], [x[:, batch, PAD + half * P:PAD + half * P + P]
                                                        for x in (g.xt_hi, g.xt_lo)],
                                    [a16[:, buf, a, cols] for a in range(2)], True, True, pe=nc.tensor)
                last.then_inc(scores_ready, 1)

            pe.wait_ge(joined_low, 4)
            prepare_a(1, 0)
            prepare_vw(2, 1)
            pe.wait_ge(prep_lo, 2)
            scores(1, 0, 0, 0, 0)
            pe.wait_ge(pad_clear, 3)
            with pe.Fori(0, TILES // 4) as i:
                for j in range(4):
                    if j % 2 == 0:
                        prepare_a(i * 4 + j + 3, i * 2 + 1 + j // 2)
                    else:
                        prepare_vw(i * 4 + j + 3, i * 2 + 2 + j // 2)
                        pe.wait_ge(prep_lo, i * 4 + j + 3)
                    scores(i * 4 + j + 1, i * 2 + (j + 1) // 2, (j + 1) % 2, (j + 1) % 2, (j + 1) // 2 % 2)
                    pe.wait_ge(p_ready, i * 4 + j + 1)
                    pe.wait_ge(pt_lo, i * 4 + j + 1)
                    for n in range(PAIRS):
                        last = nc.tensor.transpose(turned[:, n * P:n * P + P], es[:, j % 2, n * P:n * P + P], g.ident[:])
                    last.then_inc(pt_ready, 1)
                    pe.wait_ge(pt_lo, i * 4 + j + 2)
                    if j % 2 == 0:
                        pe.wait_ge(prep_lo, i * 4 + j + 3)
                    for n in range(PAIRS):
                        last = product3(score[j % 2][:, 0:D], [pt16[:, a, n * P:n * P + P] for a in range(2)],
                                        [vw16[:, j // 2, a, n * D:n * D + D] for a in range(2)],
                                        n == 0, n == PAIRS - 1, pe=nc.tensor)
                    last.then_inc(pv_ready, 1)


def experts(nc, g, w):
    WS = 64.0
    GROUP = 4
    GROUPS = TILES // GROUP
    N = GROUP * P
    with ExitStack() as ctx:
        sb = lambda n, s, d: ctx.enter_context(nc.sbuf_tensor(n, s, d))
        sem = lambda n: g.semaphore(nc, n)
        gate = sb("fgate", [P, E], F32)
        gate16 = sb("fgate16", [P, 2, E], F16)
        w1 = sb("fw1", [P, E, F], F32)
        w2 = sb("fw2", [P, E, FT, D], F32)
        b1 = sb("fb1", [P, E, FT], F32)
        b1_rows = sb("fb1_rows", [E * FT, P], F32)
        b2 = sb("fb2", [E, D], F32)
        w1h = sb("fw1h", [P, 2, E + 1, F], F16)
        w2h = sb("fw2h", [P, 2, E, FT, D], F16)
        rank = sb("frank", [P, E], F32)
        logits = sb("flogits", [P, TILES, E], F32)
        key = sb("fkey", [P, TILES, E], F32)
        first = sb("ffirst", [P, TILES, E], F32)
        second = sb("fsecond", [P, TILES, E], F32)
        combine = sb("fcombine", [P, TILES, E], F32)
        scaled = sb("fscaled", [P, TILES, E], F32)
        max1 = sb("fmax1", [P, TILES], F32)
        max2 = sb("fmax2", [P, TILES], F32)
        kmax = sb("fkmax", [P, TILES], F32)
        turned = sb("fturned", [E, GROUPS, N], F32)
        h32 = sb("fh32", [P, 2, FT, N], F32)
        h16 = sb("fh16", [P, 2, 2, FT, N], F16)
        ph = [ctx.enter_context(nc.psum_tensor(f"fph{c}", [P, N], F32)) for c in range(FT)]
        py = [ctx.enter_context(nc.psum_tensor(f"fpy{k}", [P, N], F32)) for k in range(2)]
        pl = ctx.enter_context(nc.psum_tensor("fpl", [P, N], F32))
        loaded, split_hi, split_lo, dve_steps = sem("ff_loaded"), sem("ff_split_hi"), sem("ff_split_lo"), sem("ff_dve_steps")
        rank_ready, pad_clear = sem("ff_rank_ready"), sem("ff_pad_clear")
        logits_ready, gap_ready, exp_ready = sem("ff_logits_ready"), sem("ff_gap_ready"), sem("ff_exp_ready")
        combined, comb_turned, comb_copied, bias_ready, bias_added = sem("ff_combined"), sem("ff_comb_turned"), sem("ff_comb_copied"), sem("ff_bias_ready"), sem("ff_bias_added")
        hidden_ready, gelu_ready, h_high, h_low = sem("ff_hidden_ready"), sem("ff_gelu_ready"), sem("ff_h_high"), sem("ff_h_low")
        y_ready, added = sem("ff_y_ready"), sem("ff_added")
        stored = sem("ff_stored")
        block = ctx.enter_context(nc.Block())
        TURNS = E * GROUPS

        @block.sync
        def _(sp):
            sp.dma_start(gate[:], w["L0_ffn_gate_w"]).then_inc(loaded, 16)
            sp.dma_start(b1_rows[:], w["L0_ffn_b1"].rearrange("e (c p) -> (e c) p", p=P)).then_inc(loaded, 16)
            sp.dma_start(b2[:], w["L0_ffn_b2"]).then_inc(loaded, 16)
            for n in range(4):
                at = slice(n * E // 4, (n + 1) * E // 4)
                sp.dma_start(w1[:, at], w["L0_ffn_w1"][at].rearrange("e p f -> p e f")).then_inc(loaded, 16)
                sp.dma_start(w2[:, at], w["L0_ffn_w2"][at].rearrange("e (c p) d -> p e c d", p=P)).then_inc(loaded, 16)
            y_view = g.out.rearrange("b (h p) d -> p (b h) d", p=P)
            for t in range(GROUPS):
                sp.wait_ge(added, TURNS - GROUPS + t + 1 + 2)
                at = slice(t * GROUP, (t + 1) * GROUP)
                sp.dma_start(y_view[:, at, :], g.x[:, at, :]).then_inc(stored, 16)
            sp.wait_ge(stored, 16 * GROUPS)

        @block.gpsimd
        def _(pool):
            for e in range(E):
                nc.gpsimd.memset(rank[:, e:e + 1], float(E - e)).then_inc(rank_ready, 1)
            nc.gpsimd.memset(w1h[:, :, E], 0.0).then_inc(pad_clear, 1)

        @block.scalar
        def _(act):
            act.wait_ge(loaded, 16 * 11)
            nc.scalar.activation(gate16[:, 0], gate[:], ACT.Copy, scale=WS).then_inc(split_hi, 1)
            for n in range(4):
                at = slice(n * E // 4, (n + 1) * E // 4)
                nc.scalar.activation(w1h[:, 0, at], w1[:, at], ACT.Copy, scale=WS).then_inc(split_hi, 1)
                nc.scalar.activation(w2h[:, 0, at], w2[:, at], ACT.Copy, scale=WS).then_inc(split_hi, 1)
            act.wait_ge(gap_ready, 1)
            nc.scalar.activation(max2[:], max2[:], ACT.Exp, scale=1 / WS).then_inc(exp_ready, 1)
            for t in range(GROUPS):
                act.wait_ge(comb_turned, t + 1)
                nc.scalar.activation(turned[:, t, :], py[t % 2][0:E, :], ACT.Copy).then_inc(comb_copied, 1)
            act.sem_inc(gelu_ready, FT)
            with act.Fori(0, E) as e:
                with act.Fori(0, GROUPS // 2) as t:
                    for k in range(2):
                        turn = e * GROUPS + t * 2 + k
                        for c in range(FT):
                            if c == 0:
                                act.wait_ge(h_low, turn + 1)
                            wait_apart(act, hidden_ready, turn * FT + c + 1, g.passed)
                            nc.scalar.activation(h32[:, k, c], ph[c][:], ACT.Gelu, bias=b1[:, e, c:c + 1],
                                                 scale=1 / WS).then_inc(gelu_ready, 1)
                        act.wait_ge(gelu_ready, turn * FT + 2 * FT)
                        act.wait_ge(y_ready, turn + 1)
                        nc.scalar.activation(h16[:, k, 0], h32[:, k], ACT.Copy).then_inc(h_high, 1)

        @block.vector
        def _(dve):
            step = Chain(dve, dve_steps)
            dve.wait_ge(split_hi, 1)
            nc.vector.scalar_tensor_tensor(out=gate16[:, 1], in0=gate[:], scalar=WS, in1=gate16[:, 0], op0=ALU.mult,
                                           op1=ALU.subtract).then_inc(split_lo, 1)
            for n in range(4):
                at = slice(n * E // 4, (n + 1) * E // 4)
                flat = lambda a: a.rearrange("p e f -> p (e f)")
                flat2 = lambda a: a.rearrange("p e c d -> p (e c d)")
                dve.wait_ge(split_hi, 2 * n + 3)
                nc.vector.scalar_tensor_tensor(out=flat(w1h[:, 1, at]), in0=flat(w1[:, at]), scalar=WS,
                                               in1=flat(w1h[:, 0, at]), op0=ALU.mult,
                                               op1=ALU.subtract).then_inc(split_lo, 1)
                nc.vector.scalar_tensor_tensor(out=flat2(w2h[:, 1, at]), in0=flat2(w2[:, at]), scalar=WS,
                                               in1=flat2(w2h[:, 0, at]), op0=ALU.mult,
                                               op1=ALU.subtract).then_inc(split_lo, 1)
            wide = lambda a: a[:].unsqueeze(2).to_broadcast([P, TILES, E])

            def pick(one_hot, values, largest):
                step(nc.vector.tensor_reduce(largest[:], values[:], AX.X, ALU.max))
                step.settle()
                step(nc.vector.tensor_tensor(key[:], values[:], wide(largest), ALU.is_equal))
                step.settle()
                step(nc.vector.tensor_tensor(key[:], key[:], rank[:].unsqueeze(1).to_broadcast([P, TILES, E]), ALU.mult))
                step.settle()
                step(nc.vector.tensor_reduce(kmax[:], key[:], AX.X, ALU.max))
                step.settle()
                step(nc.vector.tensor_tensor(one_hot[:], key[:], wide(kmax), ALU.is_equal))
                step.settle()

            dve.wait_ge(logits_ready, 1)
            step(nc.vector.tensor_copy(logits[:].rearrange("p t e -> p (t e)"), pl[:, 0:TILES * E]))
            step(nc.vector.tensor_copy(b1[:].rearrange("p e c -> p (e c)"), pl[:, TILES * E:TILES * E + E * FT]))
            step.settle()
            dve.wait_ge(rank_ready, E)
            pick(first, logits, max1)
            step(nc.vector.scalar_tensor_tensor(out=logits[:].rearrange("p t e -> p (t e)"),
                                                in0=first[:].rearrange("p t e -> p (t e)"), scalar=-1e30,
                                                in1=logits[:].rearrange("p t e -> p (t e)"), op0=ALU.mult, op1=ALU.add))
            step.settle()
            pick(second, logits, max2)
            nc.vector.tensor_tensor(max2[:], max2[:], max1[:], ALU.subtract).then_inc(gap_ready, 1)
            dve.wait_ge(exp_ready, 1)
            step(nc.vector.tensor_scalar(max1[:], max2[:], 1.0, None, ALU.add))
            step.settle()
            step(nc.vector.reciprocal(max1[:], max1[:]))
            step.settle()
            step(nc.vector.tensor_tensor(max2[:], max2[:], max1[:], ALU.mult))
            step(nc.vector.tensor_tensor(first[:], first[:], wide(max1), ALU.mult))
            step.settle()
            step(nc.vector.tensor_tensor(second[:], second[:], wide(max2), ALU.mult))
            step.settle()
            step(nc.vector.tensor_tensor(combine[:], first[:], second[:], ALU.add))
            step.settle()
            nc.vector.tensor_scalar(scaled[:], combine[:], 1 / WS, None, ALU.mult).then_inc(combined, 1)
            for t in range(GROUPS):
                at = slice(t * GROUP, (t + 1) * GROUP)
                dve.wait_ge(bias_ready, t + 1)
                nc.vector.tensor_tensor(g.x[:, at].rearrange("p t d -> p (t d)"),
                                        g.x[:, at].rearrange("p t d -> p (t d)"), ph[t % FT][:],
                                        ALU.add).then_inc(bias_added, 1)
            dve.wait_ge(bias_added, GROUPS)
            dve.sem_inc(added, 2)
            dve.sem_inc(h_low, 2)
            with dve.Fori(0, E) as e:
                with dve.Fori(0, GROUPS // 2) as t:
                    for k in range(2):
                        turn = e * GROUPS + t * 2 + k
                        dve.wait_ge(h_high, turn + 1)
                        nc.vector.tensor_tensor(h16[:, k, 1], h32[:, k], h16[:, k, 0], ALU.subtract).then_inc(h_low, 1)
                        dve.wait_ge(y_ready, turn + 3)
                        for m in range(GROUP):
                            tile = t * 2 * GROUP + k * GROUP + m
                            xs = g.x[:, tile, :]
                            last = nc.vector.scalar_tensor_tensor(
                                out=xs, in0=py[k][:, m * D:m * D + D], scalar=scaled[:, tile, bass.ds(e, 1)],
                                in1=xs, op0=ALU.mult, op1=ALU.add)
                        last.then_inc(added, 1)

        @block.tensor
        def _(pe):
            pe.wait_ge(loaded, 16 * 11)
            pe.wait_ge(split_lo, 1)
            nc.tensor.transpose(pl[:, TILES * E:TILES * E + E * FT], b1_rows[:], g.ident[0:E * FT, 0:E * FT])
            for t in range(TILES):
                at = slice(PAD + t % 2 * P, PAD + t % 2 * P + P)
                last = product3(pl[:, t * E:t * E + E], (g.xt_hi[:, t // 2, at], g.xt_lo[:, t // 2, at]),
                                (gate16[:, 0], gate16[:, 1]), True, True, pe=nc.tensor)
            last.then_inc(logits_ready, 1)
            pe.wait_ge(combined, 1)
            for t in range(GROUPS):
                if t >= 2:
                    pe.wait_ge(comb_copied, t - 1)
                for m in range(GROUP):
                    last = nc.tensor.transpose(py[t % 2][0:E, m * P:m * P + P], combine[:, t * GROUP + m, :], g.ident[:])
                last.then_inc(comb_turned, 1)
            for t in range(GROUPS):
                pe.wait_ge(comb_copied, t + 1)
                if t >= FT:
                    pe.wait_ge(bias_added, t - FT + 1)
                for m in range(GROUP):
                    last = nc.tensor.matmul(ph[t % FT][:, m * D:m * D + D], turned[:, t, m * P:m * P + P], b2[:],
                                            start=True, stop=True)
                last.then_inc(bias_ready, 1)
            pe.wait_ge(split_lo, 9)
            pe.sem_inc(y_ready, 2)

            def hidden(turn, e, t, k):
                for c in range(FT):
                    pe.wait_ge(gelu_ready, turn * FT + c + 1)
                    batch = t * 4 + k * 2
                    w_at = lambda a: w1h[:, a, e, c * P:c * P + P]
                    last = product3(ph[c][:], (w_at(0), w_at(1)),
                                    [x[:, bass.ds(batch, 2), PAD:PAD + L] for x in (g.xt_hi, g.xt_lo)],
                                    True, True, pe=nc.tensor)
                    last.then_inc(hidden_ready, 1)

            def outputs(turn, e, k):
                pe.wait_ge(added, turn + 1)
                pe.wait_ge(h_low, turn + 3)
                for m in range(GROUP):
                    cols = slice(m * P, m * P + P)
                    for c in range(FT):
                        last = product3(py[k][:, m * D:m * D + D], (h16[:, k, 0, c, cols], h16[:, k, 1, c, cols]),
                                        (w2h[:, 0, e, c, :], w2h[:, 1, e, c, :]), c == 0, c == FT - 1, pe=nc.tensor)
                last.then_inc(y_ready, 1)

            pe.wait_ge(pad_clear, 1)
            pe.wait_ge(added, 2)
            hidden(0, 0, 0, 0)
            with pe.Fori(0, E) as e:
                with pe.Fori(0, GROUPS // 2 - 1) as t:
                    turn = e * GROUPS + t * 2
                    hidden(turn + 1, e, t, 1)
                    outputs(turn, e, 0)
                    hidden(turn + 2, e, t + 1, 0)
                    outputs(turn + 1, e, 1)
                turn = e * GROUPS + GROUPS - 2
                hidden(turn + 1, e, GROUPS // 2 - 1, 1)
                outputs(turn, e, 0)
                hidden(turn + 2, e + 1, 0, 0)
                outputs(turn + 1, e, 1)


_INS = ["x", "ctx_768"] + ["L0_attn_" + n for n in (
    "q_w", "k_w", "v_w", "b_w", "q_cw", "k_cw", "v_cw", "mlp1_w", "mlp1_b", "mlp2_w", "mlp2_b", "logit_temp",
    "conv_res_logit", "norm_w", "o_w")] + ["L0_xattn_" + n for n in ("w_q", "w_k", "w_v", "w_out", "b_out")] + [
    "L0_ffn_" + n for n in ("gate_w", "w1", "b1", "w2", "b2")]


def decoder_layer(nc, w, out):
    with ExitStack() as ctx:
        g = Shared(nc, ctx)
        g.out = out
        with ExitStack() as attention:
            g.hold_attention(nc, attention)
            load(nc, g, w)
            norm_and_transpose(nc, g)
            project(nc, g, w)
            delta_rule(nc, g)
            with ExitStack() as branches:
                g.hold_fir(nc, branches)
                fir(nc, g, w)
                gate_and_add(nc, g, w)
        g.clear_semaphores(nc)
        norm_and_transpose(nc, g, "ln2")
        cross_attention(nc, g, w)
        norm_and_transpose(nc, g, "ln3")
        experts(nc, g, w)


def kernel(**inputs):
    import numpy as np
    import concourse.bacc as bacc
    from concourse.bass_utils import run_bass_kernel_spmd

    nc = bacc.Bacc("TRN2", target_bir_lowering=False, num_devices=1)
    laid_out = {n: inputs[n] for n in _INS}
    for n in ("short", "long"):
        laid_out["fir_" + n] = lay_out_fir(inputs[f"L0_attn_fir_{n}_w"])
    arrays, w = {}, {}
    for name, value in laid_out.items():
        a = np.ascontiguousarray(value)
        arrays[f"in_{name}"] = a
        w[name] = nc.dram_tensor(f"in_{name}", a.shape, mybir.dt.from_np(a.dtype), kind="ExternalInput").ap()
    out = nc.dram_tensor("out_x", (B, L, D), F32, kind="ExternalOutput").ap()
    decoder_layer(nc, w, out)
    r = run_bass_kernel_spmd(nc, [arrays], core_ids=[0])
    return r.results[0]["out_x"]
```

```python
from contextlib import ExitStack, contextmanager

import concourse.bass as bass
from concourse import mybir

F32 = mybir.dt.float32
F16 = mybir.dt.float16
I32 = mybir.dt.int32
ALU = mybir.AluOpType
ACT = mybir.ActivationFunctionType
AX = mybir.AxisListType

P = 128
B, L, D = 16, 256, 128
TILES = B * L // P
H, DH = 4, 32
C = 32
CT = P // C
NCH = L // C
TAPS = 4
PAD = TAPS - 1
FS, FL = 5, 64
XH, XD, SKV, DC = 16, 64, 64, 96
E, F = 8, 512
FT = F // P
BLOCKS = (2 * B * L + E * (P - 1)) // P

FG = 16

W_SCALE = 1024.0
V_SCALE = 64.0
ST_SCALE = 64.0


def wait_apart(eng, sem, value, passed):
    eng.wait_ge(sem, value)
    eng.sem_inc(passed, 1)


class Chain:

    def __init__(self, eng, sem):
        self.eng, self.sem, self.base, self.k = eng, sem, 0, 0

    def __call__(self, ins):
        self.k += 1
        return ins.then_inc(self.sem, 1)

    def settle(self):
        self.eng.wait_ge(self.sem, self.base + self.k)

    def settle_apart(self, passed):
        wait_apart(self.eng, self.sem, self.base + self.k, passed)

    @contextmanager
    def loop(self, n, per):
        start = self.base + self.k
        with self.eng.Fori(0, n) as i:
            self.base, self.k = i * per + start, 0
            yield i
            assert self.k == per, f"{self.k} steps a turn"
        self.base, self.k = start + n * per, 0


def product3(out, a, b, start, stop, **kw):
    bass_tensor = kw.pop("pe")
    (ah, al), (bh, bl) = a, b
    bass_tensor.matmul(out, ah, bh, start=start, stop=False, **kw)
    bass_tensor.matmul(out, ah, bl, start=False, stop=False, **kw)
    return bass_tensor.matmul(out, al, bh, start=False, stop=stop, **kw)


class Shared:

    def __init__(self, nc, ctx):
        sb = lambda n, s, d: ctx.enter_context(nc.sbuf_tensor(n, s, d))
        self.x = sb("x_tok", [P, TILES, D], F32)
        self.xt_hi = sb("xt_hi", [P, B + 1, PAD + L + 1], F16)
        self.xt_lo = sb("xt_lo", [P, B + 1, PAD + L + 1], F16)
        self.ident = sb("ident", [P, P], F32)
        self.ident16 = sb("ident16", [P, P], F16)
        self.causal = sb("causal", [P, C], F32)
        self.eps5 = sb("eps5", [P, 1], F32)
        self.eps6 = sb("eps6", [P, 1], F32)
        self.semaphores = []
        self.passed = ctx.enter_context(nc.semaphore("passed"))

    def semaphore(self, nc, name):
        self.semaphores.append(nc.alloc_semaphore(name))
        return self.semaphores[-1]

    def clear_semaphores(self, nc):
        nc.clear_and_free_semaphores(self.semaphores)
        nc.all_engine_barrier()
        self.semaphores = []

    def hold_attention(self, nc, ctx):
        sb = lambda n, s, d: ctx.enter_context(nc.sbuf_tensor(n, s, d))
        self.qk = sb("qk", [P, TILES, 2 * D], F32)
        self.v = sb("v", [P, TILES, D], F32)
        self.qk_norm = sb("qk_norm", [P, TILES, 2 * H], F32)
        self.beta = sb("beta", [P, TILES, H], F32)
        self.delta = sb("delta", [P, TILES, D], F32)

    def hold_fir(self, nc, ctx):
        sb = lambda n, s, d: ctx.enter_context(nc.sbuf_tensor(n, s, d))
        self.short = sb("short", [P, TILES, D], F32)
        self.long = sb("long", [P, TILES, D], F32)


def norm_and_transpose(nc, g, stage="ln1"):
    GROUP = 4
    GROUPS = TILES // GROUP
    with ExitStack() as ctx:
        sb = lambda n, s, d: ctx.enter_context(nc.sbuf_tensor(n, s, d))
        sem = lambda n: g.semaphore(nc, n)
        stats = sb(f"{stage}_stats", [P, TILES, 6], F32)
        mean_var = sb(f"{stage}_mean_var", [P, TILES, 2], F32)
        rstd = sb(f"{stage}_rstd", [P, TILES], F32)
        xn = sb(f"{stage}_xn", [P, 2, GROUP, D], F32)
        pt = [ctx.enter_context(nc.psum_tensor(f"{stage}_pt{k}", [P, GROUP * P], F32)) for k in range(2)]
        dve_steps, var_ready, root_ready = sem(f"{stage}_dve_steps"), sem(f"{stage}_var_ready"), sem(f"{stage}_root_ready")
        normed, turned, hi_ready, lo_ready = sem(f"{stage}_normed"), sem(f"{stage}_turned"), sem(f"{stage}_hi_ready"), sem(f"{stage}_lo_ready")
        block = ctx.enter_context(nc.Block())
        of_group = lambda x, i: x[:, bass.ds(i * 2, 2), PAD:PAD + L]
        bank = lambda k: pt[k][:].rearrange("p (b l) -> p b l", l=L)

        @block.vector
        def _(dve):
            step = Chain(dve, dve_steps)
            for t in range(TILES):
                step(nc.vector.bn_stats(stats[:, t, :], g.x[:, t, :]))
            step.settle()
            for t in range(TILES):
                step(nc.vector.bn_aggr(mean_var[:, t, :], stats[:, t, :]))
            step.settle()
            step(nc.vector.memset(g.eps5[:], 1e-5))
            nc.vector.memset(g.eps6[:], 1e-6).then_inc(var_ready, 1)
            dve.wait_ge(root_ready, 1)
            step(nc.vector.reciprocal(rstd[:], rstd[:]))
            step.settle()
            dve.sem_inc(lo_ready, 2)

            def normalise(i, k):
                dve.wait_ge(turned, i + 1)
                for m in range(GROUP):
                    tile = i * GROUP + m
                    last = nc.vector.tensor_scalar(xn[:, k, m, :], g.x[:, tile, :], mean_var[:, tile, 0:1],
                                                   rstd[:, bass.ds(tile, 1)], ALU.subtract, ALU.mult)
                last.then_inc(normed, 1)

            def low(i, k):
                dve.wait_ge(hi_ready, i + 1)
                nc.vector.tensor_tensor(of_group(g.xt_lo, i), bank(k), of_group(g.xt_hi, i),
                                        ALU.subtract).then_inc(lo_ready, 1)

            normalise(0, 0)
            with dve.Fori(0, GROUPS // 2 - 1) as t:
                for k in range(2):
                    normalise(t * 2 + k + 1, 1 - k)
                    low(t * 2 + k, k)
            normalise(GROUPS - 1, 1)
            low(GROUPS - 2, 0)
            low(GROUPS - 1, 1)

        @block.tensor
        def _(pe):
            pe.sem_inc(turned, 2)
            with pe.Fori(0, GROUPS // 2) as t:
                for k in range(2):
                    pe.wait_ge(normed, t * 2 + k + 1)
                    pe.wait_ge(lo_ready, t * 2 + k + 1)
                    for m in range(GROUP):
                        last = nc.tensor.transpose(pt[k][:, m * P:m * P + P], xn[:, k, m, :], g.ident[:])
                    last.then_inc(turned, 1)

        @block.scalar
        def _(act):
            act.wait_ge(var_ready, 1)
            nc.scalar.activation(rstd[:], mean_var[:, :, 1], ACT.Sqrt, bias=g.eps5[:]).then_inc(root_ready, 1)
            with act.Fori(0, GROUPS // 2) as t:
                for k in range(2):
                    act.wait_ge(turned, t * 2 + k + 3)
                    nc.scalar.activation(of_group(g.xt_hi, t * 2 + k), bank(k), ACT.Copy).then_inc(hi_ready, 1)


def load(nc, g, w):
    with ExitStack() as ctx:
        sem = lambda n: g.semaphore(nc, n)
        x_loaded, pool_steps = sem("x_loaded"), sem("const_steps")
        block = ctx.enter_context(nc.Block())

        @block.sync
        def _(sp):
            x_view = w["x"].rearrange("b (h p) d -> p (b h) d", p=P)
            for n in range(4):
                sp.dma_start(g.x[:, 8 * n:8 * n + 8, :], x_view[:, 8 * n:8 * n + 8, :]).then_inc(x_loaded, 16)
            sp.wait_ge(x_loaded, 64)

        @block.gpsimd
        def _(pool):
            step = Chain(pool, pool_steps)
            step(nc.gpsimd.memset(g.ident[:], 0.0))
            step(nc.gpsimd.memset(g.causal[:], 1.0))
            step(nc.gpsimd.memset(g.xt_hi[:, :, 0:PAD], 0.0))
            step(nc.gpsimd.memset(g.xt_lo[:, :, 0:PAD], 0.0))
            step.settle()
            step(nc.gpsimd.affine_select(out=g.ident[:], in_=g.ident[:], compare_op=ALU.not_equal, fill=1.0,
                                         base=0, pattern=[[-1, P]], channel_multiplier=1))
            for c in range(CT):
                step.settle()
                rows = g.causal[C * c:C * c + C, :]
                step(nc.gpsimd.affine_select(out=rows, in_=rows, compare_op=ALU.is_ge, fill=0.0, base=0,
                                             pattern=[[1, C]], channel_multiplier=-1))
            step.settle()
            step(nc.gpsimd.tensor_scalar(g.ident16[:], g.ident[:], 1.0, None, ALU.mult))
            step.settle()


def project(nc, g, w):
    with ExitStack() as ctx:
        sb = lambda n, s, d: ctx.enter_context(nc.sbuf_tensor(n, s, d))
        sem = lambda n: g.semaphore(nc, n)
        QKV = 3 * D + H
        w_nat = sb("w_nat", [P, 3, D], F32)
        cw = sb("cw", [P, 3, TAPS], F32)
        b_w = sb("b_w_nat", [H, D], F32)
        w_tap = sb("w_tap", [P, TAPS, 3, D], F32)
        b_tap = sb("b_tap", [H, D], F32)
        wc_hi = sb("wc_hi", [P, TAPS, QKV], F16)
        wc_lo = sb("wc_lo", [P, TAPS, QKV], F16)
        square = sb("square", [P, 2, 2 * D], F32)
        pw = [ctx.enter_context(nc.psum_tensor(f"pw{j}", [P, 512], F32)) for j in range(2)]
        pq = [ctx.enter_context(nc.psum_tensor(f"pq{j}", [P, 512], F32)) for j in range(4)]
        loaded, dve_steps = sem("loaded"), sem("dve_steps")
        taps_ready, tap_turned, tap_hi_ready = sem("taps_ready"), sem("tap_turned"), sem("tap_hi_ready")
        weights_ready, qkv_ready, qkv_stored = sem("weights_ready"), sem("qkv_ready"), sem("qkv_stored")
        beta_stored, squared, squares_summed = sem("beta_stored"), sem("squared"), sem("squares_summed")
        root_ready = sem("root_ready")
        block = ctx.enter_context(nc.Block())

        @block.sync
        def _(sp):
            for n, name in enumerate(("q", "k", "v")):
                sp.dma_start(w_nat[:, n, :], w[f"L0_attn_{name}_w"]).then_inc(loaded, 16)
                sp.dma_start(cw[:, n, :], w[f"L0_attn_{name}_cw"]).then_inc(loaded, 16)
            sp.dma_start(b_w[:], w["L0_attn_b_w"]).then_inc(loaded, 16)

        @block.gpsimd
        def _(pool):
            with pool.Fori(0, B) as b:
                for k in range(2):
                    pool.wait_ge(qkv_stored, b * 2 + k + 5)
                    pool.wait_ge(squares_summed, b * 2 + k + 1)
                    qk = g.qk[:, b * 2 + k, :]
                    nc.gpsimd.tensor_tensor(square[:, k, :], qk, qk, ALU.mult).then_inc(squared, 1)

        @block.vector
        def _(dve):
            step = Chain(dve, dve_steps)
            dve.sem_inc(squares_summed, 2)
            dve.wait_ge(loaded, 16 * 7)
            for j in range(TAPS):
                for n in range(3):
                    step(nc.vector.tensor_scalar(w_tap[:, j, n, :], w_nat[:, n, :], cw[:, n, j:j + 1],
                                                 W_SCALE, ALU.mult, ALU.mult))
            nc.vector.tensor_scalar(b_tap[:], b_w[:], W_SCALE, None, ALU.mult).then_inc(taps_ready, 1)
            for j in range(TAPS):
                n = QKV if j == TAPS - 1 else 3 * D
                dve.wait_ge(tap_hi_ready, j + 1)
                nc.vector.tensor_tensor(wc_lo[:, j, 0:n], pw[j % 2][:, 0:n], wc_hi[:, j, 0:n],
                                        ALU.subtract).then_inc(weights_ready, 1)
            with dve.Fori(0, B // 2) as b:
                for k in range(4):
                    dve.wait_ge(qkv_ready, b * 4 + k + 1)
                    nc.vector.tensor_copy(g.beta[:, b * 4 + k, :], pq[k][:, 3 * D:QKV]).then_inc(beta_stored, 1)
                    dve.wait_ge(squared, b * 4 + k + 1)
                    nc.vector.tensor_reduce(g.qk_norm[:, b * 4 + k, :],
                                            square[:, k % 2, :].rearrange("p (h d) -> p h d", d=DH),
                                            AX.X, ALU.add).then_inc(squares_summed, 1)
            dve.wait_ge(root_ready, 2)
            step(nc.vector.reciprocal(g.qk_norm[:], g.qk_norm[:]))
            step(nc.vector.tensor_scalar(g.beta[:], g.beta[:], 1e-6, None, ALU.max))
            step.settle()

        @block.tensor
        def _(pe):
            pe.wait_ge(taps_ready, 1)
            for j in range(TAPS):
                if j >= 2:
                    pe.wait_ge(weights_ready, j - 1)
                for n in range(3):
                    last = nc.tensor.transpose(pw[j % 2][:, n * D:(n + 1) * D], w_tap[:, j, n, :], g.ident[:])
                if j == TAPS - 1:
                    last = nc.tensor.transpose(pw[j % 2][:, 3 * D:QKV], b_tap[:], g.ident[0:H, 0:H])
                last.then_inc(tap_turned, 1)
            pe.wait_ge(weights_ready, TAPS)
            with pe.Fori(0, B // 2) as b:
                for k in range(4):
                    pe.wait_ge(qkv_stored, b * 4 + k + 1)
                    for m, j in enumerate(reversed(range(TAPS))):
                        n = QKV if j == TAPS - 1 else 3 * D
                        at = bass.ds(k % 2 * P + j, P)
                        last = product3(pq[k][:, 0:n], (g.xt_hi[:, b * 2 + k // 2, at], g.xt_lo[:, b * 2 + k // 2, at]),
                                        (wc_hi[:, j, 0:n], wc_lo[:, j, 0:n]), m == 0, m == TAPS - 1, pe=nc.tensor)
                    last.then_inc(qkv_ready, 1)

        @block.scalar
        def _(act):
            for j in range(TAPS):
                n = QKV if j == TAPS - 1 else 3 * D
                act.wait_ge(tap_turned, j + 1)
                nc.scalar.activation(wc_hi[:, j, 0:n], pw[j % 2][:, 0:n], ACT.Copy).then_inc(tap_hi_ready, 1)
            act.sem_inc(qkv_stored, 4)
            with act.Fori(0, B // 2) as b:
                for k in range(4):
                    act.wait_ge(beta_stored, b * 4 + k + 1)
                    nc.scalar.activation(g.qk[:, b * 4 + k, :], pq[k][:, 0:2 * D], ACT.Silu, scale=1 / W_SCALE)
                    nc.scalar.activation(g.v[:, b * 4 + k, :], pq[k][:, 2 * D:3 * D], ACT.Silu,
                                         scale=1 / W_SCALE).then_inc(qkv_stored, 1)
            act.wait_ge(squares_summed, TILES + 2)
            nc.scalar.activation(g.beta[:], g.beta[:], ACT.Sigmoid, scale=1 / W_SCALE).then_inc(root_ready, 1)
            nc.scalar.activation(g.qk_norm[:], g.qk_norm[:], ACT.Sqrt, bias=g.eps6[:]).then_inc(root_ready, 1)


def delta_solve(nc, g, tt, vb, ak, q16):
    with ExitStack() as ctx:
        sb = lambda n, s, d: ctx.enter_context(nc.sbuf_tensor(n, s, d))
        sem = lambda n: g.semaphore(nc, n)
        ps = lambda n: ctx.enter_context(nc.psum_tensor(n, [P, 512], F32))
        W2 = 2 * DH
        negb = sb("negb", [P, TILES, H], F32)
        bv = sb("bv", [P, TILES, H], F32)
        qkn = sb("qkn", [P, 2, 2, 2, D], F32)
        kv = sb("kv", [P, 2, 2 * H, W2], F32)
        kqt = sb("kqt", [P, 2, 2, 2, 2, P], F16)
        at = sb("at", [P, 2, 2 * H, C], F32)
        flat = g.qk[:].rearrange("p t n -> p (t n)")
        ng = flat[:, 0:TILES * H * C].rearrange("p (u s) -> p u s", s=C)
        nu = flat[:, TILES * H * C:].rearrange("p (s m) -> p s m", s=C)
        t_u = flat[:, 0:CT * C * C].rearrange("p (t c j) -> p t c j", c=CT, t=C)
        tmp = sb("fs_tmp", [P, CT * 256], F32)
        bank = [ps(f"dl{n}") for n in range(8)]

        pe_steps = sem("dl_pe_steps")
        betas, normed, scaled, vb_hi, qk_hi = sem("dl_betas"), sem("dl_normed"), sem("dl_scaled"), sem("dl_vb_hi"), sem("dl_qk_hi")
        turned, kqt_hi, kqt_ready, gram_ready = sem("dl_turned"), sem("dl_kqt_hi"), sem("dl_kqt_ready"), sem("dl_gram_ready")
        masked, at_hi, at_stored = sem("dl_masked"), sem("dl_at_hi"), sem("dl_at_stored")
        ng_ready, nu_turned, nu_dve, nu_act = sem("dl_ng_ready"), sem("dl_nu_turned"), sem("dl_nu_dve"), sem("dl_nu_act")
        t_clear, t_one, sub_dve, sub_pool = sem("dl_t_clear"), sem("dl_t_one"), sem("dl_sub_dve"), sem("dl_sub_pool")
        tt_turned, tt_hi, tt_lo = sem("dl_tt_turned"), sem("dl_tt_hi"), sem("dl_tt_lo")
        block = ctx.enter_context(nc.Block())

        @block.vector
        def _(dve):
            step = Chain(dve, sub_dve)
            nc.vector.tensor_scalar(negb[:], g.beta[:], -1.0, None, ALU.mult).then_inc(betas, 1)
            nc.vector.tensor_scalar(bv[:], g.beta[:], V_SCALE, None, ALU.mult).then_inc(betas, 1)
            dve.wait_ge(betas, 2)
            with dve.Fori(0, B // 2) as t:
                for k in range(2):
                    i = t * 2 + k
                    two = bass.ds(i * 2, 2)
                    nc.vector.tensor_tensor(
                        qkn[:, k].rearrange("p t a (h d) -> p (t a h) d", d=DH),
                        g.qk[:, two, :].rearrange("p t (h d) -> p (t h) d", d=DH),
                        g.qk_norm[:, two, :].rearrange("p t h -> p (t h)").unsqueeze(2).to_broadcast([P, 4 * H, DH]),
                        ALU.mult).then_inc(normed, 1)
                for k in range(2):
                    i = t * 2 + k
                    two = bass.ds(i * 2, 2)
                    dve.wait_ge(vb_hi, i + 1)
                    nc.vector.tensor_tensor(
                        vb[:, two, 1].rearrange("p t h w -> p t (h w)"),
                        kv[:, k].rearrange("p (t h) w -> p t (h w)", t=2),
                        vb[:, two, 0].rearrange("p t h w -> p t (h w)"), ALU.subtract)
                    dve.wait_ge(qk_hi, i + 1)
                    nc.vector.tensor_tensor(q16[:, two, 1, :], qkn[:, k, :, 0, :], q16[:, two, 0, :], ALU.subtract)
                    for half in range(2):
                        nc.vector.tensor_tensor(
                            ak[:, i * 2 + half, 1, :, DH:], qkn[:, k, half, 1, :].rearrange("p (h d) -> p h d", d=DH),
                            ak[:, i * 2 + half, 0, :, DH:], ALU.subtract)
                    dve.wait_ge(kqt_hi, i + 1)
                    nc.vector.tensor_tensor(kqt[:, k, 1].rearrange("p t a n -> p (t a n)"), bank[k][:],
                                            kqt[:, k, 0].rearrange("p t a n -> p (t a n)"),
                                            ALU.subtract).then_inc(kqt_ready, 1)
                for k in range(2):
                    i = t * 2 + k
                    two = bass.ds(i * 2, 2)
                    dve.wait_ge(gram_ready, i + 1)
                    gram = bank[2 + k][:].rearrange("p (u a n) -> p u a n", a=2, n=C)
                    nc.vector.tensor_tensor(
                        ng[:, bass.ds(i * 2 * H, 2 * H), :], gram[:, :, 1, :],
                        negb[:, two, :].rearrange("p t h -> p (t h)").unsqueeze(2).to_broadcast([P, 2 * H, C]),
                        ALU.mult)
                    dve.wait_ge(at_stored, i + 1)
                    nc.vector.tensor_tensor(at[:, k], gram[:, :, 0, :],
                                            g.causal[:].unsqueeze(1).to_broadcast([P, 2 * H, C]),
                                            ALU.mult).then_inc(masked, 1)
            for m in range(C // 4):
                if m % 2 == 0:
                    dve.wait_ge(nu_turned, m + 1)
                    nc.vector.tensor_copy(nu[:, 4 * m:4 * m + 4, :], bank[m % 8][:].rearrange("p (s m) -> p s m", s=4)
                                          ).then_inc(nu_dve, 1)
            dve.wait_ge(nu_turned, C // 4)
            nc.vector.memset(t_u[:], 0.0).then_inc(t_clear, 1)
            dve.wait_ge(t_clear, 1)
            for c in range(CT):
                ones = flat[:, c * C:c * C + (C - 1) * (CT * C + 1) + 1:CT * C + 1]
                nc.vector.memset(ones, 1.0).then_inc(t_one, 1)
            dve.wait_ge(nu_dve, C // 8)
            dve.wait_ge(nu_act, C // 8)
            dve.wait_ge(t_one, CT)
            for s in range(C - 1):
                substitute(nc.vector, step, nu, t_u, tmp, s, 0, 3)
            for m in range(C // 4):
                dve.wait_ge(tt_hi, m + 1)
                nc.vector.tensor_tensor(
                    tt[:, :, 1, :].rearrange("p t (h n) -> p t h n", h=H)[:, :, :, 4 * m:4 * m + 4],
                    bank[m % 8][:].rearrange("p (n t h) -> p t h n", n=4, h=H),
                    tt[:, :, 0, :].rearrange("p t (h n) -> p t h n", h=H)[:, :, :, 4 * m:4 * m + 4],
                    ALU.subtract).then_inc(tt_lo, 1)

        @block.gpsimd
        def _(pool):
            step = Chain(pool, sub_pool)
            pool.wait_ge(betas, 2)
            pool.sem_inc(at_stored, 2)
            with pool.Fori(0, B // 2) as t:
                for k in range(2):
                    i = t * 2 + k
                    two = bass.ds(i * 2, 2)
                    pool.wait_ge(normed, i + 1)
                    nc.gpsimd.tensor_tensor(
                        kv[:, k, :, 0:DH], g.v[:, two, :].rearrange("p t (h d) -> p (t h) d", d=DH),
                        bv[:, two, :].rearrange("p t h -> p (t h)").unsqueeze(2).to_broadcast([P, 2 * H, DH]),
                        ALU.mult).then_inc(scaled, 1)
                    for half in range(2):
                        nc.gpsimd.tensor_tensor(
                            kv[:, k, H * half:H * half + H, DH:],
                            qkn[:, k, half, 1, :].rearrange("p (h d) -> p h d", d=DH),
                            negb[:, i * 2 + half, :].unsqueeze(2).to_broadcast([P, H, DH]),
                            ALU.mult).then_inc(scaled, 1)
                for k in range(2):
                    i = t * 2 + k
                    pool.wait_ge(at_hi, i + 1)
                    nc.gpsimd.tensor_tensor(
                        ak[:, bass.ds(i * 2, 2), 1, :, 0:C], at[:, k].rearrange("p (t h) n -> p t h n", t=2),
                        ak[:, bass.ds(i * 2, 2), 0, :, 0:C], ALU.subtract).then_inc(at_stored, 1)
            pool.wait_ge(nu_dve, C // 8)
            pool.wait_ge(nu_act, C // 8)
            pool.wait_ge(t_one, CT)
            for s in range(C - 1):
                substitute(nc.gpsimd, step, nu, t_u, tmp, s, 3, 4)

        @block.scalar
        def _(act):
            with act.Fori(0, B // 2) as t:
                for k in range(2):
                    i = t * 2 + k
                    two = bass.ds(i * 2, 2)
                    act.wait_ge(scaled, i * 3 + 3)
                    nc.scalar.activation(vb[:, two, 0].rearrange("p t h w -> p t (h w)"),
                                         kv[:, k].rearrange("p (t h) w -> p t (h w)", t=2),
                                         ACT.Copy).then_inc(vb_hi, 1)
                    nc.scalar.activation(q16[:, two, 0, :], qkn[:, k, :, 0, :], ACT.Copy)
                    nc.scalar.activation(ak[:, two, 0, :, DH:],
                                         qkn[:, k, :, 1, :].rearrange("p t (h d) -> p t h d", d=DH),
                                         ACT.Copy).then_inc(qk_hi, 1)
                    act.wait_ge(turned, i + 1)
                    nc.scalar.activation(kqt[:, k, 0].rearrange("p t a n -> p (t a n)"), bank[k][:],
                                         ACT.Copy).then_inc(kqt_hi, 1)
                for k in range(2):
                    i = t * 2 + k
                    act.wait_ge(masked, i + 1)
                    nc.scalar.activation(ak[:, bass.ds(i * 2, 2), 0, :, 0:C],
                                         at[:, k].rearrange("p (t h) n -> p t h n", t=2), ACT.Copy).then_inc(at_hi, 1)
            for m in range(C // 4):
                if m % 2 == 1:
                    act.wait_ge(nu_turned, m + 1)
                    nc.scalar.activation(nu[:, 4 * m:4 * m + 4, :], bank[m % 8][:].rearrange("p (s m) -> p s m", s=4),
                                         ACT.Copy).then_inc(nu_act, 1)
            for m in range(C // 4):
                act.wait_ge(tt_turned, m + 1)
                nc.scalar.activation(tt[:, :, 0, :].rearrange("p t (h n) -> p t h n", h=H)[:, :, :, 4 * m:4 * m + 4],
                                     bank[m % 8][:].rearrange("p (n t h) -> p t h n", n=4, h=H),
                                     ACT.Copy).then_inc(tt_hi, 1)

        @block.tensor
        def _(pe):
            step = Chain(pe, pe_steps)
            with step.loop(B // 2, 2 * (H - 1)) as t:
                for k in range(2):
                    i = t * 2 + k
                    pe.wait_ge(normed, i + 1)
                    for half in range(2):
                        for a in range(2):
                            n = (half * 2 + a) * P
                            last = nc.tensor.transpose(bank[k][:, n:n + P], qkn[:, k, half, a, :], g.ident[:])
                    last.then_inc(turned, 1)
                for k in range(2):
                    i = t * 2 + k
                    wait_apart(pe, kqt_ready, i + 1, g.passed)
                    for h in range(H):
                        rows = slice(DH * h, DH * h + DH)
                        for half in range(2):
                            for c in range(CT):
                                toks = slice(C * c, C * c + C)
                                n = (half * H + h) * 2 * C
                                last = product3(bank[2 + k][toks, n:n + 2 * C],
                                                [kqt[rows, k, a, half, 1, toks] for a in range(2)],
                                                [kqt[rows, k, a, half, :, toks] for a in range(2)],
                                                True, True, pe=nc.tensor)
                        if h < H - 1:
                            step(last)
                            step.settle_apart(g.passed)
                    last.then_inc(gram_ready, 1)
            pe.wait_ge(masked, B)
            for m in range(C // 4):
                for s in range(4):
                    last = nc.tensor.transpose(bank[m % 8][:, s * P:s * P + P], ng[:, :, 4 * m + s], g.ident[:])
                last.then_inc(nu_turned, 1)
            pe.wait_ge(sub_dve, 2 * (C - 1))
            pe.wait_ge(sub_pool, 2 * (C - 1))
            for m in range(C // 4):
                for s in range(4):
                    last = nc.tensor.transpose(bank[m % 8][:, s * P:s * P + P], t_u[:, 4 * m + s].rearrange("p c j -> p (c j)"), g.ident[:])
                last.then_inc(tt_turned, 1)


def substitute(engine, step, nu, t_u, tmp, s, c0, c1):
    n, rows, cols = c1 - c0, C - 1 - s, s + 1
    part = tmp[:, c0 * 256:c0 * 256 + n * rows * cols].rearrange("p (t c j) -> p t c j", c=n, t=rows)
    factor = nu[:, s, :].rearrange("p (c t) -> p t c", c=CT)[:, s + 1:C, c0:c1]
    if s:
        step.settle()
    step(engine.tensor_tensor(part, factor.unsqueeze(3).to_broadcast([P, rows, n, cols]),
                              t_u[:, s:s + 1, c0:c1, 0:cols].to_broadcast([P, rows, n, cols]), ALU.mult))
    step.settle()
    below = t_u[:, s + 1:C, c0:c1, 0:cols]
    step(engine.tensor_tensor(below, below, part, ALU.add))


def delta_rule(nc, g):
    with ExitStack() as ctx:
        sb = lambda n, s, d: ctx.enter_context(nc.sbuf_tensor(n, s, d))
        tt = sb("tt", [P, TILES, 2, H * C], F16)
        vb = sb("vb", [P, TILES, 2, H, 2 * DH], F16)
        ak = sb("ak", [P, TILES, 2, H, 2 * DH], F16)
        q16 = g.delta[:].bitcast(F16).rearrange("p t (a n) -> p t a n", a=2)
        delta_solve(nc, g, tt, vb, ak, q16)
        delta_apply(nc, g, tt, vb, ak, q16)


def delta_apply(nc, g, tt, vb, ak, q16):
    with ExitStack() as ctx:
        sb = lambda n, s, d: ctx.enter_context(nc.sbuf_tensor(n, s, d))
        sem = lambda n: g.semaphore(nc, n)
        W2 = 2 * DH
        s_tt = sb("s_tt", [P, 2, 2, 2, H, C], F16)
        s_vb = sb("s_vb", [P, 2, 2, 2, H, W2], F16)
        s_ak = sb("s_ak", [P, 2, 2, 2, H, W2], F16)
        wu = sb("wu", [P, 2, 2, H, W2], F16)
        wide_tt = sb("wide_tt", [P, 2, 2, H, CT, C], F16)
        wide_ak = sb("wide_ak", [P, 2, 2, H, 2, CT, C], F16)
        wide_u = sb("wide_u", [P, 2, 2, H, CT, DH], F16)
        spare = wide_ak[:].rearrange("p k a h m c n -> p (k a h m c n)")
        s_bt = spare[:, 0:2048].rearrange("p (q c a n) -> p q c a n", q=2, c=2 * CT, a=2)
        wide_state = wide_tt[:].rearrange("p k a h c n -> p k (a h c n)").rearrange(
            "p k (c a h n) -> p k c a h n", c=CT, a=2, h=H)
        bt = g.qk[:].bitcast(F16).rearrange("p t (c a n) -> p (t c) a n", c=CT, a=2)
        ku = tt[:].bitcast(F32).rearrange("p t a n -> p (t a n)").rearrange("p (t n) -> p t n", n=CT * DH)
        states = vb[:].rearrange("p t a h w -> p (t a h w)")[:, 0:B * NCH * 2 * DH].rearrange(
            "p (m a d) -> p m a d", a=2, d=DH)
        flat = s_vb[:].rearrange("p q k a h w -> p (q k a h w)")
        bt_chunk = bt.rearrange("p (b n) a d -> p b n a d", n=NCH)
        move = ak[:, 0:TILES // 2].rearrange("p t a h w -> p (t a h w)").rearrange(
            "p (r b a h d) -> p r b a h d", r=2, b=B, a=2, h=H)
        state16 = flat[:, B * 2 * DH:2 * B * 2 * DH].rearrange("p (a b d) -> p a b d", a=2, b=B)
        state = s_ak[:].bitcast(F32).rearrange("p q k a h w -> p (q k a h w)")[:, 0:B * DH].rearrange(
            "p (b d) -> p b d", b=B)
        bank = [ctx.enter_context(nc.psum_tensor(f"da{n}", [P, 512], F32)) for n in range(2)]
        part = [ctx.enter_context(nc.psum_tensor(f"da_part{n}", [P, 512], F32)) for n in range(2)]
        moves = [ctx.enter_context(nc.psum_tensor(f"da_moves{n}", [P, 1024], F32)) for n in range(2)]
        both = lambda k: moves[k][:].rearrange("p (m x) -> p m x", x=512)[:, :, 0:CT * C].rearrange(
            "p m (c n) -> p c m n", c=CT)
        bt_of = lambda i, a: bt[:, bass.ds(i * CT, CT), a, :].rearrange("p c (m n) -> p c m n", m=2)
        staged = [sem("da_staged0"), sem("da_staged1")]
        staged_out = [sem("da_staged_out0"), sem("da_staged_out1")]
        wu_ready, wu_hi, wu_lo = sem("da_wu_ready"), sem("da_wu_hi"), sem("da_wu_lo")
        state_spread, move_clear, move_dve, move_act = sem("da_state_spread"), sem("da_move_clear"), sem("da_move_dve"), sem("da_move_act")
        out_ready, cleared = sem("da_out_ready"), sem("da_cleared")
        tt_spread, ak_spread, u_spread = sem("da_tt_spread"), sem("da_ak_spread"), sem("da_u_spread")
        bt_hi, bt_lo, ku_stored, part_stored = sem("da_bt_hi"), sem("da_bt_lo"), sem("da_ku_stored"), sem("da_part_stored")
        dve_steps, state_ready = sem("da_dve_steps"), sem("da_state_ready")
        s_hi, s_lo, moved = sem("da_s_hi"), sem("da_s_lo"), sem("da_moved")
        read_out, out_added, states_stored = sem("da_read_out"), sem("da_out_added"), sem("da_states_stored")
        block = ctx.enter_context(nc.Block())

        @block.sync
        def _(sp):
            with sp.Fori(0, TILES // 4) as t:
                for q in range(2):
                    pair = bass.ds(t * 4 + q * 2, 2)
                    sp.wait_ge(out_ready, t * 4 + q * 2 + 2)
                    sp.dma_start(s_tt[:, q], tt[:, pair].rearrange("p t a (h n) -> p t a h n", h=H)).then_inc(staged[q], 16)
                    sp.dma_start(s_vb[:, q], vb[:, pair]).then_inc(staged[q], 16)
                    sp.dma_start(s_ak[:, q], ak[:, pair]).then_inc(staged[q], 16)
            sp.wait_ge(states_stored, NCH)
            with sp.Fori(0, TILES // 4) as t:
                for q in range(2):
                    chunks = bass.ds((t * 4 + q * 2) * CT, 2 * CT)
                    sp.wait_ge(read_out, t * 4 + q * 2 + 2)
                    sp.dma_start(s_bt[:, q], bt[:, chunks]).then_inc(staged_out[q], 16)

        @block.gpsimd
        def _(pool):
            nc.gpsimd.memset(wide_tt[:], 0.0).then_inc(cleared, 1)
            pool.wait_ge(cleared, 2)
            nc.gpsimd.memset(wide_ak[:], 0.0).then_inc(cleared, 1)
            for q in range(2):
                pool.wait_ge(staged[q], 48 * TILES // 8)
            nc.gpsimd.memset(move, 0.0).then_inc(move_clear, 1)

        @block.tensor
        def _(pe):
            pe.sem_inc(out_ready, 4)
            with pe.Fori(0, TILES // 4) as t:
                for q in range(2):
                    pe.wait_ge(staged[q], t * 48 + 48)
                    for k in range(2):
                        pe.wait_ge(tt_spread, t * 4 + q * 2 + k + 1)
                        for h in range(H):
                            last = product3(bank[k][:, h * W2:h * W2 + W2],
                                            [wide_tt[:, k, a, h].rearrange("p c t -> p (c t)") for a in range(2)],
                                            [s_vb[:, q, k, a, h, :] for a in range(2)], True, True, pe=nc.tensor)
                        last.then_inc(wu_ready, 1)
                    for k in range(2):
                        i = t * 4 + q * 2 + k
                        pe.wait_ge(u_spread, i + 1)
                        pe.wait_ge(ak_spread, i + 1)
                        wide = lambda a, h, kind: wide_ak[:, k, a, h, kind].rearrange("p c n -> p (c n)")
                        turned = moves[k][:, 0:CT * C]
                        nc.tensor.matmul(turned, q16[:, i, 0, :], g.ident16[:], start=True, stop=False,
                                         skip_group_check=True)
                        nc.tensor.matmul(turned, q16[:, i, 1, :], g.ident16[:], start=False, stop=False,
                                         skip_group_check=True)
                        for h in range(H):
                            product3(moves[k][DH * h:DH * h + DH, 0:CT * C], [wu[:, k, a, h, DH:] for a in range(2)],
                                     [wide(a, h, 0) for a in range(2)], False, True, pe=nc.tensor,
                                     skip_group_check=True)
                        for h in range(H):
                            rows = slice(DH * h, DH * h + DH)
                            product3(moves[k][rows, 512:512 + CT * C], [wu[:, k, a, h, DH:] for a in range(2)],
                                     [wide(a, h, 1) for a in range(2)], True, True, pe=nc.tensor)
                            product3(moves[k][rows, 512 + CT * C:512 + 2 * CT * C],
                                     [s_ak[:, q, k, a, h, C:] for a in range(2)],
                                     [wide_u[:, k, a, h].rearrange("p c n -> p (c n)") for a in range(2)],
                                     True, True, pe=nc.tensor)
                        for h in range(H):
                            last = product3(part[k][:, h * DH:h * DH + DH], [wide(a, h, 0) for a in range(2)],
                                            [wu[:, k, a, h, 0:DH] for a in range(2)], True, True, pe=nc.tensor)
                        last.then_inc(out_ready, 1)
            def advance(n, r):
                pe.wait_ge(move_dve, n + 1)
                pe.wait_ge(move_act, n + 1)
                pe.wait_ge(s_lo, n + 1)
                for b in range(B):
                    last = product3(bank[0][:, b * DH:b * DH + DH],
                                    [move[:, r, b, a].rearrange("p h d -> p (h d)") for a in range(2)],
                                    [state16[:, a, b, :] for a in range(2)], True, True, pe=nc.tensor)
                last.then_inc(moved, 1)

            with pe.Fori(0, NCH // 2 - 1) as n:
                advance(n * 2, 0)
                advance(n * 2 + 1, 1)
            advance(NCH - 2, 0)
            pe.sem_inc(read_out, 4)
            with pe.Fori(0, TILES // 4) as t:
                for q in range(2):
                    pe.wait_ge(staged_out[q], t * 16 + 16)
                    for k in range(2):
                        i = t * 4 + q * 2 + k
                        pe.wait_ge(out_added, i + 1)
                        pe.wait_ge(state_spread, i + 1)
                        for c in range(CT):
                            last = product3(part[k][C * c:C * c + C, 0:H * DH],
                                            [s_bt[:, q, k * CT + c, a, 0:C] for a in range(2)],
                                            [wide_state[:, k, c, a].rearrange("p h n -> p (h n)") for a in range(2)],
                                            True, True, pe=nc.tensor)
                        last.then_inc(read_out, 1)

        @block.scalar
        def _(act):
            def spread_tt(i, q, k):
                for c in range(CT):
                    rows = slice(C * c, C * c + C)
                    last = nc.scalar.activation(wide_tt[rows, k, :, :, c, :].rearrange("p a h n -> p (a h) n"),
                                                s_tt[rows, q, k].rearrange("p a h n -> p (a h) n"), ACT.Copy)
                last.then_inc(tt_spread, 1)

            def pair(t, q, ahead):
                for k in range(2):
                    act.wait_ge(wu_ready, t * 4 + q * 2 + k + 1)
                    nc.scalar.activation(wu[:, k, 0].rearrange("p h w -> p (h w)"), bank[k][:, 0:H * W2],
                                         ACT.Copy).then_inc(wu_hi, 1)
                if ahead:
                    act.wait_ge(staged[1 - q], (t + q) * 48 + 48)
                    for k in range(2):
                        spread_tt(t * 4 + q * 2 + 2 + k, 1 - q, k)
                for k in range(2):
                    i = t * 4 + q * 2 + k
                    act.wait_ge(out_ready, i + 5)
                    nc.scalar.activation(bt_of(i, 0), both(k), ACT.Copy).then_inc(bt_hi, 1)
                    nc.scalar.activation(ku[:, i, :], moves[k][:, 512 + CT * C:512 + 2 * CT * C], ACT.Copy
                                         ).then_inc(ku_stored, 1)

            act.wait_ge(cleared, 3)
            act.wait_ge(staged[0], 48)
            for k in range(2):
                spread_tt(k, 0, k)
            with act.Fori(0, TILES // 4 - 1) as t:
                pair(t, 0, True)
                pair(t, 1, True)
            pair(TILES // 4 - 1, 0, True)
            pair(TILES // 4 - 1, 1, False)

            def spread_move(n):
                for h in range(H // 2, H):
                    rows = slice(DH * h, DH * h + DH)
                    last = nc.scalar.activation(move[rows, n % 2, :, :, h, :], bt_chunk[rows, :, n, :, C:], ACT.Copy)
                last.then_inc(move_act, 1)

            act.wait_ge(move_clear, 1)
            act.wait_ge(bt_lo, TILES)
            spread_move(0)
            with act.Fori(0, NCH - 1) as n:
                act.wait_ge(state_ready, n + 1)
                nc.scalar.activation(state16[:, 0], state, ACT.Copy).then_inc(s_hi, 1)
                spread_move(n + 1)
            act.wait_ge(state_ready, NCH)
            nc.scalar.activation(state16[:, 0], state, ACT.Copy).then_inc(s_hi, 1)

        @block.vector
        def _(dve):
            step = Chain(dve, dve_steps)
            nc.vector.memset(wide_u[:], 0.0).then_inc(cleared, 1)

            def spread_ak(q, k):
                for c in range(CT):
                    rows = slice(C * c, C * c + C)
                    last = nc.vector.tensor_copy(wide_ak[rows, k, :, :, :, c, :].rearrange("p a h m n -> p (a h) m n"),
                                                 s_ak[rows, q, k].rearrange("p a h (m n) -> p (a h) m n", m=2))
                last.then_inc(ak_spread, 1)

            def pair(t, q, ahead):
                for k in range(2):
                    i = t * 4 + q * 2 + k
                    dve.wait_ge(wu_hi, i + 1)
                    nc.vector.tensor_tensor(wu[:, k, 1].rearrange("p h w -> p (h w)"), bank[k][:, 0:H * W2],
                                            wu[:, k, 0].rearrange("p h w -> p (h w)"),
                                            ALU.subtract).then_inc(wu_lo, 1)
                    dve.wait_ge(wu_lo, i + 1)
                    for c in range(CT):
                        rows = slice(C * c, C * c + C)
                        last = nc.vector.tensor_copy(wide_u[rows, k, :, :, c, :].rearrange("p a h n -> p (a h) n"),
                                                     wu[rows, k, :, :, 0:DH].rearrange("p a h n -> p (a h) n"))
                    last.then_inc(u_spread, 1)
                spread_ak(q, 1)
                for k in range(2):
                    i = t * 4 + q * 2 + k
                    dve.wait_ge(out_ready, i + 5)
                    nc.vector.tensor_scalar(g.delta[:, i, :], part[k][:, 0:H * DH], 1 / V_SCALE, None,
                                            ALU.mult).then_inc(part_stored, 1)
                    dve.wait_ge(ku_stored, i + 1)
                    nc.vector.tensor_tensor(bt_of(i, 1), both(k), bt_of(i, 0), ALU.subtract).then_inc(bt_lo, 1)
                    if ahead and k == 0:
                        dve.wait_ge(staged[1 - q], (t + q) * 48 + 48)
                        spread_ak(1 - q, 0)

            dve.wait_ge(cleared, 3)
            dve.wait_ge(staged[0], 48)
            spread_ak(0, 0)
            with dve.Fori(0, TILES // 4 - 1) as t:
                pair(t, 0, True)
                pair(t, 1, True)
            pair(TILES // 4 - 1, 0, True)
            pair(TILES // 4 - 1, 1, False)
            step(nc.vector.memset(wide_state, 0.0))
            nc.vector.memset(state, 0.0).then_inc(state_ready, 1)
            dve.wait_ge(ku_stored, TILES)
            dve.wait_ge(bt_lo, TILES)
            ku_chunk = ku.rearrange("p t (c d) -> p (t c) d", d=DH).rearrange("p (b n) d -> p b n d", n=NCH)
            st_chunk = states.rearrange("p (b n) a d -> p b n a d", n=NCH)

            def spread_move(n):
                for h in range(H // 2):
                    rows = slice(DH * h, DH * h + DH)
                    last = nc.vector.tensor_copy(move[rows, n % 2, :, :, h, :], bt_chunk[rows, :, n, :, C:])
                last.then_inc(move_dve, 1)

            dve.wait_ge(move_clear, 1)
            spread_move(0)
            with step.loop(NCH - 1, 1) as n:
                dve.wait_ge(s_hi, n + 1)
                nc.vector.tensor_tensor(state16[:, 1], state, state16[:, 0], ALU.subtract).then_inc(s_lo, 1)
                step(nc.vector.tensor_tensor(state, state, ku_chunk[:, :, n, :], ALU.add))
                dve.wait_ge(s_lo, n + 1)
                nc.vector.tensor_copy(st_chunk[:, :, n], state16.rearrange("p a b d -> p b a d")
                                      ).then_inc(states_stored, 1)
                spread_move(n + 1)
                step.settle()
                dve.wait_ge(moved, n + 1)
                nc.vector.tensor_tensor(state, state, bank[0][:].rearrange("p (b d) -> p b d", d=DH),
                                        ALU.add).then_inc(state_ready, 1)
            dve.wait_ge(s_hi, NCH)
            nc.vector.tensor_tensor(state16[:, 1], state, state16[:, 0], ALU.subtract).then_inc(s_lo, 1)
            dve.wait_ge(s_lo, NCH)
            nc.vector.tensor_copy(st_chunk[:, :, NCH - 1], state16.rearrange("p a b d -> p b a d")
                                  ).then_inc(states_stored, 1)
            dve.sem_inc(out_added, 2)
            dve.wait_ge(states_stored, NCH)

            def spread_state(i, k):
                dve.wait_ge(read_out, i + 3)
                for h in range(H):
                    rows = slice(DH * h, DH * h + DH)
                    last = nc.vector.tensor_copy(wide_state[rows, k, :, :, h, :], states[rows, bass.ds(i * CT, CT)])
                last.then_inc(state_spread, 1)

            def add(i, k):
                dve.wait_ge(read_out, i + 5)
                nc.vector.scalar_tensor_tensor(out=g.delta[:, i, :], in0=part[k][:, 0:H * DH],
                                               scalar=1 / V_SCALE, in1=g.delta[:, i, :], op0=ALU.mult,
                                               op1=ALU.add).then_inc(out_added, 1)

            spread_state(0, 0)
            with dve.Fori(0, TILES // 2 - 1) as t:
                for k in range(2):
                    spread_state(t * 2 + k + 1, 1 - k)
                    add(t * 2 + k, k)
            spread_state(TILES - 1, 1)
            add(TILES - 2, 0)
            add(TILES - 1, 1)


def lay_out_fir(weight):
    import numpy as np
    w = np.asarray(weight).reshape(D, -1)
    taps = w.shape[1]
    rows = np.zeros((2 * P + taps + taps % 2, D), w.dtype)
    rows[P - 1:P - 1 + taps] = w[:, ::-1].T
    return np.ascontiguousarray(rows.reshape(-1, D // FG, FG).transpose(1, 0, 2))


def fir(nc, g, w):
    with ExitStack() as ctx:
        sb = lambda n, s, d: ctx.enter_context(nc.sbuf_tensor(n, s, d))
        sem = lambda n: g.semaphore(nc, n)
        kinds = []
        for name, taps in (("short", FS), ("long", FL)):
            rows = w[f"fir_{name}"].shape[1]
            width = P + taps - 1 + (taps - 1) % 2
            kinds.append((name, taps, rows, width))
        n_src = [D * rows // P for _, _, rows, _ in kinds]
        raw = [sb(f"raw_{kind[0]}", [P, n], F32) for kind, n in zip(kinds, n_src)]
        half = [sb(f"half_{kind[0]}", [P, 2, n], F16) for kind, n in zip(kinds, n_src)]
        store = [nc.dram_tensor(f"fir_halves_{kind[0]}", (2, D // FG, kind[2], FG), F16, kind="Internal") for kind in kinds]
        toep = [sb(f"toep_{kind[0]}", [P, 2, 2, kind[3], FG], F16) for kind in kinds]
        v16 = sb("v16", [P, 2, TILES, D], F16)
        flip = sb("flip", [P, P], F32)
        bank = [[ctx.enter_context(nc.psum_tensor(f"fir{f}{k}", [P, FG * TILES], F32)) for k in range(2)] for f in range(2)]
        flat_banks = bank[0] + bank[1]
        PART = 4
        PARTS = TILES // PART
        v_turned, flip_steps = sem("fir_v_turned"), sem("fir_flip_steps")
        loaded, high, low, stored = sem("fir_loaded"), sem("fir_high"), sem("fir_low"), sem("fir_stored")
        expanded = [[sem(f"fir_expanded{f}{k}") for k in range(2)] for f in range(2)]
        v_high, v_low, product_ready = sem("fir_v_high"), sem("fir_v_low"), sem("fir_product_ready")
        short_stored, long_stored = sem("fir_short_stored"), sem("fir_long_stored")
        block = ctx.enter_context(nc.Block())
        NG = D // FG

        @block.sync
        def _(sp):
            for f, kind in enumerate(kinds):
                src = w[f"fir_{kind[0]}"].rearrange("g u c -> (g u c)").rearrange("(p n) -> p n", p=P)
                sp.dma_start(raw[f][:], src).then_inc(loaded, 16)
            sp.wait_ge(low, 2)
            for f, kind in enumerate(kinds):
                for a in range(2):
                    dst = store[f].ap()[a].rearrange("g u c -> (g u c)").rearrange("(p n) -> p n", p=P)
                    sp.dma_start(dst, half[f][:, a, :]).then_inc(stored, 16)
            sp.wait_ge(stored, 64)
            for n in range(NG):
                if n >= 2:
                    sp.wait_ge(product_ready, n - 1)
                for f, (name, taps, rows, width) in enumerate(kinds):
                    for a in range(2):
                        first = (a * NG + n) * rows * FG
                        src = bass.AP(store[f], first, [[FG, P], [1, width * FG]])
                        sp.dma_start(toep[f][:, n % 2, a].rearrange("p t c -> p (t c)"), src
                                     ).then_inc(expanded[f][n % 2], 16)

        @block.gpsimd
        def _(pool):
            nc.gpsimd.memset(flip[:], 0.0).then_inc(flip_steps, 1)
            pool.wait_ge(flip_steps, 1)
            nc.gpsimd.affine_select(out=flip[:], in_=flip[:], compare_op=ALU.not_equal, fill=1.0, base=1 - P,
                                    pattern=[[1, P]], channel_multiplier=1).then_inc(flip_steps, 1)

        @block.vector
        def _(dve):
            for f in range(2):
                dve.wait_ge(high, f + 1)
                nc.vector.scalar_tensor_tensor(out=half[f][:, 1, :], in0=raw[f][:], scalar=W_SCALE,
                                               in1=half[f][:, 0, :], op0=ALU.mult,
                                               op1=ALU.subtract).then_inc(low, 1)
            for n in range(PARTS):
                at = slice(n * PART, (n + 1) * PART)
                dve.wait_ge(v_high, n + 1)
                nc.vector.scalar_tensor_tensor(out=v16[:, 1, at].rearrange("p t d -> p (t d)"), in0=flat_banks[n % 4][:],
                                               scalar=V_SCALE, in1=v16[:, 0, at].rearrange("p t d -> p (t d)"),
                                               op0=ALU.mult, op1=ALU.subtract).then_inc(v_low, 1)
            dve.sem_inc(short_stored, 2)
            with dve.Fori(0, NG // 2) as t:
                for k in range(2):
                    i = t * 2 + k
                    dve.wait_ge(product_ready, i + 1)
                    nc.vector.tensor_scalar(g.short[:, :, bass.ds(i * FG, FG)],
                                            bank[0][k][:].rearrange("p (c t) -> p t c", c=FG),
                                            1 / (V_SCALE * W_SCALE), None, ALU.mult).then_inc(short_stored, 1)

        @block.scalar
        def _(act):
            act.wait_ge(loaded, 32)
            for f in range(2):
                nc.scalar.activation(half[f][:, 0, :], raw[f][:], ACT.Copy, scale=W_SCALE).then_inc(high, 1)
            for n in range(PARTS):
                at = slice(n * PART, (n + 1) * PART)
                act.wait_ge(v_turned, n + 1)
                nc.scalar.activation(v16[:, 0, at].rearrange("p t d -> p (t d)"), flat_banks[n % 4][:], ACT.Copy,
                                     scale=V_SCALE).then_inc(v_high, 1)
            act.sem_inc(long_stored, 2)
            with act.Fori(0, NG // 2) as t:
                for k in range(2):
                    i = t * 2 + k
                    act.wait_ge(product_ready, i + 1)
                    nc.scalar.activation(g.long[:, :, bass.ds(i * FG, FG)],
                                         bank[1][k][:].rearrange("p (c t) -> p t c", c=FG),
                                         ACT.Copy, scale=1 / (V_SCALE * W_SCALE)).then_inc(long_stored, 1)

        @block.tensor
        def _(pe):
            pe.wait_ge(flip_steps, 2)
            for n in range(PARTS):
                if n >= 4:
                    pe.wait_ge(v_low, n - 3)
                nc.tensor.matmul(flat_banks[n % 4][:], flip[:],
                                 g.v[:, n * PART:(n + 1) * PART].rearrange("p t d -> p (t d)"), start=True, stop=True
                                 ).then_inc(v_turned, 1)
            pe.wait_ge(v_low, PARTS)
            with pe.Fori(0, NG // 2) as t:
                for k in range(2):
                    i = t * 2 + k
                    pe.wait_ge(short_stored, i + 1)
                    pe.wait_ge(long_stored, i + 1)
                    for f, (name, taps, rows, width) in enumerate(kinds):
                        pe.wait_ge(expanded[f][k], t * 32 + 32)
                        for c in range(FG):
                            ch = bass.ds(i * FG + c, 1)
                            own = [v16[:, a, :, ch].rearrange("p t c -> p (t c)") for a in range(2)]
                            before = [v16[:, a, 0:TILES:2, ch].rearrange("p t c -> p (t c)") for a in range(2)]
                            out = bank[f][k][:, c * TILES:(c + 1) * TILES]
                            product3(out, [toep[f][:, k, a, 0:P, c] for a in range(2)], own, True, False,
                                     pe=nc.tensor, skip_group_check=True)
                            n = taps - 1
                            last = product3(out[0:n, 1:TILES:2], [toep[f][:, k, a, P:P + n, c] for a in range(2)],
                                            before, False, True, pe=nc.tensor, skip_group_check=True)
                    last.then_inc(product_ready, 1)


def gate_and_add(nc, g, w):
    U = TILES * H
    paths = (g.short, g.long, g.delta, g.v)
    with ExitStack() as ctx:
        sb = lambda n, s, d: ctx.enter_context(nc.sbuf_tensor(n, s, d))
        sem = lambda n: g.semaphore(nc, n)
        m1 = sb("m1", [P, D + 16], F32)
        m1_pad = sb("m1_pad", [P, H, 2, H, 16], F32)
        m2 = sb("m2", [4, P], F32)
        ow = sb("ow", [P, D], F32)
        nw = sb("nw", [P, 1], F32)
        b1 = sb("b1", [P, 1], F32)
        b2 = sb("b2", [P, 4], F32)
        temp = sb("temp", [P, 4], F32)
        keep = sb("keep", [P, H], F32)
        hs_w = sb("hs_w", [P, 2, P], F16)
        st_w = sb("st_w", [P, 2, H, P], F16)
        m2_w = sb("m2_w", [P, 2, 4], F16)
        o_w = sb("o_w", [P, 2, D], F16)
        o_wf = sb("o_wf", [P, D], F32)
        sq = sb("sq", [P, 2, U // 4, DH], F32)
        raw = sb("st_raw", [P, 3, 4, U], F32)
        stf = sb("stf", [P, TILES, H, 16], F32)
        st16 = sb("st16", [P, TILES, 2, H * 16], F16)
        stt = sb("stt", [P, 2, 2 * P], F16)
        h1 = sb("h1", [P, 2, H, 2 * P], F32)
        h16 = sb("h16", [P, 2, 2, H, 2 * P], F16)
        pr = sb("pr", [P, U, 4], F32)
        ex = sb("ex", [P, U, 4], F32)
        one = sb("one", [P, 2, U], F32)
        on = sb("on", [P, 2, 2, D], F32)
        ot = sb("ot", [P, 2, 2, 2 * P], F16)
        bank = [ctx.enter_context(nc.psum_tensor(f"gt{n}", [P, 512], F32)) for n in range(8)]
        loaded, padded, dve_steps, act_steps, pool_steps = sem("gt_loaded"), sem("gt_padded"), sem("gt_dve_steps"), sem("gt_act_steps"), sem("gt_pool_steps")
        w_turned, w_high, w_low, sq_ready, sq_read = sem("gt_w_turned"), sem("gt_w_high"), sem("gt_w_low"), sem("gt_sq_ready"), sem("gt_sq_read")
        raw_ready, root_ready, st_ready, st16_hi = sem("gt_raw_ready"), sem("gt_root_ready"), sem("gt_st_ready"), sem("gt_st16_hi")
        st16_ready, st_turned, stt_ready, h_ready = sem("gt_st16_ready"), sem("gt_st_turned"), sem("gt_stt_ready"), sem("gt_h_ready")
        gelu_done, h_hi, h_lo, logits_ready = sem("gt_gelu_done"), sem("gt_h_hi"), sem("gt_h_lo"), sem("gt_logits_ready")
        logits_stored, e_in, e_out, p_ready = sem("gt_logits_stored"), sem("gt_e_in"), sem("gt_e_out"), sem("gt_p_ready")
        mixed_dve, mixed_pool, squared, rms_in, rms_out = sem("gt_mixed_dve"), sem("gt_mixed_pool"), sem("gt_squared"), sem("gt_rms_in"), sem("gt_rms_out")
        on_ready, on_turned, ot_hi, ot_lo, out_ready = sem("gt_on_ready"), sem("gt_on_turned"), sem("gt_ot_hi"), sem("gt_ot_lo"), sem("gt_out_ready")
        keep_ready, misc_ready, sq2_ready, sq2_read = sem("gt_keep_ready"), sem("gt_misc_ready"), sem("gt_sq2_ready"), sem("gt_sq2_read")
        added, w_scaled = sem("gt_added"), sem("gt_w_scaled")
        block = ctx.enter_context(nc.Block())
        units = lambda x: x[:].rearrange("p t (h d) -> p (t h) d", d=DH)
        Q = U // 4
        CUT = 88

        turned_weights = (((hs_w[:, 0], hs_w[:, 1]), bank[0][:, 0:P]),
                          ([st_w[:, a].rearrange("p h n -> p (h n)") for a in range(2)], bank[1][:]),
                          ((m2_w[:, 0], m2_w[:, 1]), bank[2][:, 0:4]))

        @block.sync
        def _(sp):
            sp.dma_start(m1[:], w["L0_attn_mlp1_w"]).then_inc(loaded, 16)
            sp.dma_start(m2[:], w["L0_attn_mlp2_w"]).then_inc(loaded, 16)
            sp.dma_start(ow[:], w["L0_attn_o_w"]).then_inc(loaded, 16)
            for h in range(H):
                sp.dma_start(nw[DH * h:DH * h + DH, :], w["L0_attn_norm_w"].unsqueeze(1)).then_inc(loaded, 16)
            sp.dma_start(b1[:], w["L0_attn_mlp1_b"].unsqueeze(1)).then_inc(loaded, 16)
            sp.dma_start(b2[:], w["L0_attn_mlp2_b"].partition_broadcast(P)).then_inc(loaded, 16)
            sp.dma_start(temp[:, 0:1], w["L0_attn_logit_temp"].partition_broadcast(P)).then_inc(loaded, 16)
            sp.dma_start(keep[:], w["L0_attn_conv_res_logit"].partition_broadcast(P)).then_inc(loaded, 16)

        @block.gpsimd
        def _(pool):
            step = Chain(pool, pool_steps)
            step(nc.gpsimd.memset(m1_pad[:], 0.0))
            pool.wait_ge(loaded, 16 * 11)
            step.settle()
            for h in range(H):
                for a in range(2):
                    if h or a:
                        pool.wait_ge(padded, 2 * h + a)
                    nc.gpsimd.tensor_scalar(m1_pad[:, h, a, h, :], m1[:, D:], W_SCALE / ST_SCALE, None,
                                            ALU.mult).then_inc(padded, 1)
            pool.sem_inc(h_lo, 2)
            with pool.Fori(0, B // 2) as t:
                for k in range(2):
                    pool.wait_ge(h_hi, t * 2 + k + 1)
                    nc.gpsimd.tensor_tensor(h16[:, k, 1].rearrange("p h n -> p (h n)"),
                                            h1[:, k].rearrange("p h n -> p (h n)"),
                                            h16[:, k, 0].rearrange("p h n -> p (h n)"), ALU.subtract).then_inc(h_lo, 1)
            pool.wait_ge(p_ready, 1)
            mix(nc.gpsimd, step, [units(x)[:, CUT:] for x in paths], pr[:, CUT:], U - CUT)
            step.settle()
            nc.gpsimd.memset(h1[:, 0, 0, 0:1], 0.0).then_inc(mixed_pool, 1)

        @block.scalar
        def _(act):
            step = Chain(act, act_steps)
            act.wait_ge(loaded, 16 * 11)
            step(nc.scalar.activation(temp[:, 1:2], temp[:, 0:1], ACT.Abs))
            step.settle()
            step(nc.scalar.activation(temp[:, 1:2], temp[:, 1:2], ACT.Exp, scale=-1.0))
            step.settle()
            nc.scalar.activation(temp[:, 1:2], temp[:, 1:2], ACT.Ln, bias=1.0).then_inc(misc_ready, 1)
            nc.scalar.activation(keep[:], keep[:], ACT.Sigmoid).then_inc(keep_ready, 1)
            for n, (dst, src) in enumerate(turned_weights):
                act.wait_ge(w_turned, n + 1)
                nc.scalar.activation(dst[0], src, ACT.Copy).then_inc(w_high, 1)
            for n, x in enumerate(paths):
                for m in range(4):
                    i = 4 * n + m
                    if i >= 2:
                        act.wait_ge(sq_read, i - 1)
                    nc.scalar.activation(sq[:, i % 2], units(x)[:, Q * m:Q * m + Q], ACT.Square).then_inc(sq_ready, 1)
            act.wait_ge(raw_ready, 1)
            nc.scalar.activation(stf[:].rearrange("p t h (x s) -> p (t h) x s", s=4)[:, :, :, 3],
                                 raw[:, 2].rearrange("p x u -> p u x"), ACT.Sqrt,
                                 scale=ST_SCALE * ST_SCALE).then_inc(root_ready, 1)
            act.wait_ge(st_ready, 1)
            nc.scalar.activation(st16[:, :, 0, :], stf[:].rearrange("p t h s -> p t (h s)"), ACT.Copy
                                 ).then_inc(st16_hi, 1)
            with act.Fori(0, B // 2) as t:
                for k in range(2):
                    act.wait_ge(h_ready, t * 2 + k + 1)
                    act.wait_ge(h_lo, t * 2 + k + 1)
                    for n in range(2):
                        last = nc.scalar.activation(h1[:, k, 2 * n:2 * n + 2, :].rearrange("p h n -> p (h n)"),
                                                    bank[2 + 2 * k + n][:], ACT.Gelu_apprx_tanh, bias=b1[:],
                                                    scale=1 / W_SCALE)
                    last.then_inc(gelu_done, 1)
            act.wait_ge(e_in, 1)
            nc.scalar.activation(ex[:], ex[:], ACT.Exp).then_inc(e_out, 1)
            act.wait_ge(mixed_dve, 1)
            act.wait_ge(mixed_pool, 1)
            for m in range(4):
                if m >= 2:
                    act.wait_ge(sq2_read, m - 1)
                nc.scalar.activation(sq[:, m % 2], units(g.short)[:, Q * m:Q * m + Q], ACT.Square
                                     ).then_inc(sq2_ready, 1)
            act.wait_ge(rms_in, 1)
            nc.scalar.activation(one[:, 0], one[:, 0], ACT.Sqrt, bias=g.eps5[:], scale=1 / DH).then_inc(rms_out, 1)
            with act.Fori(0, B // 2) as t:
                for k in range(2):
                    act.wait_ge(on_turned, t * 2 + k + 1)
                    nc.scalar.activation(ot[:, k, 0, :], bank[k][:, 0:2 * P], ACT.Copy).then_inc(ot_hi, 1)

        @block.vector
        def _(dve):
            step = Chain(dve, dve_steps)
            dve.wait_ge(loaded, 16 * 11)
            step(nc.vector.tensor_scalar(m1[:, 0:D], m1[:, 0:D], W_SCALE, None, ALU.mult))
            nc.vector.tensor_scalar(m2[:], m2[:], W_SCALE, None, ALU.mult).then_inc(w_scaled, 1)
            dve.wait_ge(misc_ready, 1)
            step(nc.vector.tensor_scalar(temp[:, 2:3], temp[:, 0:1], 0.0, None, ALU.max))
            step.settle()
            step(nc.vector.tensor_tensor(temp[:, 2:3], temp[:, 2:3], temp[:, 1:2], ALU.add))
            step.settle()
            step(nc.vector.reciprocal(temp[:, 3:4], temp[:, 2:3]))
            step.settle()
            for n, (dst, src) in enumerate(turned_weights):
                dve.wait_ge(w_high, n + 1)
                nc.vector.tensor_tensor(dst[1], src, dst[0], ALU.subtract).then_inc(w_low, 1)
            dve.wait_ge(w_turned, 4)
            step(nc.vector.tensor_scalar(o_wf[:], bank[3][:, 0:D], nw[:], W_SCALE, ALU.mult, ALU.mult))
            step.settle()
            step(nc.vector.tensor_copy(o_w[:, 0], o_wf[:]))
            step.settle()
            nc.vector.tensor_tensor(o_w[:, 1], o_wf[:], o_w[:, 0], ALU.subtract).then_inc(w_low, 1)
            for n, x in enumerate(paths):
                step(nc.vector.tensor_reduce(raw[:, 0, n], units(x), AX.X, ALU.add))
                step(nc.vector.tensor_reduce(raw[:, 1, n], units(x), AX.X, ALU.add, apply_absolute_value=True))
                for m in range(4):
                    i = 4 * n + m
                    dve.wait_ge(sq_ready, i + 1)
                    nc.vector.tensor_reduce(raw[:, 2, n, Q * m:Q * m + Q], sq[:, i % 2], AX.X, ALU.add
                                            ).then_inc(sq_read, 1)
            dve.wait_ge(sq_read, 16)
            stat = lambda s: stf[:].rearrange("p t h (x s) -> p (t h) x s", s=4)[:, :, :, s]
            by_path = lambda n: raw[:, n].rearrange("p x u -> p u x")
            step(nc.vector.tensor_scalar(stat(0), by_path(0), ST_SCALE / DH, None, ALU.mult))
            nc.vector.tensor_scalar(stat(2), by_path(1), ST_SCALE / DH, None, ALU.mult).then_inc(raw_ready, 1)
            dve.wait_ge(root_ready, 1)
            step(nc.vector.scalar_tensor_tensor(out=raw[:, 1].rearrange("p x u -> p (x u)"),
                                                in0=raw[:, 0].rearrange("p x u -> p (x u)"),
                                                scalar=ST_SCALE / DH / DH,
                                                in1=raw[:, 0].rearrange("p x u -> p (x u)"), op0=ALU.mult, op1=ALU.mult))
            step.settle()
            nc.vector.scalar_tensor_tensor(out=stat(1), in0=by_path(2), scalar=ST_SCALE / DH, in1=by_path(1),
                                           op0=ALU.mult, op1=ALU.subtract).then_inc(st_ready, 1)
            dve.wait_ge(st16_hi, 1)
            nc.vector.tensor_tensor(st16[:, :, 1, :], stf[:].rearrange("p t h s -> p t (h s)"), st16[:, :, 0, :],
                                    ALU.subtract).then_inc(st16_ready, 1)

            def keep_stats(i, k):
                dve.wait_ge(st_turned, i + 1)
                nc.vector.tensor_copy(stt[:, k], bank[k][:, 0:2 * P]).then_inc(stt_ready, 1)

            def hidden_high(i, k):
                dve.wait_ge(gelu_done, i + 1)
                nc.vector.tensor_copy(h16[:, k, 0].rearrange("p h n -> p (h n)"),
                                      h1[:, k].rearrange("p h n -> p (h n)")).then_inc(h_hi, 1)

            def store_logits(i, k):
                dve.wait_ge(logits_ready, i + 1)
                nc.vector.tensor_scalar(ex[:, bass.ds(i * 2 * H, 2 * H), :].rearrange("p u n -> p (u n)"),
                                        bank[6 + k][:, 0:2 * H * 4], 1 / W_SCALE, None,
                                        ALU.mult).then_inc(logits_stored, 1)

            keep_stats(0, 0)
            keep_stats(1, 1)
            with dve.Fori(0, B // 2 - 1) as t:
                for k in range(2):
                    keep_stats(t * 2 + 2 + k, k)
                for k in range(2):
                    hidden_high(t * 2 + k, k)
                for k in range(2):
                    store_logits(t * 2 + k, k)
            for k in range(2):
                hidden_high(B - 2 + k, k)
            for k in range(2):
                store_logits(B - 2 + k, k)
            dve.wait_ge(logits_stored, B)
            step(nc.vector.tensor_tensor(ex[:], ex[:], b2[:].unsqueeze(1).to_broadcast([P, U, 4]), ALU.add))
            step.settle()
            step(nc.vector.tensor_reduce(one[:, 0], ex[:], AX.X, ALU.max))
            step.settle()
            step(nc.vector.tensor_tensor(ex[:], ex[:], one[:, 0].unsqueeze(2).to_broadcast([P, U, 4]), ALU.subtract))
            step.settle()
            nc.vector.tensor_scalar(ex[:], ex[:], temp[:, 3:4], None, ALU.mult).then_inc(e_in, 1)
            dve.wait_ge(e_out, 1)
            for n in range(2):
                step(nc.vector.tensor_reduce(one[:, n], ex[:], AX.X, ALU.add))
                step.settle()
                step(nc.vector.reciprocal(one[:, n], one[:, n]))
                step.settle()
                step(nc.vector.tensor_tensor(ex[:], ex[:], one[:, n].unsqueeze(2).to_broadcast([P, U, 4]), ALU.mult))
                step.settle()
                if n == 0:
                    step(nc.vector.tensor_scalar(ex[:], ex[:], 0.02, None, ALU.max))
                    step.settle()
            dve.wait_ge(keep_ready, 1)
            step(nc.vector.tensor_tensor(pr[:, :, 0].rearrange("p (t h) -> p t h", h=H),
                                         ex[:, :, 0].rearrange("p (t h) -> p t h", h=H),
                                         keep[:].unsqueeze(1).to_broadcast([P, TILES, H]), ALU.add))
            nc.vector.tensor_copy(pr[:, :, 1:4], ex[:, :, 1:4]).then_inc(p_ready, 1)
            dve.wait_ge(p_ready, 1)
            mix(nc.vector, step, [units(x)[:, 0:CUT] for x in paths], pr[:, 0:CUT], CUT)
            step.settle()
            nc.vector.memset(h1[:, 1, 0, 0:1], 0.0).then_inc(mixed_dve, 1)
            for m in range(4):
                dve.wait_ge(sq2_ready, m + 1)
                nc.vector.tensor_reduce(one[:, 0, Q * m:Q * m + Q], sq[:, m % 2], AX.X, ALU.add).then_inc(sq2_read, 1)
            dve.wait_ge(sq2_read, 4)
            dve.sem_inc(rms_in, 1)
            dve.wait_ge(rms_out, 1)
            step(nc.vector.reciprocal(one[:, 1], one[:, 0]))
            step.settle()

            def norm(i, k):
                nc.vector.tensor_tensor(
                    on[:, k].rearrange("p t (h d) -> p (t h) d", d=DH),
                    units(g.short)[:, bass.ds(i * 2 * H, 2 * H), :],
                    one[:, 1, bass.ds(i * 2 * H, 2 * H)].unsqueeze(2).to_broadcast([P, 2 * H, DH]),
                    ALU.mult).then_inc(on_ready, 1)

            def turned_low(i, k):
                dve.wait_ge(ot_hi, i + 1)
                nc.vector.tensor_tensor(ot[:, k, 1, :], bank[k][:, 0:2 * P], ot[:, k, 0, :], ALU.subtract
                                        ).then_inc(ot_lo, 1)

            def add(i, k):
                dve.wait_ge(out_ready, i + 1)
                xs = g.x[:, bass.ds(i * 2, 2), :].rearrange("p t d -> p (t d)")
                nc.vector.scalar_tensor_tensor(out=xs, in0=bank[2 + k][:, 0:2 * D], scalar=1 / W_SCALE, in1=xs,
                                               op0=ALU.mult, op1=ALU.add).then_inc(added, 1)

            norm(0, 0)
            norm(1, 1)
            with dve.Fori(0, B // 2 - 1) as t:
                for k in range(2):
                    dve.wait_ge(on_turned, t * 2 + k + 1)
                    norm(t * 2 + 2 + k, k)
                for k in range(2):
                    turned_low(t * 2 + k, k)
                for k in range(2):
                    add(t * 2 + k, k)
            for k in range(2):
                turned_low(B - 2 + k, k)
            for k in range(2):
                add(B - 2 + k, k)
            dve.wait_ge(added, B)

        @block.tensor
        def _(pe):
            pe.wait_ge(padded, 2 * H)
            pe.wait_ge(w_scaled, 1)
            nc.tensor.transpose(bank[0][:, 0:P], m1[:, 0:D], g.ident[:]).then_inc(w_turned, 1)
            for h in range(H):
                last = nc.tensor.transpose(bank[1][:, h * P:h * P + P],
                                           m1_pad[:, h].rearrange("p a h s -> p (a h s)"), g.ident[:])
            last.then_inc(w_turned, 1)
            nc.tensor.transpose(bank[2][:, 0:4], m2[:], g.ident[0:4, 0:4]).then_inc(w_turned, 1)
            nc.tensor.transpose(bank[3][:, 0:D], ow[:], g.ident[:]).then_inc(w_turned, 1)
            pe.wait_ge(w_low, 4)
            pe.wait_ge(st16_ready, 1)

            def turn_stats(i, k):
                for half in range(2):
                    last = nc.tensor.matmul(bank[k][:, half * P:half * P + P],
                                            st16[:, i * 2 + half].rearrange("p a n -> p (a n)"), g.ident16[:],
                                            start=True, stop=True)
                last.then_inc(st_turned, 1)

            def hidden(i, k):
                pe.wait_ge(stt_ready, i + 1)
                x_t = [x[:, i, PAD:PAD + L] for x in (g.xt_hi, g.xt_lo)]
                for h in range(H):
                    out = bank[2 + 2 * k + h // 2][:, h % 2 * L:h % 2 * L + L]
                    product3(out, (hs_w[:, 0], hs_w[:, 1]), x_t, True, False, pe=nc.tensor)
                    nc.tensor.matmul(out, st_w[:, 0, h], stt[:, k], start=False, stop=False)
                    last = nc.tensor.matmul(out, st_w[:, 1, h], stt[:, k], start=False, stop=True)
                last.then_inc(h_ready, 1)

            def logits(i, k):
                pe.wait_ge(h_lo, i + 3)
                for half in range(2):
                    for h in range(H):
                        n = (half * H + h) * 4
                        last = product3(bank[6 + k][:, n:n + 4],
                                        [h16[:, k, a, h, half * P:half * P + P] for a in range(2)],
                                        (m2_w[:, 0], m2_w[:, 1]), True, True, pe=nc.tensor)
                last.then_inc(logits_ready, 1)

            for k in range(2):
                turn_stats(k, k)
            for k in range(2):
                hidden(k, k)
            with pe.Fori(0, B // 2 - 1) as t:
                for k in range(2):
                    turn_stats(t * 2 + 2 + k, k)
                for k in range(2):
                    pe.wait_ge(gelu_done, t * 2 + k + 1)
                    hidden(t * 2 + 2 + k, k)
                for k in range(2):
                    logits(t * 2 + k, k)
            for k in range(2):
                logits(B - 2 + k, k)

            def turn(i, k):
                pe.wait_ge(on_ready, i + 1)
                for half in range(2):
                    last = nc.tensor.transpose(bank[k][:, half * P:half * P + P], on[:, k, half], g.ident[:])
                last.then_inc(on_turned, 1)

            def project_out(i, k):
                pe.wait_ge(ot_lo, i + 1)
                for half in range(2):
                    last = product3(bank[2 + k][:, half * D:half * D + D],
                                    [ot[:, k, a, half * P:half * P + P] for a in range(2)],
                                    (o_w[:, 0], o_w[:, 1]), True, True, pe=nc.tensor)
                last.then_inc(out_ready, 1)

            turn(0, 0)
            turn(1, 1)
            with pe.Fori(0, B // 2 - 1) as t:
                for k in range(2):
                    project_out(t * 2 + k, k)
                    turn(t * 2 + 2 + k, k)
            for k in range(2):
                project_out(B - 2 + k, k)


def mix(engine, step, paths, weights, n):
    for j in range(4):
        step(engine.tensor_tensor(paths[j], paths[j], weights[:, :, j:j + 1].to_broadcast([P, n, DH]), ALU.mult))
    step.settle()
    step(engine.tensor_tensor(paths[0], paths[0], paths[1], ALU.add))
    step(engine.tensor_tensor(paths[2], paths[2], paths[3], ALU.add))
    step.settle()
    step(engine.tensor_tensor(paths[0], paths[0], paths[2], ALU.add))


def cross_attention(nc, g, w):
    XW = XH * XD
    PAIRS = XH // 2
    WS = 64.0
    with ExitStack() as ctx:
        sb = lambda n, s, d: ctx.enter_context(nc.sbuf_tensor(n, s, d))
        sem = lambda n: g.semaphore(nc, n)
        wq = sb("xwq", [P, XW], F32)
        wk = sb("xwk", [DC, XW], F32)
        wv = sb("xwv", [DC, XW], F32)
        wo = sb("xwo", [P, PAIRS, D], F32)
        bo = sb("xbo", [P, D], F32)
        cx = sb("xctx", [P, B // 2, DC], F32)
        wqt = sb("xwqt", [P, 2, PAIRS, D], F16)
        wkt = sb("xwkt", [P, 2, PAIRS, DC], F16)
        wvt = sb("xwvt", [P, 2, PAIRS, DC], F16)
        wo16 = sb("xwo16", [P, 2, PAIRS, D], F16)
        g16 = sb("xg16", [DC, 2, 2, PAIRS, D], F16)
        r16 = sb("xr16", [DC, 2, 2, PAIRS, D], F16)
        ct = sb("xct", [DC, 2, B + 2, SKV], F16)
        ct_now = sb("xct_now", [DC, 2, SKV], F16)
        a16 = sb("xa16", [P, 2, 2, XW], F16)
        vw16 = sb("xvw16", [P, 2, 2, PAIRS * D], F16)
        es = sb("xes", [P, 2, XW], F32)
        mx = sb("xmx", [P, 2, XH], F32)
        rs = sb("xrs", [P, 2, XH], F32)
        pt16 = sb("xpt16", [P, 2, XW], F16)
        prep = ctx.enter_context(nc.psum_tensor("xprep", [P, XW], F32))
        turned = ctx.enter_context(nc.psum_tensor("xturned", [P, XW], F32))
        score = [ctx.enter_context(nc.psum_tensor(f"xscore{k}", [P, XW], F32)) for k in range(2)]
        loaded, w_turned, w_high, w_low = sem("xa_loaded"), sem("xa_w_turned"), sem("xa_w_high"), sem("xa_w_low")
        wo_high, joined, joined_high, joined_low = sem("xa_wo_high"), sem("xa_joined"), sem("xa_joined_high"), sem("xa_joined_low")
        bias_added, ctx_copied, dve_steps = sem("xa_bias_added"), sem("xa_ctx_copied"), sem("xa_dve_steps")
        prep_ready, prep_hi, prep_lo = sem("xa_prep_ready"), sem("xa_prep_hi"), sem("xa_prep_lo")
        scores_ready, shifted, e_ready, recip_ready = sem("xa_scores_ready"), sem("xa_shifted"), sem("xa_e_ready"), sem("xa_recip_ready")
        p_ready, pt_ready, pt_hi, pt_lo = sem("xa_p_ready"), sem("xa_pt_ready"), sem("xa_pt_hi"), sem("xa_pt_lo")
        pv_ready, added, pad_clear = sem("xa_pv_ready"), sem("xa_added"), sem("xa_pad_clear")
        block = ctx.enter_context(nc.Block())
        turns = [(wqt, score[0], P, WS, D), (wkt, score[1], P, WS, DC), (wvt, turned, P, WS, DC), (ct, prep, DC, 1.0, P)]
        joins = [(g16, (score[0], score[1])), (r16, (turned, prep))]

        def turned_view(n):
            dst, src, rows, scale, width = turns[n]
            if n == 3:
                return ([dst[:, a, 0:B].rearrange("p b k -> p (b k)") for a in range(2)], src[0:DC, 0:B * SKV], scale)
            return ([dst[:, a] for a in range(2)], src[:].rearrange("p (j n) -> p j n", n=P)[:, :, 0:width], scale)

        def destination(j):
            return a16[:, (j + 3) // 2 % 2] if j % 2 else vw16[:, (j // 2 + 1) % 2]

        @block.sync
        def _(sp):
            sp.dma_start(wq[:], w["L0_xattn_w_q"]).then_inc(loaded, 16)
            sp.dma_start(wk[:], w["L0_xattn_w_k"]).then_inc(loaded, 16)
            sp.dma_start(wv[:], w["L0_xattn_w_v"]).then_inc(loaded, 16)
            sp.dma_start(cx[:], w["ctx_768"].rearrange("(m c) k d -> (c k) m d", c=2)).then_inc(loaded, 16)
            sp.dma_start(wo[:], w["L0_xattn_w_out"].rearrange("(j p) d -> p j d", p=P)).then_inc(loaded, 16)
            sp.dma_start(bo[:], w["L0_xattn_b_out"].partition_broadcast(P)).then_inc(loaded, 16)

        @block.gpsimd
        def _(pool):
            nc.gpsimd.memset(ct[:, :, B:, :], 0.0).then_inc(pad_clear, 1)
            pool.wait_ge(pad_clear, 1)
            nc.gpsimd.memset(g.xt_hi[:, B, :], 0.0).then_inc(pad_clear, 1)
            pool.wait_ge(pad_clear, 2)
            nc.gpsimd.memset(g.xt_lo[:, B, :], 0.0).then_inc(pad_clear, 1)
            pool.wait_ge(pad_clear, 3)
            pool.wait_ge(loaded, 96)
            for n in range(4):
                at = slice(n * TILES // 4, (n + 1) * TILES // 4)
                if n:
                    pool.wait_ge(bias_added, n)
                nc.gpsimd.tensor_tensor(g.x[:, at], g.x[:, at], bo[:].unsqueeze(1).to_broadcast([P, TILES // 4, D]),
                                        ALU.add).then_inc(bias_added, 1)

            def normalise(count, k):
                pool.wait_ge(recip_ready, count)
                p = es[:, k].rearrange("p (h n) -> p h n", n=SKV)
                nc.gpsimd.tensor_tensor(p, p, rs[:, k].unsqueeze(2).to_broadcast([P, XH, SKV]),
                                        ALU.mult).then_inc(p_ready, 1)

            normalise(1, 0)
            with pool.Fori(0, TILES // 4) as i:
                for j in range(4):
                    normalise(i * 4 + j + 2, (j + 1) % 2)

        @block.scalar
        def _(act):
            act.wait_ge(loaded, 96)
            for n in range(4):
                hi, src, scale = turned_view(n)
                act.wait_ge(w_turned, n + 1)
                nc.scalar.activation(hi[0], src, ACT.Copy, scale=scale).then_inc(w_high, 1)
            nc.scalar.activation(wo16[:, 0], wo[:], ACT.Copy, scale=WS).then_inc(wo_high, 1)
            for n, (dst, src) in enumerate(joins):
                for e in range(2):
                    act.wait_ge(joined, 2 * n + e + 1)
                    nc.scalar.activation(dst[:, 0, e].rearrange("p j d -> p (j d)"), src[e][0:DC, :], ACT.Copy,
                                         scale=1 / WS).then_inc(joined_high, 1)

            def prepared(count, dst):
                act.wait_ge(prep_ready, count)
                nc.scalar.activation(dst, prep[:], ACT.Copy).then_inc(prep_hi, 1)

            def exponent(count, k):
                act.wait_ge(shifted, count)
                nc.scalar.activation(es[:, k], es[:, k], ACT.Exp, scale=XD ** -0.5 / WS).then_inc(e_ready, 1)

            prepared(1, a16[:, 0, 0])
            prepared(2, vw16[:, 0, 0])
            prepared(3, a16[:, 1, 0])
            exponent(1, 0)
            with act.Fori(0, TILES // 4) as i:
                for j in range(4):
                    act.wait_ge(pt_ready, i * 4 + j + 1)
                    nc.scalar.activation(pt16[:, 0], turned[:], ACT.Copy).then_inc(pt_hi, 1)
                    exponent(i * 4 + j + 2, (j + 1) % 2)
                    prepared(i * 4 + j + 4, destination(j)[:, 0])

        @block.vector
        def _(dve):
            step = Chain(dve, dve_steps)
            for n in range(4):
                (hi, lo), src, scale = turned_view(n)
                dve.wait_ge(w_high, n + 1)
                if n < 3:
                    for j in range(PAIRS):
                        last = nc.vector.scalar_tensor_tensor(out=lo[:, j], in0=src[:, j], scalar=scale, in1=hi[:, j],
                                                              op0=ALU.mult, op1=ALU.subtract)
                else:
                    last = nc.vector.tensor_tensor(lo, src, hi, ALU.subtract)
                last.then_inc(w_low, 1)
            dve.wait_ge(wo_high, 1)
            nc.vector.scalar_tensor_tensor(out=wo16[:, 1], in0=wo[:], scalar=WS, in1=wo16[:, 0], op0=ALU.mult,
                                           op1=ALU.subtract).then_inc(w_low, 1)
            for n, (dst, src) in enumerate(joins):
                for e in range(2):
                    dve.wait_ge(joined_high, 2 * n + e + 1)
                    nc.vector.scalar_tensor_tensor(out=dst[:, 1, e].rearrange("p j d -> p (j d)"), in0=src[e][0:DC, :],
                                                   scalar=1 / WS, in1=dst[:, 0, e].rearrange("p j d -> p (j d)"),
                                                   op0=ALU.mult, op1=ALU.subtract).then_inc(joined_low, 1)
            dve.sem_inc(prep_lo, 1)
            dve.sem_inc(pt_lo, 1)
            dve.sem_inc(added, 1)

            def prepared(count, hi, lo):
                dve.wait_ge(prep_hi, count)
                nc.vector.tensor_tensor(lo, prep[:], hi, ALU.subtract).then_inc(prep_lo, 1)

            def shift(count, k):
                s = score[k][:].rearrange("p (h n) -> p h n", n=SKV)
                dve.wait_ge(scores_ready, count)
                step(nc.vector.tensor_reduce(mx[:, k], s, AX.X, ALU.max))
                step.settle()
                nc.vector.tensor_tensor(es[:, k].rearrange("p (h n) -> p h n", n=SKV), s,
                                        mx[:, k].unsqueeze(2).to_broadcast([P, XH, SKV]),
                                        ALU.subtract).then_inc(shifted, 1)

            def total(count, k):
                dve.wait_ge(e_ready, count)
                step(nc.vector.tensor_reduce(mx[:, k], es[:, k].rearrange("p (h n) -> p h n", n=SKV), AX.X, ALU.add))
                step.settle()
                nc.vector.reciprocal(rs[:, k], mx[:, k]).then_inc(recip_ready, 1)

            def copy_ctx(b):
                nc.vector.tensor_copy(ct_now[:], ct[:, :, b, :]).then_inc(ctx_copied, 1)

            dve.wait_ge(w_low, 5)
            copy_ctx(0)
            prepared(1, a16[:, 0, 0], a16[:, 0, 1])
            prepared(2, vw16[:, 0, 0], vw16[:, 0, 1])
            copy_ctx(1)
            prepared(3, a16[:, 1, 0], a16[:, 1, 1])
            shift(1, 0)
            total(1, 0)
            dve.wait_ge(bias_added, 4)
            dve.wait_ge(pad_clear, 3)
            with step.loop(TILES // 4, 8) as i:
                for j in range(4):
                    if j % 2:
                        copy_ctx(i * 2 + (j + 1) // 2 + 1)
                    shift(i * 4 + j + 2, (j + 1) % 2)
                    dve.wait_ge(pt_hi, i * 4 + j + 1)
                    nc.vector.tensor_tensor(pt16[:, 1], turned[:], pt16[:, 0], ALU.subtract).then_inc(pt_lo, 1)
                    total(i * 4 + j + 2, (j + 1) % 2)
                    dst = destination(j)
                    prepared(i * 4 + j + 4, dst[:, 0], dst[:, 1])
                    dve.wait_ge(pv_ready, i * 4 + j + 1)
                    xs = g.x[:, i * 4 + j, :]
                    nc.vector.scalar_tensor_tensor(out=xs, in0=score[(j + 1) % 2][:, 0:D], scalar=1 / WS, in1=xs,
                                                   op0=ALU.mult, op1=ALU.add).then_inc(added, 1)
            dve.wait_ge(added, TILES + 1)

        @block.tensor
        def _(pe):
            pe.wait_ge(loaded, 96)
            for j in range(PAIRS):
                last = nc.tensor.transpose(score[0][:, j * P:j * P + P], wq[:, j * P:j * P + P], g.ident[:])
            last.then_inc(w_turned, 1)
            for src, to in ((wk, score[1]), (wv, turned)):
                for j in range(PAIRS):
                    last = nc.tensor.transpose(to[:, j * P:j * P + DC], src[:, j * P:j * P + P],
                                               g.ident[0:DC, 0:DC])
                last.then_inc(w_turned, 1)
            for m in range(B // 2):
                last = nc.tensor.transpose(prep[0:DC, m * P:m * P + P], cx[:, m], g.ident[:])
            last.then_inc(w_turned, 1)
            pe.wait_ge(w_low, 5)
            for dst, lhs, rhs in ((joins[0][1], wkt, wqt), (joins[1][1], wvt, wo16)):
                for e in range(2):
                    rows = slice(XD * e, XD * e + XD)
                    for j in range(PAIRS):
                        last = product3(dst[e][0:DC, j * D:j * D + D], [lhs[rows, a, j, :] for a in range(2)],
                                        [rhs[rows, a, j, :] for a in range(2)], True, True, pe=nc.tensor)
                    last.then_inc(joined, 1)

            def prepare_a(count, b):
                pe.wait_ge(prep_lo, count)
                for n in range(XH):
                    last = product3(prep[:, n * SKV:n * SKV + SKV], [g16[:, a, n % 2, n // 2, :] for a in range(2)],
                                    [ct[:, a, b, :] for a in range(2)], True, True, pe=nc.tensor)
                last.then_inc(prep_ready, 1)

            def prepare_vw(count, copied):
                pe.wait_ge(prep_lo, count)
                pe.wait_ge(ctx_copied, copied)
                for e in range(2):
                    for n in range(2):
                        cols = slice(n * 512, n * 512 + 512)
                        last = product3(prep[SKV * e:SKV * e + SKV, cols], (ct_now[:, 0], ct_now[:, 1]),
                                        [r16[:, a, e].rearrange("p j d -> p (j d)")[:, cols] for a in range(2)],
                                        True, True, pe=nc.tensor)
                last.then_inc(prep_ready, 1)

            def scores(batch, half, buf):
                for n in range(2):
                    cols = slice(n * 512, n * 512 + 512)
                    last = product3(score[half][:, cols], [x[:, batch, PAD + half * P:PAD + half * P + P]
                                                           for x in (g.xt_hi, g.xt_lo)],
                                    [a16[:, buf, a, cols] for a in range(2)], True, True, pe=nc.tensor)
                last.then_inc(scores_ready, 1)

            pe.wait_ge(joined_low, 4)
            prepare_a(1, 0)
            prepare_vw(2, 1)
            scores(0, 0, 0)
            scores(0, 1, 0)
            prepare_a(3, 1)
            pe.wait_ge(pad_clear, 3)
            with pe.Fori(0, TILES // 4) as i:
                for j in range(4):
                    pe.wait_ge(p_ready, i * 4 + j + 1)
                    pe.wait_ge(pt_lo, i * 4 + j + 1)
                    for n in range(PAIRS):
                        last = nc.tensor.transpose(turned[:, n * P:n * P + P], es[:, j % 2, n * P:n * P + P], g.ident[:])
                    last.then_inc(pt_ready, 1)
                    if j % 2:
                        prepare_a(i * 4 + j + 4, i * 2 + (j + 3) // 2)
                    else:
                        prepare_vw(i * 4 + j + 4, i * 2 + 2 + j // 2)
                    pe.wait_ge(shifted, i * 4 + j + 1)
                    pe.wait_ge(added, i * 4 + j + 1)
                    scores(i * 2 + (j + 2) // 2, j % 2, (j + 2) // 2 % 2)
                    pe.wait_ge(pt_lo, i * 4 + j + 2)
                    pe.wait_ge(shifted, i * 4 + j + 2)
                    for n in range(PAIRS):
                        last = product3(score[(j + 1) % 2][:, 0:D], [pt16[:, a, n * P:n * P + P] for a in range(2)],
                                        [vw16[:, j // 2, a, n * D:n * D + D] for a in range(2)],
                                        n == 0, n == PAIRS - 1, pe=nc.tensor)
                    last.then_inc(pv_ready, 1)


def experts(nc, g, w):
    WS = 64.0
    GROUP = 4
    GROUPS = TILES // GROUP
    N = GROUP * P
    with ExitStack() as ctx:
        sb = lambda n, s, d: ctx.enter_context(nc.sbuf_tensor(n, s, d))
        sem = lambda n: g.semaphore(nc, n)
        gate = sb("fgate", [P, E], F32)
        gate16 = sb("fgate16", [P, 2, E], F16)
        w1 = sb("fw1", [P, E, F], F32)
        w2 = sb("fw2", [P, E, FT, D], F32)
        b1 = sb("fb1", [P, E, FT], F32)
        b1_rows = sb("fb1_rows", [E * FT, P], F32)
        b2 = sb("fb2", [E, D], F32)
        w1h = sb("fw1h", [P, 2, E, F], F16)
        w2h = sb("fw2h", [P, 2, E, FT, D], F16)
        rank = sb("frank", [P, E], F32)
        logits = sb("flogits", [P, TILES, E], F32)
        key = sb("fkey", [P, TILES, E], F32)
        first = sb("ffirst", [P, TILES, E], F32)
        second = sb("fsecond", [P, TILES, E], F32)
        combine = sb("fcombine", [P, TILES, E], F32)
        scaled = sb("fscaled", [P, TILES, E], F32)
        max1 = sb("fmax1", [P, TILES], F32)
        max2 = sb("fmax2", [P, TILES], F32)
        kmax = sb("fkmax", [P, TILES], F32)
        turned = sb("fturned", [E, GROUPS, N], F32)
        h32 = sb("fh32", [P, 2, FT, N], F32)
        h16 = sb("fh16", [P, 2, 2, FT, N], F16)
        ph = [ctx.enter_context(nc.psum_tensor(f"fph{c}", [P, N], F32)) for c in range(FT)]
        py = [ctx.enter_context(nc.psum_tensor(f"fpy{k}", [P, N], F32)) for k in range(2)]
        pl = ctx.enter_context(nc.psum_tensor("fpl", [P, N], F32))
        loaded, split_hi, split_lo, dve_steps = sem("ff_loaded"), sem("ff_split_hi"), sem("ff_split_lo"), sem("ff_dve_steps")
        rank_ready = sem("ff_rank_ready")
        logits_ready, gap_ready, exp_ready = sem("ff_logits_ready"), sem("ff_gap_ready"), sem("ff_exp_ready")
        combined, comb_turned, comb_copied, bias_ready, bias_added = sem("ff_combined"), sem("ff_comb_turned"), sem("ff_comb_copied"), sem("ff_bias_ready"), sem("ff_bias_added")
        hidden_ready, gelu_ready, h_high, h_low = sem("ff_hidden_ready"), sem("ff_gelu_ready"), sem("ff_h_high"), sem("ff_h_low")
        y_ready, added = sem("ff_y_ready"), sem("ff_added")
        stored = sem("ff_stored")
        block = ctx.enter_context(nc.Block())
        TURNS = E * GROUPS
        PAIRS = GROUPS // 2

        @block.sync
        def _(sp):
            sp.dma_start(gate[:], w["L0_ffn_gate_w"]).then_inc(loaded, 16)
            sp.dma_start(b1_rows[:], w["L0_ffn_b1"].rearrange("e (c p) -> (e c) p", p=P)).then_inc(loaded, 16)
            sp.dma_start(b2[:], w["L0_ffn_b2"]).then_inc(loaded, 16)
            for n in range(4):
                at = slice(n * E // 4, (n + 1) * E // 4)
                sp.dma_start(w1[:, at], w["L0_ffn_w1"][at].rearrange("e p f -> p e f")).then_inc(loaded, 16)
                sp.dma_start(w2[:, at], w["L0_ffn_w2"][at].rearrange("e (c p) d -> p e c d", p=P)).then_inc(loaded, 16)
            y_view = g.out.rearrange("b (h p) d -> p (b h) d", p=P)
            for t in range(GROUPS):
                sp.wait_ge(added, TURNS - GROUPS + t + 1 + 2)
                at = slice(t * GROUP, (t + 1) * GROUP)
                sp.dma_start(y_view[:, at, :], g.x[:, at, :]).then_inc(stored, 16)
            sp.wait_ge(stored, 16 * GROUPS)

        @block.gpsimd
        def _(pool):
            for e in range(E):
                nc.gpsimd.memset(rank[:, e:e + 1], float(E - e)).then_inc(rank_ready, 1)

        @block.scalar
        def _(act):
            act.wait_ge(loaded, 16 * 11)
            nc.scalar.activation(gate16[:, 0], gate[:], ACT.Copy, scale=WS).then_inc(split_hi, 1)
            for n in range(4):
                at = slice(n * E // 4, (n + 1) * E // 4)
                nc.scalar.activation(w1h[:, 0, at], w1[:, at], ACT.Copy, scale=WS).then_inc(split_hi, 1)
                nc.scalar.activation(w2h[:, 0, at], w2[:, at], ACT.Copy, scale=WS).then_inc(split_hi, 1)
            act.wait_ge(gap_ready, 1)
            nc.scalar.activation(max2[:], max2[:], ACT.Exp, scale=1 / WS).then_inc(exp_ready, 1)
            for t in range(GROUPS):
                act.wait_ge(comb_turned, t + 1)
                nc.scalar.activation(turned[:, t, :], py[t % 2][0:E, :], ACT.Copy).then_inc(comb_copied, 1)
            act.sem_inc(gelu_ready, FT)
            with act.Fori(0, TURNS // 2) as i:
                for k in range(2):
                    turn = i * 2 + k
                    act.wait_ge(h_low, i * 4 + 2 * k + 2)
                    for c in range(FT):
                        wait_apart(act, hidden_ready, turn * FT + c + 1, g.passed)
                        nc.scalar.activation(h32[:, k, c], ph[c][:], ACT.Gelu, bias=b1[:, i // PAIRS, c:c + 1],
                                             scale=1 / WS).then_inc(gelu_ready, 1)
                        if c == FT // 2 - 1:
                            act.wait_ge(y_ready, turn + 1)
                        if c % 2:
                            at = slice(c - 1, c + 1)
                            act.wait_ge(gelu_ready, turn * FT + FT + c + 1)
                            nc.scalar.activation(h16[:, k, 0, at], h32[:, k, at], ACT.Copy).then_inc(h_high, 1)

        @block.vector
        def _(dve):
            step = Chain(dve, dve_steps)
            dve.wait_ge(split_hi, 1)
            nc.vector.scalar_tensor_tensor(out=gate16[:, 1], in0=gate[:], scalar=WS, in1=gate16[:, 0], op0=ALU.mult,
                                           op1=ALU.subtract).then_inc(split_lo, 1)
            for n in range(4):
                at = slice(n * E // 4, (n + 1) * E // 4)
                flat = lambda a: a.rearrange("p e f -> p (e f)")
                flat2 = lambda a: a.rearrange("p e c d -> p (e c d)")
                dve.wait_ge(split_hi, 2 * n + 3)
                nc.vector.scalar_tensor_tensor(out=flat(w1h[:, 1, at]), in0=flat(w1[:, at]), scalar=WS,
                                               in1=flat(w1h[:, 0, at]), op0=ALU.mult,
                                               op1=ALU.subtract).then_inc(split_lo, 1)
                nc.vector.scalar_tensor_tensor(out=flat2(w2h[:, 1, at]), in0=flat2(w2[:, at]), scalar=WS,
                                               in1=flat2(w2h[:, 0, at]), op0=ALU.mult,
                                               op1=ALU.subtract).then_inc(split_lo, 1)
            wide = lambda a: a[:].unsqueeze(2).to_broadcast([P, TILES, E])

            def pick(one_hot, values, largest):
                step(nc.vector.tensor_reduce(largest[:], values[:], AX.X, ALU.max))
                step.settle()
                step(nc.vector.tensor_tensor(key[:], values[:], wide(largest), ALU.is_equal))
                step.settle()
                step(nc.vector.tensor_tensor(key[:], key[:], rank[:].unsqueeze(1).to_broadcast([P, TILES, E]), ALU.mult))
                step.settle()
                step(nc.vector.tensor_reduce(kmax[:], key[:], AX.X, ALU.max))
                step.settle()
                step(nc.vector.tensor_tensor(one_hot[:], key[:], wide(kmax), ALU.is_equal))
                step.settle()

            dve.wait_ge(logits_ready, 1)
            step(nc.vector.tensor_copy(logits[:].rearrange("p t e -> p (t e)"), pl[:, 0:TILES * E]))
            step(nc.vector.tensor_copy(b1[:].rearrange("p e c -> p (e c)"), pl[:, TILES * E:TILES * E + E * FT]))
            step.settle()
            dve.wait_ge(rank_ready, E)
            pick(first, logits, max1)
            step(nc.vector.scalar_tensor_tensor(out=logits[:].rearrange("p t e -> p (t e)"),
                                                in0=first[:].rearrange("p t e -> p (t e)"), scalar=-1e30,
                                                in1=logits[:].rearrange("p t e -> p (t e)"), op0=ALU.mult, op1=ALU.add))
            step.settle()
            pick(second, logits, max2)
            nc.vector.tensor_tensor(max2[:], max2[:], max1[:], ALU.subtract).then_inc(gap_ready, 1)
            dve.wait_ge(exp_ready, 1)
            step(nc.vector.tensor_scalar(max1[:], max2[:], 1.0, None, ALU.add))
            step.settle()
            step(nc.vector.reciprocal(max1[:], max1[:]))
            step.settle()
            step(nc.vector.tensor_tensor(max2[:], max2[:], max1[:], ALU.mult))
            step(nc.vector.tensor_tensor(first[:], first[:], wide(max1), ALU.mult))
            step.settle()
            step(nc.vector.tensor_tensor(second[:], second[:], wide(max2), ALU.mult))
            step.settle()
            step(nc.vector.tensor_tensor(combine[:], first[:], second[:], ALU.add))
            step.settle()
            nc.vector.tensor_scalar(scaled[:], combine[:], 1 / WS, None, ALU.mult).then_inc(combined, 1)
            for t in range(GROUPS):
                at = slice(t * GROUP, (t + 1) * GROUP)
                dve.wait_ge(bias_ready, t + 1)
                nc.vector.tensor_tensor(g.x[:, at].rearrange("p t d -> p (t d)"),
                                        g.x[:, at].rearrange("p t d -> p (t d)"), ph[t % FT][:],
                                        ALU.add).then_inc(bias_added, 1)
            dve.wait_ge(bias_added, GROUPS)
            dve.sem_inc(added, 2)
            dve.sem_inc(h_low, 4)

            def low(turn, k):
                for n in range(2):
                    at = slice(2 * n, 2 * n + 2)
                    dve.wait_ge(h_high, turn * 2 + n + 1)
                    nc.vector.tensor_tensor(h16[:, k, 1, at], h32[:, k, at], h16[:, k, 0, at],
                                            ALU.subtract).then_inc(h_low, 1)

            def add(i, k):
                dve.wait_ge(y_ready, i * 2 + k + 3)
                for m in range(GROUP):
                    tile = (i % PAIRS) * 2 * GROUP + k * GROUP + m
                    xs = g.x[:, tile, :]
                    last = nc.vector.scalar_tensor_tensor(
                        out=xs, in0=py[k][:, m * D:m * D + D], scalar=scaled[:, tile, bass.ds(i // PAIRS, 1)],
                        in1=xs, op0=ALU.mult, op1=ALU.add)
                last.then_inc(added, 1)

            low(0, 0)
            with dve.Fori(0, TURNS // 2 - 1) as i:
                low(i * 2 + 1, 1)
                add(i, 0)
                low(i * 2 + 2, 0)
                add(i, 1)
            low(TURNS - 1, 1)
            add(TURNS // 2 - 1, 0)
            add(TURNS // 2 - 1, 1)

        @block.tensor
        def _(pe):
            pe.wait_ge(loaded, 16 * 11)
            pe.wait_ge(split_lo, 1)
            nc.tensor.transpose(pl[:, TILES * E:TILES * E + E * FT], b1_rows[:], g.ident[0:E * FT, 0:E * FT])
            for t in range(TILES):
                at = slice(PAD + t % 2 * P, PAD + t % 2 * P + P)
                last = product3(pl[:, t * E:t * E + E], (g.xt_hi[:, t // 2, at], g.xt_lo[:, t // 2, at]),
                                (gate16[:, 0], gate16[:, 1]), True, True, pe=nc.tensor)
            last.then_inc(logits_ready, 1)
            pe.wait_ge(combined, 1)
            for t in range(GROUPS):
                if t >= 2:
                    pe.wait_ge(comb_copied, t - 1)
                for m in range(GROUP):
                    last = nc.tensor.transpose(py[t % 2][0:E, m * P:m * P + P], combine[:, t * GROUP + m, :], g.ident[:])
                last.then_inc(comb_turned, 1)
            for t in range(GROUPS):
                pe.wait_ge(comb_copied, t + 1)
                if t >= FT:
                    pe.wait_ge(bias_added, t - FT + 1)
                for m in range(GROUP):
                    last = nc.tensor.matmul(ph[t % FT][:, m * D:m * D + D], turned[:, t, m * P:m * P + P], b2[:],
                                            start=True, stop=True)
                last.then_inc(bias_ready, 1)
            pe.wait_ge(split_lo, 9)
            pe.sem_inc(y_ready, 2)

            def hidden(i, k):
                turn, e = i * 2 + k, i // PAIRS
                batch = (i % PAIRS) * 4 + k * 2
                for c in range(FT):
                    pe.wait_ge(gelu_ready, turn * FT + c + 1)
                    w_at = lambda a: w1h[:, a, e, c * P:c * P + P]
                    product3(ph[c][:], (w_at(0), w_at(1)),
                             [x[:, bass.ds(batch, 2), PAD:PAD + L] for x in (g.xt_hi, g.xt_lo)],
                             True, True, pe=nc.tensor).then_inc(hidden_ready, 1)

            def outputs(i, k):
                turn, e = i * 2 + k, i // PAIRS
                pe.wait_ge(added, turn + 1)
                pe.wait_ge(h_low, turn * 2 + 6)
                for m in range(GROUP):
                    cols = slice(m * P, m * P + P)
                    for c in range(FT):
                        last = product3(py[k][:, m * D:m * D + D], (h16[:, k, 0, c, cols], h16[:, k, 1, c, cols]),
                                        (w2h[:, 0, e, c, :], w2h[:, 1, e, c, :]), c == 0, c == FT - 1, pe=nc.tensor)
                last.then_inc(y_ready, 1)

            pe.wait_ge(added, 2)
            hidden(0, 0)
            with pe.Fori(0, TURNS // 2 - 1) as i:
                hidden(i, 1)
                outputs(i, 0)
                hidden(i + 1, 0)
                outputs(i, 1)
            hidden(TURNS // 2 - 1, 1)
            outputs(TURNS // 2 - 1, 0)
            outputs(TURNS // 2 - 1, 1)


_INS = ["x", "ctx_768"] + ["L0_attn_" + n for n in (
    "q_w", "k_w", "v_w", "b_w", "q_cw", "k_cw", "v_cw", "mlp1_w", "mlp1_b", "mlp2_w", "mlp2_b", "logit_temp",
    "conv_res_logit", "norm_w", "o_w")] + ["L0_xattn_" + n for n in ("w_q", "w_k", "w_v", "w_out", "b_out")] + [
    "L0_ffn_" + n for n in ("gate_w", "w1", "b1", "w2", "b2")]


def decoder_layer(nc, w, out):
    with ExitStack() as ctx:
        g = Shared(nc, ctx)
        g.out = out
        with ExitStack() as attention:
            g.hold_attention(nc, attention)
            load(nc, g, w)
            norm_and_transpose(nc, g)
            project(nc, g, w)
            delta_rule(nc, g)
            with ExitStack() as branches:
                g.hold_fir(nc, branches)
                fir(nc, g, w)
                gate_and_add(nc, g, w)
        g.clear_semaphores(nc)
        norm_and_transpose(nc, g, "ln2")
        cross_attention(nc, g, w)
        norm_and_transpose(nc, g, "ln3")
        experts(nc, g, w)


def kernel(**inputs):
    import numpy as np
    import concourse.bacc as bacc
    from concourse.bass_utils import run_bass_kernel_spmd

    nc = bacc.Bacc("TRN2", target_bir_lowering=False, num_devices=1)
    laid_out = {n: inputs[n] for n in _INS}
    for n in ("short", "long"):
        laid_out["fir_" + n] = lay_out_fir(inputs[f"L0_attn_fir_{n}_w"])
    arrays, w = {}, {}
    for name, value in laid_out.items():
        a = np.ascontiguousarray(value)
        arrays[f"in_{name}"] = a
        w[name] = nc.dram_tensor(f"in_{name}", a.shape, mybir.dt.from_np(a.dtype), kind="ExternalInput").ap()
    out = nc.dram_tensor("out_x", (B, L, D), F32, kind="ExternalOutput").ap()
    decoder_layer(nc, w, out)
    r = run_bass_kernel_spmd(nc, [arrays], core_ids=[0])
    return r.results[0]["out_x"]
```

```python
from contextlib import ExitStack, contextmanager

import concourse.bass as bass
from concourse import mybir

F32 = mybir.dt.float32
F16 = mybir.dt.float16
I32 = mybir.dt.int32
ALU = mybir.AluOpType
ACT = mybir.ActivationFunctionType
AX = mybir.AxisListType

P = 128
B, L, D = 16, 256, 128
TILES = B * L // P
H, DH = 4, 32
C = 32
CT = P // C
NCH = L // C
TAPS = 4
PAD = TAPS - 1
FS, FL = 5, 64
XH, XD, SKV, DC = 16, 64, 64, 96
E, F = 8, 512
FT = F // P
BLOCKS = (2 * B * L + E * (P - 1)) // P

FG = 16

W_SCALE = 1024.0
V_SCALE = 64.0
ST_SCALE = 64.0


def wait_apart(eng, sem, value, passed):
    eng.wait_ge(sem, value)
    eng.sem_inc(passed, 1)


class Chain:

    def __init__(self, eng, sem):
        self.eng, self.sem, self.base, self.k = eng, sem, 0, 0

    def __call__(self, ins):
        self.k += 1
        return ins.then_inc(self.sem, 1)

    def settle(self):
        self.eng.wait_ge(self.sem, self.base + self.k)

    def settle_apart(self, passed):
        wait_apart(self.eng, self.sem, self.base + self.k, passed)

    @contextmanager
    def loop(self, n, per):
        start = self.base + self.k
        with self.eng.Fori(0, n) as i:
            self.base, self.k = i * per + start, 0
            yield i
            assert self.k == per, f"{self.k} steps a turn"
        self.base, self.k = start + n * per, 0


def product3(out, a, b, start, stop, **kw):
    bass_tensor = kw.pop("pe")
    (ah, al), (bh, bl) = a, b
    bass_tensor.matmul(out, ah, bh, start=start, stop=False, **kw)
    bass_tensor.matmul(out, ah, bl, start=False, stop=False, **kw)
    return bass_tensor.matmul(out, al, bh, start=False, stop=stop, **kw)


class Shared:

    def __init__(self, nc, ctx):
        sb = lambda n, s, d: ctx.enter_context(nc.sbuf_tensor(n, s, d))
        self.x = sb("x_tok", [P, TILES, D], F32)
        self.xt_hi = sb("xt_hi", [P, B + 1, PAD + L + 1], F16)
        self.xt_lo = sb("xt_lo", [P, B + 1, PAD + L + 1], F16)
        self.ident = sb("ident", [P, P], F32)
        self.ident16 = sb("ident16", [P, P], F16)
        self.causal = sb("causal", [P, C], F32)
        self.eps5 = sb("eps5", [P, 1], F32)
        self.eps6 = sb("eps6", [P, 1], F32)
        self.arena = sb("arena", [P, TILES * 2 * D], F32)
        sem = lambda n: ctx.enter_context(nc.semaphore(n))
        self.qkv_fetched, self.gate_fetched = sem("qkv_fetched"), sem("gate_fetched")
        self.cross_fetched, self.expert_fetched = sem("cross_fetched"), sem("expert_fetched")
        self.semaphores = []
        self.passed = ctx.enter_context(nc.semaphore("passed"))

    def semaphore(self, nc, name):
        self.semaphores.append(nc.alloc_semaphore(name))
        return self.semaphores[-1]

    def clear_semaphores(self, nc):
        nc.clear_and_free_semaphores(self.semaphores)
        nc.all_engine_barrier()
        self.semaphores = []

    def hold_attention(self, nc, ctx):
        sb = lambda n, s, d: ctx.enter_context(nc.sbuf_tensor(n, s, d))
        self.qk = self.arena[:].rearrange("p (t n) -> p t n", t=TILES)
        self.v = sb("v", [P, TILES, D], F32)
        self.qk_norm = sb("qk_norm", [P, TILES, 2 * H], F32)
        self.beta = sb("beta", [P, TILES, H], F32)
        self.delta = sb("delta", [P, TILES, D], F32)

    def hold_qkv_weights(self, nc, ctx):
        sb = lambda n, s, d: ctx.enter_context(nc.sbuf_tensor(n, s, d))
        self.w_nat = sb("w_nat", [P, 3, D], F32)
        self.cw = sb("cw", [P, 3, TAPS], F32)
        self.b_w = sb("b_w_nat", [H, D], F32)

    def fetch_qkv_weights(self, sp, w):
        for n, name in enumerate(("q", "k", "v")):
            sp.dma_start(self.w_nat[:, n, :], w[f"L0_attn_{name}_w"]).then_inc(self.qkv_fetched, 16)
            sp.dma_start(self.cw[:, n, :], w[f"L0_attn_{name}_cw"]).then_inc(self.qkv_fetched, 16)
        sp.dma_start(self.b_w[:], w["L0_attn_b_w"]).then_inc(self.qkv_fetched, 16)

    def hold_gate_weights(self, nc, ctx):
        sb = lambda n, s, d: ctx.enter_context(nc.sbuf_tensor(n, s, d))
        self.m1 = sb("m1", [P, D + 16], F32)
        self.m2 = sb("m2", [4, P], F32)
        self.ow = sb("ow", [P, D], F32)
        self.nw = sb("nw", [P, 1], F32)
        self.gate_b1 = sb("gate_b1", [P, 1], F32)
        self.gate_b2 = sb("gate_b2", [P, 4], F32)
        self.temp = sb("temp", [P, 4], F32)
        self.keep = sb("keep", [P, H], F32)

    def fetch_gate_weights(self, sp, w):
        sp.dma_start(self.m1[:], w["L0_attn_mlp1_w"]).then_inc(self.gate_fetched, 16)
        sp.dma_start(self.m2[:], w["L0_attn_mlp2_w"]).then_inc(self.gate_fetched, 16)
        sp.dma_start(self.ow[:], w["L0_attn_o_w"]).then_inc(self.gate_fetched, 16)
        for h in range(H):
            sp.dma_start(self.nw[DH * h:DH * h + DH, :], w["L0_attn_norm_w"].unsqueeze(1)).then_inc(self.gate_fetched, 16)
        sp.dma_start(self.gate_b1[:], w["L0_attn_mlp1_b"].unsqueeze(1)).then_inc(self.gate_fetched, 16)
        sp.dma_start(self.gate_b2[:], w["L0_attn_mlp2_b"].partition_broadcast(P)).then_inc(self.gate_fetched, 16)
        sp.dma_start(self.temp[:, 0:1], w["L0_attn_logit_temp"].partition_broadcast(P)).then_inc(self.gate_fetched, 16)
        sp.dma_start(self.keep[:], w["L0_attn_conv_res_logit"].partition_broadcast(P)).then_inc(self.gate_fetched, 16)

    def cross_weights(self):
        XW = XH * XD
        wo = self.arena[:, 3 * XW:4 * XW].rearrange("p (j d) -> p j d", d=D)
        bo = self.arena[:, 4 * XW:4 * XW + D]
        cx = self.arena[:, 4 * XW + D:4 * XW + D + B // 2 * DC].rearrange("p (m d) -> p m d", d=DC)
        return self.arena[:, 0:XW], self.arena[0:DC, XW:2 * XW], self.arena[0:DC, 2 * XW:3 * XW], wo, bo, cx

    def fetch_cross_weights(self, sp, w):
        wq, wk, wv, wo, bo, cx = self.cross_weights()
        sp.dma_start(wq, w["L0_xattn_w_q"]).then_inc(self.cross_fetched, 16)
        sp.dma_start(wk, w["L0_xattn_w_k"]).then_inc(self.cross_fetched, 16)
        sp.dma_start(wv, w["L0_xattn_w_v"]).then_inc(self.cross_fetched, 16)
        sp.dma_start(cx, w["ctx_768"].rearrange("(m c) k d -> (c k) m d", c=2)).then_inc(self.cross_fetched, 16)
        sp.dma_start(wo, w["L0_xattn_w_out"].rearrange("(j p) d -> p j d", p=P)).then_inc(self.cross_fetched, 16)
        sp.dma_start(bo, w["L0_xattn_b_out"].partition_broadcast(P)).then_inc(self.cross_fetched, 16)

    def expert_weights(self):
        w1 = self.arena[:, 0:E * F].rearrange("p (e f) -> p e f", e=E)
        return w1, self.arena[:, E * F:].rearrange("p (e c d) -> p e c d", e=E, c=FT)

    def fetch_expert_weights(self, sp, w):
        w1, w2 = self.expert_weights()
        for n in range(4):
            at = slice(n * E // 4, (n + 1) * E // 4)
            sp.dma_start(w1[:, at], w["L0_ffn_w1"][at].rearrange("e p f -> p e f")).then_inc(self.expert_fetched, 16)
            sp.dma_start(w2[:, at], w["L0_ffn_w2"][at].rearrange("e (c p) d -> p e c d", p=P)
                         ).then_inc(self.expert_fetched, 16)

    def hold_fir(self, nc, ctx):
        sb = lambda n, s, d: ctx.enter_context(nc.sbuf_tensor(n, s, d))
        self.short = sb("short", [P, TILES, D], F32)
        self.long = sb("long", [P, TILES, D], F32)
        self.sums = sb("sums", [P, 3, 4, TILES * H], F32)


def norm_and_transpose(nc, g, stage="ln1"):
    GROUP = 4
    GROUPS = TILES // GROUP
    with ExitStack() as ctx:
        sb = lambda n, s, d: ctx.enter_context(nc.sbuf_tensor(n, s, d))
        sem = lambda n: g.semaphore(nc, n)
        stats = sb(f"{stage}_stats", [P, TILES, 6], F32)
        mean_var = sb(f"{stage}_mean_var", [P, TILES, 2], F32)
        rstd = sb(f"{stage}_rstd", [P, TILES], F32)
        shift = sb(f"{stage}_shift", [P, TILES], F32)
        xn = sb(f"{stage}_xn", [P, 2, GROUP, D], F32)
        pt = [ctx.enter_context(nc.psum_tensor(f"{stage}_pt{k}", [P, GROUP * P], F32)) for k in range(2)]
        dve_steps, var_ready, root_ready = sem(f"{stage}_dve_steps"), sem(f"{stage}_var_ready"), sem(f"{stage}_root_ready")
        scales_ready = sem(f"{stage}_scales_ready")
        normed, turned, hi_ready, lo_ready = (sem(f"{stage}_normed_even"), sem(f"{stage}_normed_odd")), sem(f"{stage}_turned"), sem(f"{stage}_hi_ready"), sem(f"{stage}_lo_ready")
        block = ctx.enter_context(nc.Block())
        of_group = lambda x, i: x[:, bass.ds(i * 2, 2), PAD:PAD + L]
        bank = lambda k: pt[k][:].rearrange("p (b l) -> p b l", l=L)

        @block.vector
        def _(dve):
            step = Chain(dve, dve_steps)
            for t in range(TILES):
                step(nc.vector.bn_stats(stats[:, t, :], g.x[:, t, :]))
            step.settle()
            for t in range(TILES):
                step(nc.vector.bn_aggr(mean_var[:, t, :], stats[:, t, :]))
            step.settle()
            step(nc.vector.memset(g.eps5[:], 1e-5))
            nc.vector.memset(g.eps6[:], 1e-6).then_inc(var_ready, 1)
            dve.wait_ge(root_ready, 1)
            step(nc.vector.reciprocal(rstd[:], rstd[:]))
            step.settle()
            nc.vector.scalar_tensor_tensor(out=shift[:], in0=mean_var[:, :, 0], scalar=-1.0, in1=rstd[:], op0=ALU.mult,
                                           op1=ALU.mult).then_inc(scales_ready, 1)
            dve.sem_inc(lo_ready, 2)

            def normalise(t):
                for m in range(GROUP):
                    tile = t * 2 * GROUP + m
                    last = nc.vector.tensor_scalar(xn[:, 0, m, :], g.x[:, tile, :], mean_var[:, tile, 0:1],
                                                   rstd[:, bass.ds(tile, 1)], ALU.subtract, ALU.mult)
                last.then_inc(normed[0], 1)

            def low(i, k):
                dve.wait_ge(hi_ready, i + 1)
                nc.vector.tensor_tensor(of_group(g.xt_lo, i), bank(k), of_group(g.xt_hi, i),
                                        ALU.subtract).then_inc(lo_ready, 1)

            normalise(0)
            with dve.Fori(0, GROUPS // 2 - 1) as t:
                dve.wait_ge(turned, t * 2 + 3)
                normalise(t + 1)
                for k in range(2):
                    low(t * 2 + k, k)
            low(GROUPS - 2, 0)
            low(GROUPS - 1, 1)

        @block.tensor
        def _(pe):
            pe.sem_inc(turned, 2)
            with pe.Fori(0, GROUPS // 2) as t:
                for k in range(2):
                    pe.wait_ge(normed[k], t + 1)
                    pe.wait_ge(lo_ready, t * 2 + k + 1)
                    for m in range(GROUP):
                        last = nc.tensor.transpose(pt[k][:, m * P:m * P + P], xn[:, k, m, :], g.ident[:])
                    last.then_inc(turned, 1)

        @block.scalar
        def _(act):
            act.wait_ge(var_ready, 1)
            nc.scalar.activation(rstd[:], mean_var[:, :, 1], ACT.Sqrt, bias=g.eps5[:]).then_inc(root_ready, 1)
            act.wait_ge(scales_ready, 1)

            def normalise(t):
                for m in range(GROUP):
                    tile = t * 2 * GROUP + GROUP + m
                    last = nc.scalar.activation(xn[:, 1, m, :], g.x[:, tile, :], ACT.Identity,
                                                bias=shift[:, bass.ds(tile, 1)], scale=rstd[:, bass.ds(tile, 1)])
                last.then_inc(normed[1], 1)

            def high(i, k):
                act.wait_ge(turned, i + 3)
                nc.scalar.activation(of_group(g.xt_hi, i), bank(k), ACT.Copy).then_inc(hi_ready, 1)

            normalise(0)
            with act.Fori(0, GROUPS // 2 - 1) as t:
                for k in range(2):
                    high(t * 2 + k, k)
                normalise(t + 1)
            high(GROUPS - 2, 0)
            high(GROUPS - 1, 1)


def load(nc, g, w):
    with ExitStack() as ctx:
        sem = lambda n: g.semaphore(nc, n)
        x_loaded, pool_steps = sem("x_loaded"), sem("const_steps")
        block = ctx.enter_context(nc.Block())

        @block.sync
        def _(sp):
            x_view = w["x"].rearrange("b (h p) d -> p (b h) d", p=P)
            for n in range(4):
                sp.dma_start(g.x[:, 8 * n:8 * n + 8, :], x_view[:, 8 * n:8 * n + 8, :]).then_inc(x_loaded, 16)
            g.fetch_qkv_weights(sp, w)
            sp.wait_ge(x_loaded, 64)

        @block.gpsimd
        def _(pool):
            step = Chain(pool, pool_steps)
            step(nc.gpsimd.memset(g.ident[:], 0.0))
            step(nc.gpsimd.memset(g.causal[:], 1.0))
            step(nc.gpsimd.memset(g.xt_hi[:, :, 0:PAD], 0.0))
            step(nc.gpsimd.memset(g.xt_lo[:, :, 0:PAD], 0.0))
            step.settle()
            step(nc.gpsimd.affine_select(out=g.ident[:], in_=g.ident[:], compare_op=ALU.not_equal, fill=1.0,
                                         base=0, pattern=[[-1, P]], channel_multiplier=1))
            for c in range(CT):
                step.settle()
                rows = g.causal[C * c:C * c + C, :]
                step(nc.gpsimd.affine_select(out=rows, in_=rows, compare_op=ALU.is_ge, fill=0.0, base=0,
                                             pattern=[[1, C]], channel_multiplier=-1))
            step.settle()
            step(nc.gpsimd.tensor_scalar(g.ident16[:], g.ident[:], 1.0, None, ALU.mult))
            step.settle()


def project(nc, g, w):
    with ExitStack() as ctx:
        sb = lambda n, s, d: ctx.enter_context(nc.sbuf_tensor(n, s, d))
        sem = lambda n: g.semaphore(nc, n)
        QKV = 3 * D + H
        w_nat, cw, b_w = g.w_nat, g.cw, g.b_w
        w_tap = sb("w_tap", [P, TAPS, 3, D], F32)
        b_tap = sb("b_tap", [H, D], F32)
        wc_hi = sb("wc_hi", [P, TAPS, QKV], F16)
        wc_lo = sb("wc_lo", [P, TAPS, QKV], F16)
        square = sb("square", [P, 2, 2 * D], F32)
        pw = [ctx.enter_context(nc.psum_tensor(f"pw{j}", [P, 512], F32)) for j in range(2)]
        pq = [ctx.enter_context(nc.psum_tensor(f"pq{j}", [P, 512], F32)) for j in range(4)]
        dve_steps = sem("dve_steps")
        taps_ready, tap_turned, tap_hi_ready = sem("taps_ready"), sem("tap_turned"), sem("tap_hi_ready")
        weights_ready, qkv_ready, qkv_stored = sem("weights_ready"), sem("qkv_ready"), sem("qkv_stored")
        squared, squares_summed = sem("squared"), sem("squares_summed")
        root_ready = sem("root_ready")
        block = ctx.enter_context(nc.Block())

        @block.gpsimd
        def _(pool):
            with pool.Fori(0, B) as b:
                for k in range(2):
                    pool.wait_ge(qkv_stored, b * 2 + k + 5)
                    pool.wait_ge(squares_summed, b * 2 + k + 1)
                    qk = g.qk[:, b * 2 + k, :]
                    nc.gpsimd.tensor_tensor(square[:, k, :], qk, qk, ALU.mult).then_inc(squared, 1)

        @block.vector
        def _(dve):
            step = Chain(dve, dve_steps)
            dve.sem_inc(squares_summed, 2)
            dve.wait_ge(g.qkv_fetched, 16 * 7)
            for j in range(TAPS):
                for n in range(3):
                    step(nc.vector.tensor_scalar(w_tap[:, j, n, :], w_nat[:, n, :], cw[:, n, j:j + 1],
                                                 W_SCALE, ALU.mult, ALU.mult))
            nc.vector.tensor_scalar(b_tap[:], b_w[:], W_SCALE, None, ALU.mult).then_inc(taps_ready, 1)
            for j in range(TAPS):
                n = QKV if j == TAPS - 1 else 3 * D
                dve.wait_ge(tap_hi_ready, j + 1)
                nc.vector.tensor_tensor(wc_lo[:, j, 0:n], pw[j % 2][:, 0:n], wc_hi[:, j, 0:n],
                                        ALU.subtract).then_inc(weights_ready, 1)
            with dve.Fori(0, B // 2) as b:
                for k in range(4):
                    dve.wait_ge(squared, b * 4 + k + 1)
                    nc.vector.tensor_reduce(g.qk_norm[:, b * 4 + k, :],
                                            square[:, k % 2, :].rearrange("p (h d) -> p h d", d=DH),
                                            AX.X, ALU.add).then_inc(squares_summed, 1)
            dve.wait_ge(root_ready, 2)
            step(nc.vector.reciprocal(g.qk_norm[:], g.qk_norm[:]))
            step(nc.vector.tensor_scalar(g.beta[:], g.beta[:], 1e-6, None, ALU.max))
            step.settle()

        @block.tensor
        def _(pe):
            pe.wait_ge(taps_ready, 1)
            for j in range(TAPS):
                if j >= 2:
                    pe.wait_ge(weights_ready, j - 1)
                for n in range(3):
                    last = nc.tensor.transpose(pw[j % 2][:, n * D:(n + 1) * D], w_tap[:, j, n, :], g.ident[:])
                if j == TAPS - 1:
                    last = nc.tensor.transpose(pw[j % 2][:, 3 * D:QKV], b_tap[:], g.ident[0:H, 0:H])
                last.then_inc(tap_turned, 1)
            pe.wait_ge(weights_ready, TAPS)
            with pe.Fori(0, B // 2) as b:
                for k in range(4):
                    pe.wait_ge(qkv_stored, b * 4 + k + 1)
                    for m, j in enumerate(reversed(range(TAPS))):
                        n = QKV if j == TAPS - 1 else 3 * D
                        at = bass.ds(k % 2 * P + j, P)
                        last = product3(pq[k][:, 0:n], (g.xt_hi[:, b * 2 + k // 2, at], g.xt_lo[:, b * 2 + k // 2, at]),
                                        (wc_hi[:, j, 0:n], wc_lo[:, j, 0:n]), m == 0, m == TAPS - 1, pe=nc.tensor)
                    last.then_inc(qkv_ready, 1)

        @block.scalar
        def _(act):
            for j in range(TAPS):
                n = QKV if j == TAPS - 1 else 3 * D
                act.wait_ge(tap_turned, j + 1)
                nc.scalar.activation(wc_hi[:, j, 0:n], pw[j % 2][:, 0:n], ACT.Copy).then_inc(tap_hi_ready, 1)
            act.sem_inc(qkv_stored, 4)
            with act.Fori(0, B // 2) as b:
                for k in range(4):
                    act.wait_ge(qkv_ready, b * 4 + k + 1)
                    nc.scalar.activation(g.beta[:, b * 4 + k, :], pq[k][:, 3 * D:QKV], ACT.Copy)
                    nc.scalar.activation(g.qk[:, b * 4 + k, :], pq[k][:, 0:2 * D], ACT.Silu, scale=1 / W_SCALE)
                    nc.scalar.activation(g.v[:, b * 4 + k, :], pq[k][:, 2 * D:3 * D], ACT.Silu,
                                         scale=1 / W_SCALE).then_inc(qkv_stored, 1)
            act.wait_ge(squares_summed, TILES + 2)
            nc.scalar.activation(g.beta[:], g.beta[:], ACT.Sigmoid, scale=1 / W_SCALE).then_inc(root_ready, 1)
            nc.scalar.activation(g.qk_norm[:], g.qk_norm[:], ACT.Sqrt, bias=g.eps6[:]).then_inc(root_ready, 1)


def delta_solve(nc, g, tt, vb, ak, q16):
    with ExitStack() as ctx:
        sb = lambda n, s, d: ctx.enter_context(nc.sbuf_tensor(n, s, d))
        sem = lambda n: g.semaphore(nc, n)
        ps = lambda n: ctx.enter_context(nc.psum_tensor(n, [P, 512], F32))
        W2 = 2 * DH
        negb = sb("negb", [P, TILES, H], F32)
        bv = sb("bv", [P, TILES, H], F32)
        qkn = sb("qkn", [P, 2, 2, 2, D], F32)
        kv = sb("kv", [P, 2, 2 * H, W2], F32)
        kqt = sb("kqt", [P, 2, 2, 2, 2, P], F16)
        at = sb("at", [P, 2, 2 * H, C], F32)
        flat = g.qk.rearrange("p t n -> p (t n)")
        ng = flat[:, 0:TILES * H * C].rearrange("p (u s) -> p u s", s=C)
        nu = flat[:, TILES * H * C:].rearrange("p (s m) -> p s m", s=C)
        t_u = flat[:, 0:CT * C * C].rearrange("p (t c j) -> p t c j", c=CT, t=C)
        tmp = sb("fs_tmp", [P, CT * 256], F32)
        bank = [ps(f"dl{n}") for n in range(8)]

        pe_steps = sem("dl_pe_steps")
        betas, normed, scaled, vb_hi, qk_hi = sem("dl_betas"), sem("dl_normed"), sem("dl_scaled"), sem("dl_vb_hi"), sem("dl_qk_hi")
        turned, kqt_hi, kqt_ready, gram_ready = sem("dl_turned"), sem("dl_kqt_hi"), sem("dl_kqt_ready"), sem("dl_gram_ready")
        masked, at_hi, at_stored = sem("dl_masked"), sem("dl_at_hi"), sem("dl_at_stored")
        ng_ready, nu_turned, nu_dve, nu_act = sem("dl_ng_ready"), sem("dl_nu_turned"), sem("dl_nu_dve"), sem("dl_nu_act")
        t_clear, t_one, sub_dve, sub_pool = sem("dl_t_clear"), sem("dl_t_one"), sem("dl_sub_dve"), sem("dl_sub_pool")
        tt_turned, tt_hi, tt_lo = sem("dl_tt_turned"), sem("dl_tt_hi"), sem("dl_tt_lo")
        block = ctx.enter_context(nc.Block())

        @block.vector
        def _(dve):
            step = Chain(dve, sub_dve)
            nc.vector.tensor_scalar(negb[:], g.beta[:], -1.0, None, ALU.mult).then_inc(betas, 1)
            nc.vector.tensor_scalar(bv[:], g.beta[:], V_SCALE, None, ALU.mult).then_inc(betas, 1)
            dve.wait_ge(betas, 2)

            def normalise(i, k):
                two = bass.ds(i * 2, 2)
                nc.vector.tensor_tensor(
                    qkn[:, k].rearrange("p t a (h d) -> p (t a h) d", d=DH),
                    g.qk[:, two, :].rearrange("p t (h d) -> p (t h) d", d=DH),
                    g.qk_norm[:, two, :].rearrange("p t h -> p (t h)").unsqueeze(2).to_broadcast([P, 4 * H, DH]),
                    ALU.mult).then_inc(normed, 1)

            def low(i, k):
                two = bass.ds(i * 2, 2)
                dve.wait_ge(vb_hi, i + 1)
                nc.vector.tensor_tensor(
                    vb[:, two, 1].rearrange("p t h w -> p t (h w)"),
                    kv[:, k].rearrange("p (t h) w -> p t (h w)", t=2),
                    vb[:, two, 0].rearrange("p t h w -> p t (h w)"), ALU.subtract)
                dve.wait_ge(qk_hi, i + 1)
                nc.vector.tensor_tensor(q16[:, two, 1, :], qkn[:, k, :, 0, :], q16[:, two, 0, :], ALU.subtract)
                for half in range(2):
                    nc.vector.tensor_tensor(
                        ak[:, i * 2 + half, 1, :, DH:], qkn[:, k, half, 1, :].rearrange("p (h d) -> p h d", d=DH),
                        ak[:, i * 2 + half, 0, :, DH:], ALU.subtract)
                dve.wait_ge(kqt_hi, i + 1)
                nc.vector.tensor_tensor(kqt[:, k, 1].rearrange("p t a n -> p (t a n)"), bank[k][:],
                                        kqt[:, k, 0].rearrange("p t a n -> p (t a n)"),
                                        ALU.subtract).then_inc(kqt_ready, 1)

            def mask(i, k):
                two = bass.ds(i * 2, 2)
                dve.wait_ge(gram_ready, i + 1)
                gram = bank[2 + k][:].rearrange("p (u a n) -> p u a n", a=2, n=C)
                nc.vector.tensor_tensor(
                    ng[:, bass.ds(i * 2 * H, 2 * H), :], gram[:, :, 1, :],
                    negb[:, two, :].rearrange("p t h -> p (t h)").unsqueeze(2).to_broadcast([P, 2 * H, C]),
                    ALU.mult)
                dve.wait_ge(at_stored, i + 1)
                nc.vector.tensor_tensor(at[:, k], gram[:, :, 0, :],
                                        g.causal[:].unsqueeze(1).to_broadcast([P, 2 * H, C]),
                                        ALU.mult).then_inc(masked, 1)

            for k in range(2):
                normalise(k, k)
            for k in range(2):
                low(k, k)
                dve.wait_ge(kqt_ready, k + 1)
                normalise(k + 2, k)
            with dve.Fori(0, B // 2 - 2) as t:
                for k in range(2):
                    mask(t * 2 + k, k)
                    low(t * 2 + 2 + k, k)
                    dve.wait_ge(kqt_ready, t * 2 + k + 3)
                    normalise(t * 2 + 4 + k, k)
            for k in range(2):
                mask(B - 4 + k, k)
                low(B - 2 + k, k)
            for k in range(2):
                mask(B - 2 + k, k)
            for m in range(C // 4):
                if m % 2 == 0:
                    dve.wait_ge(nu_turned, m + 1)
                    nc.vector.tensor_copy(nu[:, 4 * m:4 * m + 4, :], bank[m % 8][:].rearrange("p (s m) -> p s m", s=4)
                                          ).then_inc(nu_dve, 1)
            dve.wait_ge(nu_turned, C // 4)
            nc.vector.memset(t_u[:], 0.0).then_inc(t_clear, 1)
            dve.wait_ge(t_clear, 1)
            for c in range(CT):
                ones = flat[:, c * C:c * C + (C - 1) * (CT * C + 1) + 1:CT * C + 1]
                nc.vector.memset(ones, 1.0).then_inc(t_one, 1)
            dve.wait_ge(nu_dve, C // 8)
            dve.wait_ge(nu_act, C // 8)
            dve.wait_ge(t_one, CT)
            for s in range(C - 1):
                substitute(nc.vector, step, nu, t_u, tmp, s, 0, 3)
            for m in range(C // 4):
                dve.wait_ge(tt_hi, m + 1)
                nc.vector.tensor_tensor(
                    tt[:, :, 1, :].rearrange("p t (h n) -> p t h n", h=H)[:, :, :, 4 * m:4 * m + 4],
                    bank[m % 8][:].rearrange("p (n t h) -> p t h n", n=4, h=H),
                    tt[:, :, 0, :].rearrange("p t (h n) -> p t h n", h=H)[:, :, :, 4 * m:4 * m + 4],
                    ALU.subtract).then_inc(tt_lo, 1)

        @block.gpsimd
        def _(pool):
            step = Chain(pool, sub_pool)
            pool.wait_ge(betas, 2)
            pool.sem_inc(at_stored, 2)

            def scale(i, k):
                two = bass.ds(i * 2, 2)
                pool.wait_ge(normed, i + 1)
                nc.gpsimd.tensor_tensor(
                    kv[:, k, :, 0:DH], g.v[:, two, :].rearrange("p t (h d) -> p (t h) d", d=DH),
                    bv[:, two, :].rearrange("p t h -> p (t h)").unsqueeze(2).to_broadcast([P, 2 * H, DH]),
                    ALU.mult).then_inc(scaled, 1)
                for half in range(2):
                    nc.gpsimd.tensor_tensor(
                        kv[:, k, H * half:H * half + H, DH:],
                        qkn[:, k, half, 1, :].rearrange("p (h d) -> p h d", d=DH),
                        negb[:, i * 2 + half, :].unsqueeze(2).to_broadcast([P, H, DH]),
                        ALU.mult).then_inc(scaled, 1)

            def attn_low(i, k):
                pool.wait_ge(at_hi, i + 1)
                nc.gpsimd.tensor_tensor(
                    ak[:, bass.ds(i * 2, 2), 1, :, 0:C], at[:, k].rearrange("p (t h) n -> p t h n", t=2),
                    ak[:, bass.ds(i * 2, 2), 0, :, 0:C], ALU.subtract).then_inc(at_stored, 1)

            for k in range(2):
                scale(k, k)
            with pool.Fori(0, B // 2 - 1) as t:
                for k in range(2):
                    scale(t * 2 + 2 + k, k)
                    attn_low(t * 2 + k, k)
            for k in range(2):
                attn_low(B - 2 + k, k)
            pool.wait_ge(nu_dve, C // 8)
            pool.wait_ge(nu_act, C // 8)
            pool.wait_ge(t_one, CT)
            for s in range(C - 1):
                substitute(nc.gpsimd, step, nu, t_u, tmp, s, 3, 4)

        @block.scalar
        def _(act):
            def high(i, k):
                two = bass.ds(i * 2, 2)
                act.wait_ge(scaled, i * 3 + 3)
                nc.scalar.activation(vb[:, two, 0].rearrange("p t h w -> p t (h w)"),
                                     kv[:, k].rearrange("p (t h) w -> p t (h w)", t=2),
                                     ACT.Copy).then_inc(vb_hi, 1)
                nc.scalar.activation(q16[:, two, 0, :], qkn[:, k, :, 0, :], ACT.Copy)
                nc.scalar.activation(ak[:, two, 0, :, DH:],
                                     qkn[:, k, :, 1, :].rearrange("p t (h d) -> p t h d", d=DH),
                                     ACT.Copy).then_inc(qk_hi, 1)
                act.wait_ge(turned, i + 1)
                nc.scalar.activation(kqt[:, k, 0].rearrange("p t a n -> p (t a n)"), bank[k][:],
                                     ACT.Copy).then_inc(kqt_hi, 1)

            def attn_high(i, k):
                act.wait_ge(masked, i + 1)
                nc.scalar.activation(ak[:, bass.ds(i * 2, 2), 0, :, 0:C],
                                     at[:, k].rearrange("p (t h) n -> p t h n", t=2), ACT.Copy).then_inc(at_hi, 1)

            for k in range(2):
                high(k, k)
            with act.Fori(0, B // 2 - 1) as t:
                for k in range(2):
                    high(t * 2 + 2 + k, k)
                    attn_high(t * 2 + k, k)
            for k in range(2):
                attn_high(B - 2 + k, k)
            for m in range(C // 4):
                if m % 2 == 1:
                    act.wait_ge(nu_turned, m + 1)
                    nc.scalar.activation(nu[:, 4 * m:4 * m + 4, :], bank[m % 8][:].rearrange("p (s m) -> p s m", s=4),
                                         ACT.Copy).then_inc(nu_act, 1)
            for m in range(C // 4):
                act.wait_ge(tt_turned, m + 1)
                nc.scalar.activation(tt[:, :, 0, :].rearrange("p t (h n) -> p t h n", h=H)[:, :, :, 4 * m:4 * m + 4],
                                     bank[m % 8][:].rearrange("p (n t h) -> p t h n", n=4, h=H),
                                     ACT.Copy).then_inc(tt_hi, 1)

        @block.tensor
        def _(pe):
            step = Chain(pe, pe_steps)

            def turn(i, k):
                pe.wait_ge(normed, i + 1)
                for half in range(2):
                    for a in range(2):
                        n = (half * 2 + a) * P
                        last = nc.tensor.transpose(bank[k][:, n:n + P], qkn[:, k, half, a, :], g.ident[:])
                last.then_inc(turned, 1)

            def grams(i, k):
                wait_apart(pe, kqt_ready, i + 1, g.passed)
                for h in range(H):
                    rows = slice(DH * h, DH * h + DH)
                    for half in range(2):
                        for c in range(CT):
                            toks = slice(C * c, C * c + C)
                            n = (half * H + h) * 2 * C
                            last = product3(bank[2 + k][toks, n:n + 2 * C],
                                            [kqt[rows, k, a, half, 1, toks] for a in range(2)],
                                            [kqt[rows, k, a, half, :, toks] for a in range(2)],
                                            True, True, pe=nc.tensor)
                    if h < H - 1:
                        step(last)
                        step.settle_apart(g.passed)
                last.then_inc(gram_ready, 1)

            for k in range(2):
                turn(k, k)
            with step.loop(B // 2 - 1, 2 * (H - 1)) as t:
                for k in range(2):
                    grams(t * 2 + k, k)
                    turn(t * 2 + 2 + k, k)
            for k in range(2):
                grams(B - 2 + k, k)
            pe.wait_ge(masked, B)
            for m in range(C // 4):
                for s in range(4):
                    last = nc.tensor.transpose(bank[m % 8][:, s * P:s * P + P], ng[:, :, 4 * m + s], g.ident[:])
                last.then_inc(nu_turned, 1)
            pe.wait_ge(sub_dve, 2 * (C - 1))
            pe.wait_ge(sub_pool, 2 * (C - 1))
            for m in range(C // 4):
                for s in range(4):
                    last = nc.tensor.transpose(bank[m % 8][:, s * P:s * P + P], t_u[:, 4 * m + s].rearrange("p c j -> p (c j)"), g.ident[:])
                last.then_inc(tt_turned, 1)


def substitute(engine, step, nu, t_u, tmp, s, c0, c1):
    n, rows, cols = c1 - c0, C - 1 - s, s + 1
    part = tmp[:, c0 * 256:c0 * 256 + n * rows * cols].rearrange("p (t c j) -> p t c j", c=n, t=rows)
    factor = nu[:, s, :].rearrange("p (c t) -> p t c", c=CT)[:, s + 1:C, c0:c1]
    if s:
        step.settle()
    step(engine.tensor_tensor(part, factor.unsqueeze(3).to_broadcast([P, rows, n, cols]),
                              t_u[:, s:s + 1, c0:c1, 0:cols].to_broadcast([P, rows, n, cols]), ALU.mult))
    step.settle()
    below = t_u[:, s + 1:C, c0:c1, 0:cols]
    step(engine.tensor_tensor(below, below, part, ALU.add))


def delta_rule(nc, g):
    with ExitStack() as ctx:
        sb = lambda n, s, d: ctx.enter_context(nc.sbuf_tensor(n, s, d))
        tt = sb("tt", [P, TILES, 2, H * C], F16)
        vb = sb("vb", [P, TILES, 2, H, 2 * DH], F16)
        ak = sb("ak", [P, TILES, 2, H, 2 * DH], F16)
        q16 = g.delta[:].bitcast(F16).rearrange("p t (a n) -> p t a n", a=2)
        delta_solve(nc, g, tt, vb, ak, q16)
        delta_apply(nc, g, tt, vb, ak, q16)


def delta_apply(nc, g, tt, vb, ak, q16):
    with ExitStack() as ctx:
        sb = lambda n, s, d: ctx.enter_context(nc.sbuf_tensor(n, s, d))
        sem = lambda n: g.semaphore(nc, n)
        W2 = 2 * DH
        s_tt = sb("s_tt", [P, 2, 2, 2, H, C], F16)
        s_vb = sb("s_vb", [P, 2, 2, 2, H, W2], F16)
        s_ak = sb("s_ak", [P, 2, 2, 2, H, W2], F16)
        wu = sb("wu", [P, 2, 2, H, W2], F16)
        wide_tt = sb("wide_tt", [P, 2, 2, H, CT, C], F16)
        wide_ak = sb("wide_ak", [P, 2, 2, H, 2, CT, C], F16)
        wide_u = sb("wide_u", [P, 2, 2, H, CT, DH], F16)
        spare = wide_ak[:].rearrange("p k a h m c n -> p (k a h m c n)")
        s_bt = spare[:, 0:2048].rearrange("p (q c a n) -> p q c a n", q=2, c=2 * CT, a=2)
        wide_state = wide_tt[:].rearrange("p k a h c n -> p k (a h c n)").rearrange(
            "p k (c a h n) -> p k c a h n", c=CT, a=2, h=H)
        bt = g.qk.bitcast(F16).rearrange("p t (c a n) -> p (t c) a n", c=CT, a=2)
        ku = tt[:].bitcast(F32).rearrange("p t a n -> p (t a n)").rearrange("p (t n) -> p t n", n=CT * DH)
        states = vb[:].rearrange("p t a h w -> p (t a h w)")[:, 0:B * NCH * 2 * DH].rearrange(
            "p (m a d) -> p m a d", a=2, d=DH)
        flat = s_vb[:].rearrange("p q k a h w -> p (q k a h w)")
        bt_chunk = bt.rearrange("p (b n) a d -> p b n a d", n=NCH)
        move = ak[:, 0:TILES // 2].rearrange("p t a h w -> p (t a h w)").rearrange(
            "p (r b a h d) -> p r b a h d", r=2, b=B, a=2, h=H)
        state16 = flat[:, B * 2 * DH:2 * B * 2 * DH].rearrange("p (a b d) -> p a b d", a=2, b=B)
        state = s_ak[:].bitcast(F32).rearrange("p q k a h w -> p (q k a h w)")[:, 0:B * DH].rearrange(
            "p (b d) -> p b d", b=B)
        bank = [ctx.enter_context(nc.psum_tensor(f"da{n}", [P, 512], F32)) for n in range(2)]
        part = [ctx.enter_context(nc.psum_tensor(f"da_part{n}", [P, 512], F32)) for n in range(2)]
        moves = [ctx.enter_context(nc.psum_tensor(f"da_moves{n}", [P, 1024], F32)) for n in range(2)]
        both = lambda k: moves[k][:].rearrange("p (m x) -> p m x", x=512)[:, :, 0:CT * C].rearrange(
            "p m (c n) -> p c m n", c=CT)
        bt_of = lambda i, a: bt[:, bass.ds(i * CT, CT), a, :].rearrange("p c (m n) -> p c m n", m=2)
        staged_first = [sem("da_staged_first0"), sem("da_staged_first1")]
        staged_rest = [sem("da_staged_rest0"), sem("da_staged_rest1")]
        staged_out = [sem("da_staged_out0"), sem("da_staged_out1")]
        wu_ready, wu_hi, wu_lo = sem("da_wu_ready"), sem("da_wu_hi"), sem("da_wu_lo")
        state_spread_act = sem("da_state_spread_act")
        state_spread, move_clear, move_dve, move_act = sem("da_state_spread"), sem("da_move_clear"), sem("da_move_dve"), sem("da_move_act")
        out_ready, cleared = sem("da_out_ready"), sem("da_cleared")
        tt_spread, ak_spread, u_spread = sem("da_tt_spread"), sem("da_ak_spread"), sem("da_u_spread")
        bt_hi, bt_lo, ku_stored, part_stored = sem("da_bt_hi"), sem("da_bt_lo"), sem("da_ku_stored"), sem("da_part_stored")
        dve_steps, state_ready = sem("da_dve_steps"), sem("da_state_ready")
        s_hi, s_lo, moved = sem("da_s_hi"), sem("da_s_lo"), sem("da_moved")
        read_out, out_added, states_stored = sem("da_read_out"), sem("da_out_added"), sem("da_states_stored")
        block = ctx.enter_context(nc.Block())

        @block.sync
        def _(sp):
            def fetch_first(pair, q):
                tiles = bass.ds(pair * 2, 2)
                sp.dma_start(s_tt[:, q], tt[:, tiles].rearrange("p t a (h n) -> p t a h n", h=H)
                             ).then_inc(staged_first[q], 16)
                sp.dma_start(s_vb[:, q], vb[:, tiles]).then_inc(staged_first[q], 16)

            def fetch_rest(pair, q):
                sp.dma_start(s_ak[:, q], ak[:, bass.ds(pair * 2, 2)]).then_inc(staged_rest[q], 16)

            def fetch_both(n, q, last):
                wait_apart(sp, out_ready, n * 2 + 2, g.passed)
                fetch_rest(n, q)
                if not last:
                    wait_apart(sp, wu_ready, n * 2, g.passed)
                    fetch_first(n + 1, 1 - q)

            for n in range(2):
                fetch_first(n, n)
                fetch_rest(n, n)
            sp.wait_ge(wu_ready, 2)
            fetch_first(2, 0)
            with sp.Fori(0, TILES // 4 - 2) as t:
                fetch_both(t * 2 + 2, 0, False)
                fetch_both(t * 2 + 3, 1, False)
            fetch_both(TILES // 2 - 2, 0, False)
            fetch_both(TILES // 2 - 1, 1, True)
            sp.wait_ge(states_stored, NCH)
            with sp.Fori(0, TILES // 4) as t:
                for q in range(2):
                    chunks = bass.ds((t * 4 + q * 2) * CT, 2 * CT)
                    sp.wait_ge(read_out, t * 4 + q * 2 + 2)
                    sp.dma_start(s_bt[:, q], bt[:, chunks]).then_inc(staged_out[q], 16)

        @block.gpsimd
        def _(pool):
            nc.gpsimd.memset(wide_tt[:], 0.0).then_inc(cleared, 1)
            pool.wait_ge(cleared, 2)
            nc.gpsimd.memset(wide_ak[:], 0.0).then_inc(cleared, 1)
            for q in range(2):
                pool.wait_ge(staged_rest[q], 16 * TILES // 8)
            nc.gpsimd.memset(move, 0.0).then_inc(move_clear, 1)

        @block.tensor
        def _(pe):
            pe.sem_inc(out_ready, 4)

            def find_wu(i, t, q, k):
                pe.wait_ge(staged_first[q], t * 32 + 32)
                pe.wait_ge(tt_spread, i + 1)
                for h in range(H):
                    last = product3(bank[k][:, h * W2:h * W2 + W2],
                                    [wide_tt[:, k, a, h].rearrange("p c t -> p (c t)") for a in range(2)],
                                    [s_vb[:, q, k, a, h, :] for a in range(2)], True, True, pe=nc.tensor)
                last.then_inc(wu_ready, 1)

            def find_moves(i, q, k):
                pe.wait_ge(u_spread, i + 1)
                pe.wait_ge(ak_spread, i + 1)
                wide = lambda a, h, kind: wide_ak[:, k, a, h, kind].rearrange("p c n -> p (c n)")
                turned = moves[k][:, 0:CT * C]
                nc.tensor.matmul(turned, q16[:, i, 0, :], g.ident16[:], start=True, stop=False,
                                 skip_group_check=True)
                nc.tensor.matmul(turned, q16[:, i, 1, :], g.ident16[:], start=False, stop=False,
                                 skip_group_check=True)
                for h in range(H):
                    product3(moves[k][DH * h:DH * h + DH, 0:CT * C], [wu[:, k, a, h, DH:] for a in range(2)],
                             [wide(a, h, 0) for a in range(2)], False, True, pe=nc.tensor, skip_group_check=True)
                for h in range(H):
                    rows = slice(DH * h, DH * h + DH)
                    product3(moves[k][rows, 512:512 + CT * C], [wu[:, k, a, h, DH:] for a in range(2)],
                             [wide(a, h, 1) for a in range(2)], True, True, pe=nc.tensor)
                    product3(moves[k][rows, 512 + CT * C:512 + 2 * CT * C],
                             [s_ak[:, q, k, a, h, C:] for a in range(2)],
                             [wide_u[:, k, a, h].rearrange("p c n -> p (c n)") for a in range(2)],
                             True, True, pe=nc.tensor)
                for h in range(H):
                    last = product3(part[k][:, h * DH:h * DH + DH], [wide(a, h, 0) for a in range(2)],
                                    [wu[:, k, a, h, 0:DH] for a in range(2)], True, True, pe=nc.tensor)
                last.then_inc(out_ready, 1)

            find_wu(0, 0, 0, 0)
            find_wu(1, 0, 0, 1)
            with pe.Fori(0, TILES // 4 - 1) as t:
                for j in range(4):
                    find_moves(t * 4 + j, j // 2, j % 2)
                    find_wu(t * 4 + j + 2, t + j // 2, (j // 2 + 1) % 2, j % 2)
            for j in range(4):
                find_moves(TILES - 4 + j, j // 2, j % 2)
                if j < 2:
                    find_wu(TILES - 2 + j, TILES // 4 - 1, 1, j % 2)
            def advance(n, r):
                pe.wait_ge(move_dve, n + 1)
                pe.wait_ge(move_act, n + 1)
                pe.wait_ge(s_lo, n + 1)
                for b in range(B):
                    last = product3(bank[0][:, b * DH:b * DH + DH],
                                    [move[:, r, b, a].rearrange("p h d -> p (h d)") for a in range(2)],
                                    [state16[:, a, b, :] for a in range(2)], True, True, pe=nc.tensor)
                last.then_inc(moved, 1)

            with pe.Fori(0, NCH // 2 - 1) as n:
                advance(n * 2, 0)
                advance(n * 2 + 1, 1)
            advance(NCH - 2, 0)
            pe.sem_inc(read_out, 4)
            with pe.Fori(0, TILES // 4) as t:
                for q in range(2):
                    pe.wait_ge(staged_out[q], t * 16 + 16)
                    for k in range(2):
                        i = t * 4 + q * 2 + k
                        pe.wait_ge(out_added, i + 1)
                        pe.wait_ge(state_spread, i + 1)
                        pe.wait_ge(state_spread_act, i + 1)
                        for c in range(CT):
                            last = product3(part[k][C * c:C * c + C, 0:H * DH],
                                            [s_bt[:, q, k * CT + c, a, 0:C] for a in range(2)],
                                            [wide_state[:, k, c, a].rearrange("p h n -> p (h n)") for a in range(2)],
                                            True, True, pe=nc.tensor)
                        last.then_inc(read_out, 1)

        @block.scalar
        def _(act):
            def spread_tt(t, q, k):
                act.wait_ge(staged_first[q], t * 32 + 32)
                for c in range(CT):
                    rows = slice(C * c, C * c + C)
                    last = nc.scalar.activation(wide_tt[rows, k, :, :, c, :].rearrange("p a h n -> p (a h) n"),
                                                s_tt[rows, q, k].rearrange("p a h n -> p (a h) n"), ACT.Copy)
                last.then_inc(tt_spread, 1)

            def wu_high(i, k):
                act.wait_ge(wu_ready, i + 1)
                nc.scalar.activation(wu[:, k, 0].rearrange("p h w -> p (h w)"), bank[k][:, 0:H * W2],
                                     ACT.Copy).then_inc(wu_hi, 1)

            def moves_high(i, k):
                act.wait_ge(out_ready, i + 5)
                nc.scalar.activation(bt_of(i, 0), both(k), ACT.Copy).then_inc(bt_hi, 1)
                nc.scalar.activation(ku[:, i, :], moves[k][:, 512 + CT * C:512 + 2 * CT * C], ACT.Copy
                                     ).then_inc(ku_stored, 1)

            act.wait_ge(cleared, 3)
            spread_tt(0, 0, 0)
            spread_tt(0, 0, 1)
            wu_high(0, 0)
            spread_tt(0, 1, 0)
            wu_high(1, 1)
            with act.Fori(0, TILES // 4 - 1) as t:
                for j in range(4):
                    moves_high(t * 4 + j, j % 2)
                    wu_high(t * 4 + j + 2, j % 2)
                    spread_tt(t + (j + 3) // 4, (j + 3) // 2 % 2, (j + 1) % 2)
            for j in range(4):
                moves_high(TILES - 4 + j, j % 2)
                if j < 2:
                    wu_high(TILES - 2 + j, j % 2)
                if j == 0:
                    spread_tt(TILES // 4 - 1, 1, 1)

            def spread_move(n):
                for h in range(H // 2, H):
                    rows = slice(DH * h, DH * h + DH)
                    last = nc.scalar.activation(move[rows, n % 2, :, :, h, :], bt_chunk[rows, :, n, :, C:], ACT.Copy)
                last.then_inc(move_act, 1)

            act.wait_ge(move_clear, 1)
            act.wait_ge(bt_lo, TILES)
            spread_move(0)
            with act.Fori(0, NCH - 1) as n:
                act.wait_ge(state_ready, n + 1)
                nc.scalar.activation(state16[:, 0], state, ACT.Copy).then_inc(s_hi, 1)
                spread_move(n + 1)
            act.wait_ge(state_ready, NCH)
            nc.scalar.activation(state16[:, 0], state, ACT.Copy).then_inc(s_hi, 1)
            act.wait_ge(states_stored, NCH)
            with act.Fori(0, TILES // 2) as t:
                for k in range(2):
                    i = t * 2 + k
                    wait_apart(act, read_out, i + 3, g.passed)
                    for h in range(H // 2, H):
                        rows = slice(DH * h, DH * h + DH)
                        last = nc.scalar.activation(wide_state[rows, k, :, :, h, :], states[rows, bass.ds(i * CT, CT)],
                                                    ACT.Copy)
                    last.then_inc(state_spread_act, 1)

        @block.vector
        def _(dve):
            step = Chain(dve, dve_steps)
            nc.vector.memset(wide_u[:], 0.0).then_inc(cleared, 1)

            def spread_ak(t, q, k):
                dve.wait_ge(staged_rest[q], t * 16 + 16)
                for c in range(CT):
                    rows = slice(C * c, C * c + C)
                    last = nc.vector.tensor_copy(wide_ak[rows, k, :, :, :, c, :].rearrange("p a h m n -> p (a h) m n"),
                                                 s_ak[rows, q, k].rearrange("p a h (m n) -> p (a h) m n", m=2))
                last.then_inc(ak_spread, 1)

            def wu_low(i, k):
                dve.wait_ge(wu_hi, i + 1)
                nc.vector.tensor_tensor(wu[:, k, 1].rearrange("p h w -> p (h w)"), bank[k][:, 0:H * W2],
                                        wu[:, k, 0].rearrange("p h w -> p (h w)"), ALU.subtract).then_inc(wu_lo, 1)
                dve.wait_ge(wu_lo, i + 1)
                for c in range(CT):
                    rows = slice(C * c, C * c + C)
                    last = nc.vector.tensor_copy(wide_u[rows, k, :, :, c, :].rearrange("p a h n -> p (a h) n"),
                                                 wu[rows, k, :, :, 0:DH].rearrange("p a h n -> p (a h) n"))
                last.then_inc(u_spread, 1)

            def moves_low(i, k):
                dve.wait_ge(out_ready, i + 5)
                nc.vector.tensor_scalar(g.delta[:, i, :], part[k][:, 0:H * DH], 1 / V_SCALE, None,
                                        ALU.mult).then_inc(part_stored, 1)
                dve.wait_ge(ku_stored, i + 1)
                nc.vector.tensor_tensor(bt_of(i, 1), both(k), bt_of(i, 0), ALU.subtract).then_inc(bt_lo, 1)

            dve.wait_ge(cleared, 3)
            for k in range(2):
                spread_ak(0, 0, k)
                wu_low(k, k)
            with dve.Fori(0, TILES // 4 - 1) as t:
                for j in range(4):
                    moves_low(t * 4 + j, j % 2)
                    spread_ak(t + j // 2, (j // 2 + 1) % 2, j % 2)
                    wu_low(t * 4 + j + 2, j % 2)
            for j in range(4):
                moves_low(TILES - 4 + j, j % 2)
                if j < 2:
                    spread_ak(TILES // 4 - 1, 1, j % 2)
                    wu_low(TILES - 2 + j, j % 2)
            step(nc.vector.memset(wide_state, 0.0))
            nc.vector.memset(state, 0.0).then_inc(state_ready, 1)
            dve.wait_ge(ku_stored, TILES)
            dve.wait_ge(bt_lo, TILES)
            ku_chunk = ku.rearrange("p t (c d) -> p (t c) d", d=DH).rearrange("p (b n) d -> p b n d", n=NCH)
            st_chunk = states.rearrange("p (b n) a d -> p b n a d", n=NCH)

            def spread_move(n):
                for h in range(H // 2):
                    rows = slice(DH * h, DH * h + DH)
                    last = nc.vector.tensor_copy(move[rows, n % 2, :, :, h, :], bt_chunk[rows, :, n, :, C:])
                last.then_inc(move_dve, 1)

            dve.wait_ge(move_clear, 1)
            spread_move(0)
            with step.loop(NCH - 1, 1) as n:
                dve.wait_ge(s_hi, n + 1)
                nc.vector.tensor_tensor(state16[:, 1], state, state16[:, 0], ALU.subtract).then_inc(s_lo, 1)
                step(nc.vector.tensor_tensor(state, state, ku_chunk[:, :, n, :], ALU.add))
                dve.wait_ge(s_lo, n + 1)
                nc.vector.tensor_copy(st_chunk[:, :, n], state16.rearrange("p a b d -> p b a d")
                                      ).then_inc(states_stored, 1)
                spread_move(n + 1)
                step.settle()
                dve.wait_ge(moved, n + 1)
                nc.vector.tensor_tensor(state, state, bank[0][:].rearrange("p (b d) -> p b d", d=DH),
                                        ALU.add).then_inc(state_ready, 1)
            dve.wait_ge(s_hi, NCH)
            nc.vector.tensor_tensor(state16[:, 1], state, state16[:, 0], ALU.subtract).then_inc(s_lo, 1)
            dve.wait_ge(s_lo, NCH)
            nc.vector.tensor_copy(st_chunk[:, :, NCH - 1], state16.rearrange("p a b d -> p b a d")
                                  ).then_inc(states_stored, 1)
            dve.sem_inc(out_added, 2)
            dve.wait_ge(states_stored, NCH)

            def spread_state(i, k):
                dve.wait_ge(read_out, i + 3)
                for h in range(H // 2):
                    rows = slice(DH * h, DH * h + DH)
                    last = nc.vector.tensor_copy(wide_state[rows, k, :, :, h, :], states[rows, bass.ds(i * CT, CT)])
                last.then_inc(state_spread, 1)

            def add(i, k):
                dve.wait_ge(read_out, i + 5)
                nc.vector.scalar_tensor_tensor(out=g.delta[:, i, :], in0=part[k][:, 0:H * DH],
                                               scalar=1 / V_SCALE, in1=g.delta[:, i, :], op0=ALU.mult,
                                               op1=ALU.add).then_inc(out_added, 1)

            spread_state(0, 0)
            with dve.Fori(0, TILES // 2 - 1) as t:
                for k in range(2):
                    spread_state(t * 2 + k + 1, 1 - k)
                    add(t * 2 + k, k)
            spread_state(TILES - 1, 1)
            add(TILES - 2, 0)
            add(TILES - 1, 1)


def lay_out_fir(weight):
    import numpy as np
    w = np.asarray(weight).reshape(D, -1)
    taps = w.shape[1]
    rows = np.zeros((2 * P + taps + taps % 2, D), w.dtype)
    rows[P - 1:P - 1 + taps] = w[:, ::-1].T
    return np.ascontiguousarray(rows.reshape(-1, D // FG, FG).transpose(1, 0, 2))


def fir(nc, g, w):
    with ExitStack() as ctx:
        sb = lambda n, s, d: ctx.enter_context(nc.sbuf_tensor(n, s, d))
        sem = lambda n: g.semaphore(nc, n)
        kinds = []
        for name, taps in (("short", FS), ("long", FL)):
            rows = w[f"fir_{name}"].shape[1]
            width = P + taps - 1 + (taps - 1) % 2
            kinds.append((name, taps, rows, width))
        n_src = [D * rows // P for _, _, rows, _ in kinds]
        raw = [sb(f"raw_{kind[0]}", [P, n], F32) for kind, n in zip(kinds, n_src)]
        half = [sb(f"half_{kind[0]}", [P, 2, n], F16) for kind, n in zip(kinds, n_src)]
        store = [nc.dram_tensor(f"fir_halves_{kind[0]}", (2, D // FG, kind[2], FG), F16, kind="Internal") for kind in kinds]
        toep = [sb(f"toep_{kind[0]}", [P, 2, 2, kind[3], FG], F16) for kind in kinds]
        v16 = sb("v16", [P, 2, TILES, D], F16)
        flip = sb("flip", [P, P], F32)
        bank = [[ctx.enter_context(nc.psum_tensor(f"fir{f}{k}", [P, FG * TILES], F32)) for k in range(2)] for f in range(2)]
        NG = D // FG
        flat_banks = bank[0] + bank[1]
        PART = 4
        PARTS = TILES // PART
        US = TILES * H // NG
        square = g.arena[:, 0:4 * US * DH].rearrange("p (k n u d) -> p k n u d", k=2, n=2, d=DH)
        units = lambda x, i: x[:].rearrange("p t (h d) -> p (t h) d", d=DH)[:, bass.ds(i * US, US), :]
        head_square = g.arena[:, 4 * US * DH:4 * US * DH + 2 * TILES * DH].rearrange("p (n t d) -> p n t d", n=2, d=DH)
        head_of = lambda x, h: x[:].rearrange("p t (h d) -> p t h d", d=DH)[:, :, h, :]
        head_squared, head_summed = sem("fir_head_squared"), sem("fir_head_summed")
        squared, squares_summed, sums_ready = sem("fir_squared"), sem("fir_squares_summed"), sem("fir_sums_ready")
        v_turned, flip_steps = sem("fir_v_turned"), sem("fir_flip_steps")
        loaded, high, low, stored = sem("fir_loaded"), sem("fir_high"), sem("fir_low"), sem("fir_stored")
        expanded = [[sem(f"fir_expanded{f}{k}") for k in range(2)] for f in range(2)]
        v_high, v_low, product_ready = sem("fir_v_high"), sem("fir_v_low"), sem("fir_product_ready")
        short_stored, long_stored = sem("fir_short_stored"), sem("fir_long_stored")
        block = ctx.enter_context(nc.Block())

        @block.sync
        def _(sp):
            for f, kind in enumerate(kinds):
                src = w[f"fir_{kind[0]}"].rearrange("g u c -> (g u c)").rearrange("(p n) -> p n", p=P)
                sp.dma_start(raw[f][:], src).then_inc(loaded, 16)
            sp.wait_ge(low, 2)
            for f, kind in enumerate(kinds):
                for a in range(2):
                    dst = store[f].ap()[a].rearrange("g u c -> (g u c)").rearrange("(p n) -> p n", p=P)
                    sp.dma_start(dst, half[f][:, a, :]).then_inc(stored, 16)
            sp.wait_ge(stored, 64)
            for n in range(NG):
                if n >= 2:
                    sp.wait_ge(product_ready, n - 1)
                for f, (name, taps, rows, width) in enumerate(kinds):
                    for a in range(2):
                        first = (a * NG + n) * rows * FG
                        src = bass.AP(store[f], first, [[FG, P], [1, width * FG]])
                        sp.dma_start(toep[f][:, n % 2, a].rearrange("p t c -> p (t c)"), src
                                     ).then_inc(expanded[f][n % 2], 16)
            g.fetch_gate_weights(sp, w)

        @block.gpsimd
        def _(pool):
            nc.gpsimd.memset(flip[:], 0.0).then_inc(flip_steps, 1)
            pool.wait_ge(flip_steps, 1)
            nc.gpsimd.affine_select(out=flip[:], in_=flip[:], compare_op=ALU.not_equal, fill=1.0, base=1 - P,
                                    pattern=[[1, P]], channel_multiplier=1).then_inc(flip_steps, 1)

        @block.vector
        def _(dve):
            for f in range(2):
                dve.wait_ge(high, f + 1)
                nc.vector.scalar_tensor_tensor(out=half[f][:, 1, :], in0=raw[f][:], scalar=W_SCALE,
                                               in1=half[f][:, 0, :], op0=ALU.mult,
                                               op1=ALU.subtract).then_inc(low, 1)
            for n in range(PARTS):
                at = slice(n * PART, (n + 1) * PART)
                dve.wait_ge(v_high, n + 1)
                nc.vector.scalar_tensor_tensor(out=v16[:, 1, at].rearrange("p t d -> p (t d)"), in0=flat_banks[n % 4][:],
                                               scalar=V_SCALE, in1=v16[:, 0, at].rearrange("p t d -> p (t d)"),
                                               op0=ALU.mult, op1=ALU.subtract).then_inc(v_low, 1)
            dve.sem_inc(short_stored, 2)
            with dve.Fori(0, NG // 2) as t:
                for k in range(2):
                    i = t * 2 + k
                    dve.wait_ge(product_ready, i + 1)
                    nc.vector.tensor_scalar(g.short[:, :, bass.ds(i * FG, FG)],
                                            bank[0][k][:].rearrange("p (c t) -> p t c", c=FG),
                                            1 / (V_SCALE * W_SCALE), None, ALU.mult).then_inc(short_stored, 1)
                    at = bass.ds(i * US, US)
                    for n, x in ((2, g.delta), (3, g.v)):
                        nc.vector.tensor_reduce(g.sums[:, 0, n, at], units(x, i), AX.X, ALU.add)
                        nc.vector.tensor_reduce(g.sums[:, 1, n, at], units(x, i), AX.X, ALU.add,
                                                apply_absolute_value=True).then_inc(sums_ready, 1)
                    wait_apart(dve, squared, i + 1, g.passed)
                    nc.vector.tensor_reduce(g.sums[:, 2, 2:4, at], square[:, k], AX.X, ALU.add
                                            ).then_inc(squares_summed, 1)
                to = lambda s, n: g.sums[:, s, n].rearrange("p (t h) -> p t h", h=H)[:, :, t]
                wait_apart(dve, short_stored, t * 2 + 4, g.passed)
                nc.vector.tensor_reduce(to(0, 0), head_of(g.short, t), AX.X, ALU.add)
                nc.vector.tensor_reduce(to(1, 0), head_of(g.short, t), AX.X, ALU.add, apply_absolute_value=True)
                wait_apart(dve, long_stored, t * 2 + 4, g.passed)
                nc.vector.tensor_reduce(to(0, 1), head_of(g.long, t), AX.X, ALU.add)
                nc.vector.tensor_reduce(to(1, 1), head_of(g.long, t), AX.X, ALU.add, apply_absolute_value=True)
                wait_apart(dve, head_squared, t + 1, g.passed)
                for n in range(2):
                    last = nc.vector.tensor_reduce(to(2, n), head_square[:, n], AX.X, ALU.add)
                last.then_inc(head_summed, 1)

        @block.scalar
        def _(act):
            act.wait_ge(loaded, 32)
            for f in range(2):
                nc.scalar.activation(half[f][:, 0, :], raw[f][:], ACT.Copy, scale=W_SCALE).then_inc(high, 1)
            for n in range(PARTS):
                at = slice(n * PART, (n + 1) * PART)
                act.wait_ge(v_turned, n + 1)
                nc.scalar.activation(v16[:, 0, at].rearrange("p t d -> p (t d)"), flat_banks[n % 4][:], ACT.Copy,
                                     scale=V_SCALE).then_inc(v_high, 1)
            act.sem_inc(long_stored, 2)
            act.sem_inc(squares_summed, 2)
            act.sem_inc(head_summed, 1)
            with act.Fori(0, NG // 2) as t:
                for k in range(2):
                    i = t * 2 + k
                    wait_apart(act, squares_summed, i + 1, g.passed)
                    nc.scalar.activation(square[:, k, 0], units(g.delta, i), ACT.Square)
                    nc.scalar.activation(square[:, k, 1], units(g.v, i), ACT.Square).then_inc(squared, 1)
                    act.wait_ge(product_ready, i + 1)
                    nc.scalar.activation(g.long[:, :, bass.ds(i * FG, FG)],
                                         bank[1][k][:].rearrange("p (c t) -> p t c", c=FG),
                                         ACT.Copy, scale=1 / (V_SCALE * W_SCALE)).then_inc(long_stored, 1)
                act.wait_ge(head_summed, t + 1)
                act.wait_ge(long_stored, t * 2 + 4)
                wait_apart(act, short_stored, t * 2 + 4, g.passed)
                nc.scalar.activation(head_square[:, 0], head_of(g.short, t), ACT.Square)
                nc.scalar.activation(head_square[:, 1], head_of(g.long, t), ACT.Square).then_inc(head_squared, 1)

        @block.tensor
        def _(pe):
            pe.wait_ge(flip_steps, 2)
            for n in range(PARTS):
                if n >= 4:
                    pe.wait_ge(v_low, n - 3)
                nc.tensor.matmul(flat_banks[n % 4][:], flip[:],
                                 g.v[:, n * PART:(n + 1) * PART].rearrange("p t d -> p (t d)"), start=True, stop=True
                                 ).then_inc(v_turned, 1)
            pe.wait_ge(v_low, PARTS)
            with pe.Fori(0, NG // 2) as t:
                for k in range(2):
                    i = t * 2 + k
                    pe.wait_ge(short_stored, i + 1)
                    pe.wait_ge(long_stored, i + 1)
                    for f, (name, taps, rows, width) in enumerate(kinds):
                        pe.wait_ge(expanded[f][k], t * 32 + 32)
                        for c in range(FG):
                            ch = bass.ds(i * FG + c, 1)
                            own = [v16[:, a, :, ch].rearrange("p t c -> p (t c)") for a in range(2)]
                            before = [v16[:, a, 0:TILES:2, ch].rearrange("p t c -> p (t c)") for a in range(2)]
                            out = bank[f][k][:, c * TILES:(c + 1) * TILES]
                            product3(out, [toep[f][:, k, a, 0:P, c] for a in range(2)], own, True, False,
                                     pe=nc.tensor, skip_group_check=True)
                            n = taps - 1
                            last = product3(out[0:n, 1:TILES:2], [toep[f][:, k, a, P:P + n, c] for a in range(2)],
                                            before, False, True, pe=nc.tensor, skip_group_check=True)
                    last.then_inc(product_ready, 1)


def gate_and_add(nc, g, w):
    U = TILES * H
    paths = (g.short, g.long, g.delta, g.v)
    with ExitStack() as ctx:
        sb = lambda n, s, d: ctx.enter_context(nc.sbuf_tensor(n, s, d))
        sem = lambda n: g.semaphore(nc, n)
        m1, m2, ow, nw, b1, b2, temp, keep = g.m1, g.m2, g.ow, g.nw, g.gate_b1, g.gate_b2, g.temp, g.keep
        m1_pad = sb("m1_pad", [P, H, 2, H, 16], F32)
        hs_w = sb("hs_w", [P, 2, P], F16)
        st_w = sb("st_w", [P, 2, H, P], F16)
        m2_w = sb("m2_w", [P, 2, 4], F16)
        o_w = sb("o_w", [P, 2, D], F16)
        o_wf = sb("o_wf", [P, D], F32)
        sq = sb("sq", [P, 2, U // 4, DH], F32)
        raw = g.sums
        stf = sb("stf", [P, TILES, H, 16], F32)
        st16 = sb("st16", [P, TILES, 2, H * 16], F16)
        stt = sb("stt", [P, 2, 2 * P], F16)
        h1 = sb("h1", [P, 2, H, 2 * P], F32)
        h16 = sb("h16", [P, 2, 2, H, 2 * P], F16)
        pr = sb("pr", [P, U, 4], F32)
        ex = sb("ex", [P, U, 4], F32)
        one = sb("one", [P, 2, U], F32)
        STEP = 4
        on = [h1[:, k // 2, k % 2, :].rearrange("p (t d) -> p t d", d=D) for k in range(STEP)]
        ot = [h16[:, k // 2, k % 2, 0:2, :] for k in range(STEP)]
        bank = [ctx.enter_context(nc.psum_tensor(f"gt{n}", [P, 512], F32)) for n in range(8)]
        padded, dve_steps, act_steps, pool_steps = sem("gt_padded"), sem("gt_dve_steps"), sem("gt_act_steps"), sem("gt_pool_steps")
        w_turned, w_high, w_low = sem("gt_w_turned"), sem("gt_w_high"), sem("gt_w_low")
        raw_ready, root_ready, st_ready, st16_hi = sem("gt_raw_ready"), sem("gt_root_ready"), sem("gt_st_ready"), sem("gt_st16_hi")
        st16_ready, st_turned, stt_ready, h_ready = sem("gt_st16_ready"), sem("gt_st_turned"), sem("gt_stt_ready"), sem("gt_h_ready")
        gelu_done, h_hi, h_lo, logits_ready = sem("gt_gelu_done"), sem("gt_h_hi"), sem("gt_h_lo"), sem("gt_logits_ready")
        logits_stored, e_in, e_out, p_ready = sem("gt_logits_stored"), sem("gt_e_in"), sem("gt_e_out"), sem("gt_p_ready")
        mixed_dve, mixed_pool, squared, rms_in, rms_out = sem("gt_mixed_dve"), sem("gt_mixed_pool"), sem("gt_squared"), sem("gt_rms_in"), sem("gt_rms_out")
        on_ready, on_turned, ot_hi, ot_lo, out_ready = sem("gt_on_ready"), sem("gt_on_turned"), sem("gt_ot_hi"), sem("gt_ot_lo"), sem("gt_out_ready")
        keep_ready, misc_ready, sq2_ready, sq2_read = sem("gt_keep_ready"), sem("gt_misc_ready"), sem("gt_sq2_ready"), sem("gt_sq2_read")
        added, w_scaled = sem("gt_added"), sem("gt_w_scaled")
        block = ctx.enter_context(nc.Block())
        units = lambda x: x[:].rearrange("p t (h d) -> p (t h) d", d=DH)
        Q = U // 4
        CUT = 88

        turned_weights = (((hs_w[:, 0], hs_w[:, 1]), bank[0][:, 0:P]),
                          ([st_w[:, a].rearrange("p h n -> p (h n)") for a in range(2)], bank[1][:]),
                          ((m2_w[:, 0], m2_w[:, 1]), bank[2][:, 0:4]))

        @block.sync
        def _(sp):
            g.fetch_cross_weights(sp, w)

        @block.gpsimd
        def _(pool):
            step = Chain(pool, pool_steps)
            step(nc.gpsimd.memset(m1_pad[:], 0.0))
            pool.wait_ge(g.gate_fetched, 16 * 11)
            step.settle()
            for h in range(H):
                for a in range(2):
                    if h or a:
                        pool.wait_ge(padded, 2 * h + a)
                    nc.gpsimd.tensor_scalar(m1_pad[:, h, a, h, :], m1[:, D:], W_SCALE / ST_SCALE, None,
                                            ALU.mult).then_inc(padded, 1)
            pool.sem_inc(h_lo, 2)
            with pool.Fori(0, B // 2) as t:
                for k in range(2):
                    pool.wait_ge(h_hi, t * 2 + k + 1)
                    nc.gpsimd.tensor_tensor(h16[:, k, 1].rearrange("p h n -> p (h n)"),
                                            h1[:, k].rearrange("p h n -> p (h n)"),
                                            h16[:, k, 0].rearrange("p h n -> p (h n)"), ALU.subtract).then_inc(h_lo, 1)
            pool.wait_ge(p_ready, 1)
            mix(nc.gpsimd, step, [units(x)[:, CUT:] for x in paths], pr[:, CUT:], U - CUT)
            step.settle()
            nc.gpsimd.memset(h1[:, 0, 0, 0:1], 0.0).then_inc(mixed_pool, 1)

        @block.scalar
        def _(act):
            step = Chain(act, act_steps)
            act.wait_ge(raw_ready, 1)
            nc.scalar.activation(stf[:].rearrange("p t h (x s) -> p (t h) x s", s=4)[:, :, :, 3],
                                 raw[:, 2].rearrange("p x u -> p u x"), ACT.Sqrt,
                                 scale=ST_SCALE * ST_SCALE).then_inc(root_ready, 1)
            for n, (dst, src) in enumerate(turned_weights):
                act.wait_ge(w_turned, n + 1)
                nc.scalar.activation(dst[0], src, ACT.Copy).then_inc(w_high, 1)
            act.wait_ge(st_ready, 1)
            nc.scalar.activation(st16[:, :, 0, :], stf[:].rearrange("p t h s -> p t (h s)"), ACT.Copy
                                 ).then_inc(st16_hi, 1)
            with act.Fori(0, B // 2) as t:
                for k in range(2):
                    act.wait_ge(h_ready, t * 2 + k + 1)
                    act.wait_ge(h_lo, t * 2 + k + 1)
                    for n in range(2):
                        last = nc.scalar.activation(h1[:, k, 2 * n:2 * n + 2, :].rearrange("p h n -> p (h n)"),
                                                    bank[2 + 2 * k + n][:], ACT.Gelu_apprx_tanh, bias=b1[:],
                                                    scale=1 / W_SCALE)
                    last.then_inc(gelu_done, 1)
            step(nc.scalar.activation(temp[:, 1:2], temp[:, 0:1], ACT.Abs))
            step.settle()
            step(nc.scalar.activation(temp[:, 1:2], temp[:, 1:2], ACT.Exp, scale=-1.0))
            step.settle()
            nc.scalar.activation(temp[:, 1:2], temp[:, 1:2], ACT.Ln, bias=1.0).then_inc(misc_ready, 1)
            act.wait_ge(e_in, 1)
            nc.scalar.activation(ex[:], ex[:], ACT.Exp).then_inc(e_out, 1)
            nc.scalar.activation(keep[:], keep[:], ACT.Sigmoid).then_inc(keep_ready, 1)
            act.wait_ge(mixed_dve, 1)
            act.wait_ge(mixed_pool, 1)
            for m in range(4):
                if m >= 2:
                    act.wait_ge(sq2_read, m - 1)
                nc.scalar.activation(sq[:, m % 2], units(g.short)[:, Q * m:Q * m + Q], ACT.Square
                                     ).then_inc(sq2_ready, 1)
            act.wait_ge(rms_in, 1)
            nc.scalar.activation(one[:, 0], one[:, 0], ACT.Sqrt, bias=g.eps5[:], scale=1 / DH).then_inc(rms_out, 1)
            with act.Fori(0, B // STEP) as t:
                for k in range(STEP):
                    act.wait_ge(on_turned, t * STEP + k + 1)
                    nc.scalar.activation(ot[k][:, 0, :], bank[k][:, 0:2 * P], ACT.Copy).then_inc(ot_hi, 1)

        @block.vector
        def _(dve):
            step = Chain(dve, dve_steps)
            dve.wait_ge(g.gate_fetched, 16 * 11)
            step(nc.vector.tensor_scalar(m1[:, 0:D], m1[:, 0:D], W_SCALE, None, ALU.mult))
            nc.vector.tensor_scalar(m2[:], m2[:], W_SCALE, None, ALU.mult).then_inc(w_scaled, 1)
            stat = lambda s: stf[:].rearrange("p t h (x s) -> p (t h) x s", s=4)[:, :, :, s]
            by_path = lambda n: raw[:, n].rearrange("p x u -> p u x")
            step(nc.vector.tensor_scalar(stat(0), by_path(0), ST_SCALE / DH, None, ALU.mult))
            nc.vector.tensor_scalar(stat(2), by_path(1), ST_SCALE / DH, None, ALU.mult).then_inc(raw_ready, 1)
            dve.wait_ge(root_ready, 1)
            step(nc.vector.scalar_tensor_tensor(out=raw[:, 1].rearrange("p x u -> p (x u)"),
                                                in0=raw[:, 0].rearrange("p x u -> p (x u)"),
                                                scalar=ST_SCALE / DH / DH,
                                                in1=raw[:, 0].rearrange("p x u -> p (x u)"), op0=ALU.mult, op1=ALU.mult))
            step.settle()
            nc.vector.scalar_tensor_tensor(out=stat(1), in0=by_path(2), scalar=ST_SCALE / DH, in1=by_path(1),
                                           op0=ALU.mult, op1=ALU.subtract).then_inc(st_ready, 1)
            for n, (dst, src) in enumerate(turned_weights):
                dve.wait_ge(w_high, n + 1)
                nc.vector.tensor_tensor(dst[1], src, dst[0], ALU.subtract).then_inc(w_low, 1)
            dve.wait_ge(w_turned, 4)
            step(nc.vector.tensor_scalar(o_wf[:], bank[3][:, 0:D], nw[:], W_SCALE, ALU.mult, ALU.mult))
            step.settle()
            step(nc.vector.tensor_copy(o_w[:, 0], o_wf[:]))
            step.settle()
            nc.vector.tensor_tensor(o_w[:, 1], o_wf[:], o_w[:, 0], ALU.subtract).then_inc(w_low, 1)
            dve.wait_ge(st16_hi, 1)
            nc.vector.tensor_tensor(st16[:, :, 1, :], stf[:].rearrange("p t h s -> p t (h s)"), st16[:, :, 0, :],
                                    ALU.subtract).then_inc(st16_ready, 1)

            def keep_stats(i, k):
                dve.wait_ge(st_turned, i + 1)
                nc.vector.tensor_copy(stt[:, k], bank[k][:, 0:2 * P]).then_inc(stt_ready, 1)

            def hidden_high(i, k):
                dve.wait_ge(gelu_done, i + 1)
                nc.vector.tensor_copy(h16[:, k, 0].rearrange("p h n -> p (h n)"),
                                      h1[:, k].rearrange("p h n -> p (h n)")).then_inc(h_hi, 1)

            def store_logits(i, k):
                dve.wait_ge(logits_ready, i + 1)
                nc.vector.tensor_scalar(ex[:, bass.ds(i * 2 * H, 2 * H), :].rearrange("p u n -> p (u n)"),
                                        bank[6 + k][:, 0:2 * H * 4], 1 / W_SCALE, None,
                                        ALU.mult).then_inc(logits_stored, 1)

            keep_stats(0, 0)
            keep_stats(1, 1)
            with dve.Fori(0, B // 2 - 1) as t:
                for k in range(2):
                    keep_stats(t * 2 + 2 + k, k)
                for k in range(2):
                    hidden_high(t * 2 + k, k)
                for k in range(2):
                    store_logits(t * 2 + k, k)
            for k in range(2):
                hidden_high(B - 2 + k, k)
            for k in range(2):
                store_logits(B - 2 + k, k)
            dve.wait_ge(logits_stored, B)
            step(nc.vector.tensor_tensor(ex[:], ex[:], b2[:].unsqueeze(1).to_broadcast([P, U, 4]), ALU.add))
            step.settle()
            step(nc.vector.tensor_reduce(one[:, 0], ex[:], AX.X, ALU.max))
            step.settle()
            step(nc.vector.tensor_tensor(ex[:], ex[:], one[:, 0].unsqueeze(2).to_broadcast([P, U, 4]), ALU.subtract))
            step.settle()
            dve.wait_ge(misc_ready, 1)
            step(nc.vector.tensor_scalar(temp[:, 2:3], temp[:, 0:1], 0.0, None, ALU.max))
            step.settle()
            step(nc.vector.tensor_tensor(temp[:, 2:3], temp[:, 2:3], temp[:, 1:2], ALU.add))
            step.settle()
            step(nc.vector.reciprocal(temp[:, 3:4], temp[:, 2:3]))
            step.settle()
            nc.vector.tensor_scalar(ex[:], ex[:], temp[:, 3:4], None, ALU.mult).then_inc(e_in, 1)
            dve.wait_ge(e_out, 1)
            for n in range(2):
                step(nc.vector.tensor_reduce(one[:, n], ex[:], AX.X, ALU.add))
                step.settle()
                step(nc.vector.reciprocal(one[:, n], one[:, n]))
                step.settle()
                step(nc.vector.tensor_tensor(ex[:], ex[:], one[:, n].unsqueeze(2).to_broadcast([P, U, 4]), ALU.mult))
                step.settle()
                if n == 0:
                    step(nc.vector.tensor_scalar(ex[:], ex[:], 0.02, None, ALU.max))
                    step.settle()
            dve.wait_ge(keep_ready, 1)
            step(nc.vector.tensor_tensor(pr[:, :, 0].rearrange("p (t h) -> p t h", h=H),
                                         ex[:, :, 0].rearrange("p (t h) -> p t h", h=H),
                                         keep[:].unsqueeze(1).to_broadcast([P, TILES, H]), ALU.add))
            nc.vector.tensor_copy(pr[:, :, 1:4], ex[:, :, 1:4]).then_inc(p_ready, 1)
            dve.wait_ge(p_ready, 1)
            mix(nc.vector, step, [units(x)[:, 0:CUT] for x in paths], pr[:, 0:CUT], CUT)
            step.settle()
            nc.vector.memset(h1[:, 1, 0, 0:1], 0.0).then_inc(mixed_dve, 1)
            for m in range(4):
                dve.wait_ge(sq2_ready, m + 1)
                nc.vector.tensor_reduce(one[:, 0, Q * m:Q * m + Q], sq[:, m % 2], AX.X, ALU.add).then_inc(sq2_read, 1)
            dve.wait_ge(sq2_read, 4)
            dve.sem_inc(rms_in, 1)
            dve.wait_ge(rms_out, 1)
            step(nc.vector.reciprocal(one[:, 1], one[:, 0]))
            step.settle()

            def norm(i, k):
                nc.vector.tensor_tensor(
                    on[k].rearrange("p t (h d) -> p (t h) d", d=DH),
                    units(g.short)[:, bass.ds(i * 2 * H, 2 * H), :],
                    one[:, 1, bass.ds(i * 2 * H, 2 * H)].unsqueeze(2).to_broadcast([P, 2 * H, DH]),
                    ALU.mult).then_inc(on_ready, 1)

            def turned_low(i, k):
                dve.wait_ge(ot_hi, i + 1)
                nc.vector.tensor_tensor(ot[k][:, 1, :], bank[k][:, 0:2 * P], ot[k][:, 0, :], ALU.subtract
                                        ).then_inc(ot_lo, 1)

            def add(i, k):
                dve.wait_ge(out_ready, i + 1)
                xs = g.x[:, bass.ds(i * 2, 2), :].rearrange("p t d -> p (t d)")
                nc.vector.scalar_tensor_tensor(out=xs, in0=bank[STEP + k][:, 0:2 * D], scalar=1 / W_SCALE, in1=xs,
                                               op0=ALU.mult, op1=ALU.add).then_inc(added, 1)

            for k in range(STEP):
                norm(k, k)
            with dve.Fori(0, B // STEP - 1) as t:
                for k in range(STEP):
                    turned_low(t * STEP + k, k)
                for k in range(STEP):
                    norm(t * STEP + STEP + k, k)
                for k in range(STEP):
                    add(t * STEP + k, k)
            for k in range(STEP):
                turned_low(B - STEP + k, k)
            for k in range(STEP):
                add(B - STEP + k, k)
            dve.wait_ge(added, B)

        @block.tensor
        def _(pe):
            pe.wait_ge(padded, 2 * H)
            pe.wait_ge(w_scaled, 1)
            nc.tensor.transpose(bank[0][:, 0:P], m1[:, 0:D], g.ident[:]).then_inc(w_turned, 1)
            for h in range(H):
                last = nc.tensor.transpose(bank[1][:, h * P:h * P + P],
                                           m1_pad[:, h].rearrange("p a h s -> p (a h s)"), g.ident[:])
            last.then_inc(w_turned, 1)
            nc.tensor.transpose(bank[2][:, 0:4], m2[:], g.ident[0:4, 0:4]).then_inc(w_turned, 1)
            nc.tensor.transpose(bank[3][:, 0:D], ow[:], g.ident[:]).then_inc(w_turned, 1)
            pe.wait_ge(w_low, 4)
            pe.wait_ge(st16_ready, 1)

            def turn_stats(i, k):
                for half in range(2):
                    last = nc.tensor.matmul(bank[k][:, half * P:half * P + P],
                                            st16[:, i * 2 + half].rearrange("p a n -> p (a n)"), g.ident16[:],
                                            start=True, stop=True)
                last.then_inc(st_turned, 1)

            def hidden(i, k):
                pe.wait_ge(stt_ready, i + 1)
                x_t = [x[:, i, PAD:PAD + L] for x in (g.xt_hi, g.xt_lo)]
                for h in range(H):
                    out = bank[2 + 2 * k + h // 2][:, h % 2 * L:h % 2 * L + L]
                    product3(out, (hs_w[:, 0], hs_w[:, 1]), x_t, True, False, pe=nc.tensor)
                    nc.tensor.matmul(out, st_w[:, 0, h], stt[:, k], start=False, stop=False)
                    last = nc.tensor.matmul(out, st_w[:, 1, h], stt[:, k], start=False, stop=True)
                last.then_inc(h_ready, 1)

            def logits(i, k):
                pe.wait_ge(h_lo, i + 3)
                for half in range(2):
                    for h in range(H):
                        n = (half * H + h) * 4
                        last = product3(bank[6 + k][:, n:n + 4],
                                        [h16[:, k, a, h, half * P:half * P + P] for a in range(2)],
                                        (m2_w[:, 0], m2_w[:, 1]), True, True, pe=nc.tensor)
                last.then_inc(logits_ready, 1)

            for k in range(2):
                turn_stats(k, k)
            for k in range(2):
                hidden(k, k)
            with pe.Fori(0, B // 2 - 1) as t:
                for k in range(2):
                    turn_stats(t * 2 + 2 + k, k)
                for k in range(2):
                    pe.wait_ge(gelu_done, t * 2 + k + 1)
                    hidden(t * 2 + 2 + k, k)
                for k in range(2):
                    logits(t * 2 + k, k)
            for k in range(2):
                logits(B - 2 + k, k)

            def turn(i, k):
                pe.wait_ge(on_ready, i + 1)
                for half in range(2):
                    last = nc.tensor.transpose(bank[k][:, half * P:half * P + P], on[k][:, half], g.ident[:])
                last.then_inc(on_turned, 1)

            def project_out(i, k):
                pe.wait_ge(ot_lo, i + 1)
                for half in range(2):
                    last = product3(bank[STEP + k][:, half * D:half * D + D],
                                    [ot[k][:, a, half * P:half * P + P] for a in range(2)],
                                    (o_w[:, 0], o_w[:, 1]), True, True, pe=nc.tensor)
                last.then_inc(out_ready, 1)

            for k in range(STEP):
                turn(k, k)
            with pe.Fori(0, B // STEP - 1) as t:
                for k in range(STEP):
                    project_out(t * STEP + k, k)
                for k in range(STEP):
                    turn(t * STEP + STEP + k, k)
            for k in range(STEP):
                project_out(B - STEP + k, k)


def mix(engine, step, paths, weights, n):
    for j in range(4):
        step(engine.tensor_tensor(paths[j], paths[j], weights[:, :, j:j + 1].to_broadcast([P, n, DH]), ALU.mult))
    step.settle()
    step(engine.tensor_tensor(paths[0], paths[0], paths[1], ALU.add))
    step(engine.tensor_tensor(paths[2], paths[2], paths[3], ALU.add))
    step.settle()
    step(engine.tensor_tensor(paths[0], paths[0], paths[2], ALU.add))


def cross_attention(nc, g, w):
    XW = XH * XD
    PAIRS = XH // 2
    WS = 64.0
    with ExitStack() as ctx:
        sb = lambda n, s, d: ctx.enter_context(nc.sbuf_tensor(n, s, d))
        sem = lambda n: g.semaphore(nc, n)
        wq, wk, wv, wo, bo, cx = g.cross_weights()
        wqt = sb("xwqt", [P, 2, PAIRS, D], F16)
        wkt = sb("xwkt", [P, 2, PAIRS, DC], F16)
        wvt = sb("xwvt", [P, 2, PAIRS, DC], F16)
        wo16 = sb("xwo16", [P, 2, PAIRS, D], F16)
        g16 = sb("xg16", [DC, 2, 2, PAIRS, D], F16)
        r16 = sb("xr16", [DC, 2, 2, PAIRS, D], F16)
        ct = sb("xct", [DC, 2, B + 2, SKV], F16)
        ct_now = sb("xct_now", [DC, 2, SKV], F16)
        a16 = sb("xa16", [P, 2, 2, XW], F16)
        vw16 = sb("xvw16", [P, 2, 2, PAIRS * D], F16)
        es = sb("xes", [P, 2, XW], F32)
        mx = sb("xmx", [P, 2, XH], F32)
        rs = sb("xrs", [P, 2, XH], F32)
        pt16 = sb("xpt16", [P, 2, XW], F16)
        prep = ctx.enter_context(nc.psum_tensor("xprep", [P, XW], F32))
        turned = ctx.enter_context(nc.psum_tensor("xturned", [P, XW], F32))
        score = [ctx.enter_context(nc.psum_tensor(f"xscore{k}", [P, XW], F32)) for k in range(2)]
        w_turned, w_high, w_low = sem("xa_w_turned"), sem("xa_w_high"), sem("xa_w_low")
        wo_high, joined, joined_high, joined_low = sem("xa_wo_high"), sem("xa_joined"), sem("xa_joined_high"), sem("xa_joined_low")
        bias_added, ctx_copied, dve_steps = sem("xa_bias_added"), sem("xa_ctx_copied"), sem("xa_dve_steps")
        prep_ready, prep_hi, prep_lo = sem("xa_prep_ready"), sem("xa_prep_hi"), sem("xa_prep_lo")
        scores_ready, shifted, e_ready, recip_ready = sem("xa_scores_ready"), sem("xa_shifted"), sem("xa_e_ready"), sem("xa_recip_ready")
        p_ready, pt_ready, pt_hi, pt_lo = sem("xa_p_ready"), sem("xa_pt_ready"), sem("xa_pt_hi"), sem("xa_pt_lo")
        pv_ready, added, pad_clear = sem("xa_pv_ready"), sem("xa_added"), sem("xa_pad_clear")
        block = ctx.enter_context(nc.Block())
        turns = [(wqt, score[0], P, WS, D), (wkt, score[1], P, WS, DC), (wvt, turned, P, WS, DC), (ct, prep, DC, 1.0, P)]
        joins = [(g16, (score[0], score[1])), (r16, (turned, prep))]

        def turned_view(n):
            dst, src, rows, scale, width = turns[n]
            if n == 3:
                return ([dst[:, a, 0:B].rearrange("p b k -> p (b k)") for a in range(2)], src[0:DC, 0:B * SKV], scale)
            return ([dst[:, a] for a in range(2)], src[:].rearrange("p (j n) -> p j n", n=P)[:, :, 0:width], scale)

        def destination(j):
            return a16[:, (j + 3) // 2 % 2] if j % 2 else vw16[:, (j // 2 + 1) % 2]

        @block.sync
        def _(sp):
            sp.wait_ge(w_low, 5)
            sp.wait_ge(bias_added, 4)
            g.fetch_expert_weights(sp, w)

        @block.gpsimd
        def _(pool):
            nc.gpsimd.memset(ct[:, :, B:, :], 0.0).then_inc(pad_clear, 1)
            pool.wait_ge(pad_clear, 1)
            nc.gpsimd.memset(g.xt_hi[:, B, :], 0.0).then_inc(pad_clear, 1)
            pool.wait_ge(pad_clear, 2)
            nc.gpsimd.memset(g.xt_lo[:, B, :], 0.0).then_inc(pad_clear, 1)
            pool.wait_ge(pad_clear, 3)
            pool.wait_ge(g.cross_fetched, 96)
            for n in range(4):
                at = slice(n * TILES // 4, (n + 1) * TILES // 4)
                if n:
                    pool.wait_ge(bias_added, n)
                nc.gpsimd.tensor_tensor(g.x[:, at], g.x[:, at], bo.unsqueeze(1).to_broadcast([P, TILES // 4, D]),
                                        ALU.add).then_inc(bias_added, 1)

            def normalise(count, k):
                pool.wait_ge(recip_ready, count)
                p = es[:, k].rearrange("p (h n) -> p h n", n=SKV)
                nc.gpsimd.tensor_tensor(p, p, rs[:, k].unsqueeze(2).to_broadcast([P, XH, SKV]),
                                        ALU.mult).then_inc(p_ready, 1)

            normalise(1, 0)
            with pool.Fori(0, TILES // 4) as i:
                for j in range(4):
                    normalise(i * 4 + j + 2, (j + 1) % 2)

        @block.scalar
        def _(act):
            act.wait_ge(g.cross_fetched, 96)
            for n in range(4):
                hi, src, scale = turned_view(n)
                act.wait_ge(w_turned, n + 1)
                nc.scalar.activation(hi[0], src, ACT.Copy, scale=scale).then_inc(w_high, 1)
            nc.scalar.activation(wo16[:, 0], wo, ACT.Copy, scale=WS).then_inc(wo_high, 1)
            for n, (dst, src) in enumerate(joins):
                for e in range(2):
                    act.wait_ge(joined, 2 * n + e + 1)
                    nc.scalar.activation(dst[:, 0, e].rearrange("p j d -> p (j d)"), src[e][0:DC, :], ACT.Copy,
                                         scale=1 / WS).then_inc(joined_high, 1)

            def prepared(count, dst):
                act.wait_ge(prep_ready, count)
                nc.scalar.activation(dst, prep[:], ACT.Copy).then_inc(prep_hi, 1)

            def exponent(count, k):
                act.wait_ge(shifted, count)
                nc.scalar.activation(es[:, k], es[:, k], ACT.Exp, scale=XD ** -0.5 / WS).then_inc(e_ready, 1)

            prepared(1, a16[:, 0, 0])
            prepared(2, vw16[:, 0, 0])
            prepared(3, a16[:, 1, 0])
            exponent(1, 0)
            with act.Fori(0, TILES // 4) as i:
                for j in range(4):
                    act.wait_ge(pt_ready, i * 4 + j + 1)
                    nc.scalar.activation(pt16[:, 0], turned[:], ACT.Copy).then_inc(pt_hi, 1)
                    exponent(i * 4 + j + 2, (j + 1) % 2)
                    prepared(i * 4 + j + 4, destination(j)[:, 0])

        @block.vector
        def _(dve):
            step = Chain(dve, dve_steps)
            for n in range(4):
                (hi, lo), src, scale = turned_view(n)
                dve.wait_ge(w_high, n + 1)
                if n < 3:
                    for j in range(PAIRS):
                        last = nc.vector.scalar_tensor_tensor(out=lo[:, j], in0=src[:, j], scalar=scale, in1=hi[:, j],
                                                              op0=ALU.mult, op1=ALU.subtract)
                else:
                    last = nc.vector.tensor_tensor(lo, src, hi, ALU.subtract)
                last.then_inc(w_low, 1)
            dve.wait_ge(wo_high, 1)
            nc.vector.scalar_tensor_tensor(out=wo16[:, 1], in0=wo, scalar=WS, in1=wo16[:, 0], op0=ALU.mult,
                                           op1=ALU.subtract).then_inc(w_low, 1)
            for n, (dst, src) in enumerate(joins):
                for e in range(2):
                    dve.wait_ge(joined_high, 2 * n + e + 1)
                    nc.vector.scalar_tensor_tensor(out=dst[:, 1, e].rearrange("p j d -> p (j d)"), in0=src[e][0:DC, :],
                                                   scalar=1 / WS, in1=dst[:, 0, e].rearrange("p j d -> p (j d)"),
                                                   op0=ALU.mult, op1=ALU.subtract).then_inc(joined_low, 1)
            dve.sem_inc(prep_lo, 1)
            dve.sem_inc(pt_lo, 1)
            dve.sem_inc(added, 1)

            def prepared(count, hi, lo):
                dve.wait_ge(prep_hi, count)
                nc.vector.tensor_tensor(lo, prep[:], hi, ALU.subtract).then_inc(prep_lo, 1)

            def shift(count, k):
                s = score[k][:].rearrange("p (h n) -> p h n", n=SKV)
                dve.wait_ge(scores_ready, count)
                step(nc.vector.tensor_reduce(mx[:, k], s, AX.X, ALU.max))
                step.settle()
                nc.vector.tensor_tensor(es[:, k].rearrange("p (h n) -> p h n", n=SKV), s,
                                        mx[:, k].unsqueeze(2).to_broadcast([P, XH, SKV]),
                                        ALU.subtract).then_inc(shifted, 1)

            def total(count, k):
                dve.wait_ge(e_ready, count)
                step(nc.vector.tensor_reduce(mx[:, k], es[:, k].rearrange("p (h n) -> p h n", n=SKV), AX.X, ALU.add))
                step.settle()
                nc.vector.reciprocal(rs[:, k], mx[:, k]).then_inc(recip_ready, 1)

            def copy_ctx(b):
                nc.vector.tensor_copy(ct_now[:], ct[:, :, b, :]).then_inc(ctx_copied, 1)

            dve.wait_ge(w_low, 5)
            copy_ctx(0)
            prepared(1, a16[:, 0, 0], a16[:, 0, 1])
            prepared(2, vw16[:, 0, 0], vw16[:, 0, 1])
            copy_ctx(1)
            prepared(3, a16[:, 1, 0], a16[:, 1, 1])
            shift(1, 0)
            total(1, 0)
            dve.wait_ge(bias_added, 4)
            dve.wait_ge(pad_clear, 3)
            with step.loop(TILES // 4, 8) as i:
                for j in range(4):
                    if j % 2:
                        copy_ctx(i * 2 + (j + 1) // 2 + 1)
                    shift(i * 4 + j + 2, (j + 1) % 2)
                    dve.wait_ge(pt_hi, i * 4 + j + 1)
                    nc.vector.tensor_tensor(pt16[:, 1], turned[:], pt16[:, 0], ALU.subtract).then_inc(pt_lo, 1)
                    total(i * 4 + j + 2, (j + 1) % 2)
                    dst = destination(j)
                    prepared(i * 4 + j + 4, dst[:, 0], dst[:, 1])
                    dve.wait_ge(pv_ready, i * 4 + j + 1)
                    xs = g.x[:, i * 4 + j, :]
                    nc.vector.scalar_tensor_tensor(out=xs, in0=score[(j + 1) % 2][:, 0:D], scalar=1 / WS, in1=xs,
                                                   op0=ALU.mult, op1=ALU.add).then_inc(added, 1)
            dve.wait_ge(added, TILES + 1)

        @block.tensor
        def _(pe):
            pe.wait_ge(g.cross_fetched, 96)
            for j in range(PAIRS):
                last = nc.tensor.transpose(score[0][:, j * P:j * P + P], wq[:, j * P:j * P + P], g.ident[:])
            last.then_inc(w_turned, 1)
            for src, to in ((wk, score[1]), (wv, turned)):
                for j in range(PAIRS):
                    last = nc.tensor.transpose(to[:, j * P:j * P + DC], src[:, j * P:j * P + P],
                                               g.ident[0:DC, 0:DC])
                last.then_inc(w_turned, 1)
            for m in range(B // 2):
                last = nc.tensor.transpose(prep[0:DC, m * P:m * P + P], cx[:, m], g.ident[:])
            last.then_inc(w_turned, 1)
            for dst, lhs, rhs, split in ((joins[0][1], wkt, wqt, 2), (joins[1][1], wvt, wo16, 5)):
                pe.wait_ge(w_low, split)
                for e in range(2):
                    rows = slice(XD * e, XD * e + XD)
                    for j in range(PAIRS):
                        last = product3(dst[e][0:DC, j * D:j * D + D], [lhs[rows, a, j, :] for a in range(2)],
                                        [rhs[rows, a, j, :] for a in range(2)], True, True, pe=nc.tensor)
                    last.then_inc(joined, 1)

            def prepare_a(count, b):
                pe.wait_ge(prep_lo, count)
                for n in range(XH):
                    last = product3(prep[:, n * SKV:n * SKV + SKV], [g16[:, a, n % 2, n // 2, :] for a in range(2)],
                                    [ct[:, a, b, :] for a in range(2)], True, True, pe=nc.tensor)
                last.then_inc(prep_ready, 1)

            def prepare_vw(count, copied):
                pe.wait_ge(prep_lo, count)
                pe.wait_ge(ctx_copied, copied)
                for e in range(2):
                    for n in range(2):
                        cols = slice(n * 512, n * 512 + 512)
                        last = product3(prep[SKV * e:SKV * e + SKV, cols], (ct_now[:, 0], ct_now[:, 1]),
                                        [r16[:, a, e].rearrange("p j d -> p (j d)")[:, cols] for a in range(2)],
                                        True, True, pe=nc.tensor)
                last.then_inc(prep_ready, 1)

            def scores(batch, half, buf):
                for n in range(2):
                    cols = slice(n * 512, n * 512 + 512)
                    last = product3(score[half][:, cols], [x[:, batch, PAD + half * P:PAD + half * P + P]
                                                           for x in (g.xt_hi, g.xt_lo)],
                                    [a16[:, buf, a, cols] for a in range(2)], True, True, pe=nc.tensor)
                last.then_inc(scores_ready, 1)

            pe.wait_ge(joined_low, 4)
            prepare_a(1, 0)
            prepare_vw(2, 1)
            scores(0, 0, 0)
            scores(0, 1, 0)
            prepare_a(3, 1)
            pe.wait_ge(pad_clear, 3)
            with pe.Fori(0, TILES // 4) as i:
                for j in range(4):
                    pe.wait_ge(p_ready, i * 4 + j + 1)
                    pe.wait_ge(pt_lo, i * 4 + j + 1)
                    for n in range(PAIRS):
                        last = nc.tensor.transpose(turned[:, n * P:n * P + P], es[:, j % 2, n * P:n * P + P], g.ident[:])
                    last.then_inc(pt_ready, 1)
                    if j % 2:
                        prepare_a(i * 4 + j + 4, i * 2 + (j + 3) // 2)
                    else:
                        prepare_vw(i * 4 + j + 4, i * 2 + 2 + j // 2)
                    pe.wait_ge(shifted, i * 4 + j + 1)
                    pe.wait_ge(added, i * 4 + j + 1)
                    scores(i * 2 + (j + 2) // 2, j % 2, (j + 2) // 2 % 2)
                    pe.wait_ge(pt_lo, i * 4 + j + 2)
                    pe.wait_ge(shifted, i * 4 + j + 2)
                    for n in range(PAIRS):
                        last = product3(score[(j + 1) % 2][:, 0:D], [pt16[:, a, n * P:n * P + P] for a in range(2)],
                                        [vw16[:, j // 2, a, n * D:n * D + D] for a in range(2)],
                                        n == 0, n == PAIRS - 1, pe=nc.tensor)
                    last.then_inc(pv_ready, 1)


def experts(nc, g, w):
    WS = 64.0
    GROUP = 4
    GROUPS = TILES // GROUP
    N = GROUP * P
    with ExitStack() as ctx:
        sb = lambda n, s, d: ctx.enter_context(nc.sbuf_tensor(n, s, d))
        sem = lambda n: g.semaphore(nc, n)
        gate = sb("fgate", [P, E], F32)
        gate16 = sb("fgate16", [P, 2, E], F16)
        w1, w2 = g.expert_weights()
        b1 = sb("fb1", [P, E, FT], F32)
        b1_rows = sb("fb1_rows", [E * FT, P], F32)
        b2 = sb("fb2", [2 * E, D], F32)
        b2h = sb("fb2h", [2 * E, 2, D], F16)
        comb16 = sb("fcomb16", [P, TILES, 2, E], F16)
        w1h = sb("fw1h", [P, 2, E, F], F16)
        w2h = sb("fw2h", [P, 2, E, FT, D], F16)
        rank = sb("frank", [P, E], F32)
        logits = sb("flogits", [P, TILES, E], F32)
        key = sb("fkey", [P, TILES, E], F32)
        first = sb("ffirst", [P, TILES, E], F32)
        second = sb("fsecond", [P, TILES, E], F32)
        combine = sb("fcombine", [P, TILES, E], F32)
        scaled = sb("fscaled", [P, TILES, E], F32)
        max1 = sb("fmax1", [P, TILES], F32)
        max2 = sb("fmax2", [P, TILES], F32)
        kmax = sb("fkmax", [P, TILES], F32)
        turned = sb("fturned", [2 * E, GROUPS, N], F16)
        h32 = sb("fh32", [P, 2, FT, N], F32)
        h16 = sb("fh16", [P, 2, 2, FT, N], F16)
        ph = [ctx.enter_context(nc.psum_tensor(f"fph{c}", [P, N], F32)) for c in range(FT)]
        py = [ctx.enter_context(nc.psum_tensor(f"fpy{k}", [P, N], F32)) for k in range(2)]
        pl = ctx.enter_context(nc.psum_tensor("fpl", [P, N], F32))
        loaded, split_hi, split_lo, dve_steps = sem("ff_loaded"), sem("ff_split_hi"), sem("ff_split_lo"), sem("ff_dve_steps")
        b2_high, b2_low, rank_ready, w2_scaled, w2_low = sem("ff_b2_high"), sem("ff_b2_low"), sem("ff_rank_ready"), sem("ff_w2_scaled"), sem("ff_w2_low")
        logits_ready, gap_ready, exp_ready = sem("ff_logits_ready"), sem("ff_gap_ready"), sem("ff_exp_ready")
        combined, comb_turned, comb_copied, bias_ready, bias_added = sem("ff_combined"), sem("ff_comb_turned"), sem("ff_comb_copied"), sem("ff_bias_ready"), sem("ff_bias_added")
        hidden_ready, gelu_ready, h_high, h_low = sem("ff_hidden_ready"), sem("ff_gelu_ready"), sem("ff_h_high"), sem("ff_h_low")
        y_ready, added = sem("ff_y_ready"), sem("ff_added")
        stored = sem("ff_stored")
        block = ctx.enter_context(nc.Block())
        TURNS = E * GROUPS
        PAIRS = GROUPS // 2

        @block.sync
        def _(sp):
            sp.dma_start(gate[:], w["L0_ffn_gate_w"]).then_inc(loaded, 16)
            sp.dma_start(b1_rows[:], w["L0_ffn_b1"].rearrange("e (c p) -> (e c) p", p=P)).then_inc(loaded, 16)
            for half in range(2):
                sp.dma_start(b2[half * E:half * E + E, :], w["L0_ffn_b2"]).then_inc(loaded, 16)
            y_view = g.out.rearrange("b (h p) d -> p (b h) d", p=P)
            for t in range(GROUPS):
                sp.wait_ge(added, TURNS - GROUPS + t + 1 + 2)
                at = slice(t * GROUP, (t + 1) * GROUP)
                sp.dma_start(y_view[:, at, :], g.x[:, at, :]).then_inc(stored, 16)
            sp.wait_ge(stored, 16 * GROUPS)

        @block.gpsimd
        def _(pool):
            for e in range(E):
                nc.gpsimd.memset(rank[:, e:e + 1], float(E - e)).then_inc(rank_ready, 1)
            for n in range(4):
                at = slice(n * E // 4, (n + 1) * E // 4)
                pool.wait_ge(split_hi, 2 * n + 2)
                nc.gpsimd.tensor_scalar(w2[:, at], w2[:, at], WS, None, ALU.mult).then_inc(w2_scaled, 1)
                pool.wait_ge(w2_scaled, n + 1)
                nc.gpsimd.tensor_tensor(w2h[:, 1, at], w2[:, at], w2h[:, 0, at], ALU.subtract).then_inc(w2_low, 1)

        @block.scalar
        def _(act):
            act.wait_ge(loaded, 64)
            act.wait_ge(g.expert_fetched, 16 * 8)
            nc.scalar.activation(gate16[:, 0], gate[:], ACT.Copy, scale=WS).then_inc(split_hi, 1)
            for n in range(4):
                at = slice(n * E // 4, (n + 1) * E // 4)
                nc.scalar.activation(w2h[:, 0, at], w2[:, at], ACT.Copy, scale=WS).then_inc(split_hi, 1)
                nc.scalar.activation(w1h[:, 0, at], w1[:, at], ACT.Copy, scale=WS).then_inc(split_hi, 1)
            nc.scalar.activation(b2h[:, 0], b2[:], ACT.Copy, scale=WS).then_inc(b2_high, 1)
            act.wait_ge(gap_ready, 1)
            nc.scalar.activation(max2[:], max2[:], ACT.Exp, scale=1 / WS).then_inc(exp_ready, 1)
            for t in range(GROUPS):
                act.wait_ge(comb_turned, t + 1)
                nc.scalar.activation(turned[:, t, :], py[t % 2][0:2 * E, :], ACT.Copy).then_inc(comb_copied, 1)
            act.sem_inc(gelu_ready, FT)
            with act.Fori(0, TURNS // 2) as i:
                for k in range(2):
                    turn = i * 2 + k
                    act.wait_ge(h_low, i * 4 + 2 * k + 2)
                    for c in range(FT):
                        wait_apart(act, hidden_ready, turn * FT + c + 1, g.passed)
                        nc.scalar.activation(h32[:, k, c], ph[c][:], ACT.Gelu, bias=b1[:, i // PAIRS, c:c + 1],
                                             scale=1 / WS).then_inc(gelu_ready, 1)
                        if c == FT // 2 - 1:
                            act.wait_ge(y_ready, turn + 1)
                        if c % 2:
                            at = slice(c - 1, c + 1)
                            act.wait_ge(gelu_ready, turn * FT + FT + c + 1)
                            nc.scalar.activation(h16[:, k, 0, at], h32[:, k, at], ACT.Copy).then_inc(h_high, 1)

        @block.vector
        def _(dve):
            step = Chain(dve, dve_steps)
            dve.wait_ge(split_hi, 1)
            nc.vector.scalar_tensor_tensor(out=gate16[:, 1], in0=gate[:], scalar=WS, in1=gate16[:, 0], op0=ALU.mult,
                                           op1=ALU.subtract).then_inc(split_lo, 1)
            wide = lambda a: a[:].unsqueeze(2).to_broadcast([P, TILES, E])

            def pick(one_hot, values, largest):
                step(nc.vector.tensor_reduce(largest[:], values[:], AX.X, ALU.max))
                step.settle()
                step(nc.vector.tensor_tensor(key[:], values[:], wide(largest), ALU.is_equal))
                step.settle()
                step(nc.vector.tensor_tensor(key[:], key[:], rank[:].unsqueeze(1).to_broadcast([P, TILES, E]), ALU.mult))
                step.settle()
                step(nc.vector.tensor_reduce(kmax[:], key[:], AX.X, ALU.max))
                step.settle()
                step(nc.vector.tensor_tensor(one_hot[:], key[:], wide(kmax), ALU.is_equal))
                step.settle()

            dve.wait_ge(logits_ready, 1)
            step(nc.vector.tensor_copy(logits[:].rearrange("p t e -> p (t e)"), pl[:, 0:TILES * E]))
            step(nc.vector.tensor_copy(b1[:].rearrange("p e c -> p (e c)"), pl[:, TILES * E:TILES * E + E * FT]))
            step.settle()
            dve.wait_ge(rank_ready, E)
            pick(first, logits, max1)
            step(nc.vector.scalar_tensor_tensor(out=logits[:].rearrange("p t e -> p (t e)"),
                                                in0=first[:].rearrange("p t e -> p (t e)"), scalar=-1e30,
                                                in1=logits[:].rearrange("p t e -> p (t e)"), op0=ALU.mult, op1=ALU.add))
            step.settle()
            pick(second, logits, max2)
            nc.vector.tensor_tensor(max2[:], max2[:], max1[:], ALU.subtract).then_inc(gap_ready, 1)
            dve.wait_ge(exp_ready, 1)
            step(nc.vector.tensor_scalar(max1[:], max2[:], 1.0, None, ALU.add))
            step.settle()
            step(nc.vector.reciprocal(max1[:], max1[:]))
            step.settle()
            step(nc.vector.tensor_tensor(max2[:], max2[:], max1[:], ALU.mult))
            step(nc.vector.tensor_tensor(first[:], first[:], wide(max1), ALU.mult))
            step.settle()
            step(nc.vector.tensor_tensor(second[:], second[:], wide(max2), ALU.mult))
            step.settle()
            step(nc.vector.tensor_tensor(combine[:], first[:], second[:], ALU.add))
            step.settle()
            step(nc.vector.tensor_scalar(comb16[:, :, 0], combine[:], WS, None, ALU.mult))
            step.settle()
            nc.vector.scalar_tensor_tensor(out=comb16[:, :, 1], in0=combine[:], scalar=WS, in1=comb16[:, :, 0],
                                           op0=ALU.mult, op1=ALU.subtract).then_inc(combined, 1)
            nc.vector.tensor_scalar(scaled[:], combine[:], 1 / WS, None, ALU.mult).then_inc(combined, 1)
            dve.wait_ge(b2_high, 1)
            nc.vector.scalar_tensor_tensor(out=b2h[:, 1], in0=b2[:], scalar=WS, in1=b2h[:, 0], op0=ALU.mult,
                                           op1=ALU.subtract).then_inc(b2_low, 1)
            for n in range(4):
                at = slice(n * E // 4, (n + 1) * E // 4)
                flat = lambda a: a.rearrange("p e f -> p (e f)")
                dve.wait_ge(split_hi, 2 * n + 3)
                nc.vector.scalar_tensor_tensor(out=flat(w1h[:, 1, at]), in0=flat(w1[:, at]), scalar=WS,
                                               in1=flat(w1h[:, 0, at]), op0=ALU.mult,
                                               op1=ALU.subtract).then_inc(split_lo, 1)
            for t in range(GROUPS):
                at = slice(t * GROUP, (t + 1) * GROUP)
                dve.wait_ge(bias_ready, t + 1)
                xs = g.x[:, at].rearrange("p t d -> p (t d)")
                nc.vector.scalar_tensor_tensor(out=xs, in0=ph[t % FT][:], scalar=1 / (WS * WS), in1=xs, op0=ALU.mult,
                                               op1=ALU.add).then_inc(bias_added, 1)
            dve.wait_ge(bias_added, GROUPS)
            dve.wait_ge(combined, 2)
            dve.sem_inc(added, 2)
            dve.sem_inc(h_low, 4)

            def low(turn, k):
                for n in range(2):
                    at = slice(2 * n, 2 * n + 2)
                    dve.wait_ge(h_high, turn * 2 + n + 1)
                    nc.vector.tensor_tensor(h16[:, k, 1, at], h32[:, k, at], h16[:, k, 0, at],
                                            ALU.subtract).then_inc(h_low, 1)

            def add(i, k):
                dve.wait_ge(y_ready, i * 2 + k + 3)
                for m in range(GROUP):
                    tile = (i % PAIRS) * 2 * GROUP + k * GROUP + m
                    xs = g.x[:, tile, :]
                    last = nc.vector.scalar_tensor_tensor(
                        out=xs, in0=py[k][:, m * D:m * D + D], scalar=scaled[:, tile, bass.ds(i // PAIRS, 1)],
                        in1=xs, op0=ALU.mult, op1=ALU.add)
                last.then_inc(added, 1)

            low(0, 0)
            with dve.Fori(0, TURNS // 2 - 1) as i:
                low(i * 2 + 1, 1)
                add(i, 0)
                low(i * 2 + 2, 0)
                add(i, 1)
            low(TURNS - 1, 1)
            add(TURNS // 2 - 1, 0)
            add(TURNS // 2 - 1, 1)

        @block.tensor
        def _(pe):
            pe.wait_ge(loaded, 64)
            pe.wait_ge(split_lo, 1)
            nc.tensor.transpose(pl[:, TILES * E:TILES * E + E * FT], b1_rows[:], g.ident[0:E * FT, 0:E * FT])
            for t in range(TILES):
                at = slice(PAD + t % 2 * P, PAD + t % 2 * P + P)
                last = product3(pl[:, t * E:t * E + E], (g.xt_hi[:, t // 2, at], g.xt_lo[:, t // 2, at]),
                                (gate16[:, 0], gate16[:, 1]), True, True, pe=nc.tensor)
            last.then_inc(logits_ready, 1)
            pe.wait_ge(combined, 1)
            pe.wait_ge(b2_low, 1)
            for t in range(GROUPS + 1):
                if t < GROUPS:
                    if t >= 2:
                        pe.wait_ge(comb_copied, t - 1)
                    for m in range(GROUP):
                        last = nc.tensor.matmul(py[t % 2][0:2 * E, m * P:m * P + P],
                                                comb16[:, t * GROUP + m].rearrange("p a e -> p (a e)"), g.ident16[:],
                                                start=True, stop=True)
                    last.then_inc(comb_turned, 1)
                if t >= 1:
                    n = t - 1
                    pe.wait_ge(comb_copied, n + 1)
                    if n >= FT:
                        pe.wait_ge(bias_added, n - FT + 1)
                    for m in range(GROUP):
                        for a in range(2):
                            last = nc.tensor.matmul(ph[n % FT][:, m * D:m * D + D], turned[:, n, m * P:m * P + P],
                                                    b2h[:, a], start=a == 0, stop=a == 1)
                    last.then_inc(bias_ready, 1)
            pe.wait_ge(split_lo, 5)
            pe.sem_inc(y_ready, 2)

            def hidden(i, k):
                turn, e = i * 2 + k, i // PAIRS
                batch = (i % PAIRS) * 4 + k * 2
                for c in range(FT):
                    pe.wait_ge(gelu_ready, turn * FT + c + 1)
                    w_at = lambda a: w1h[:, a, e, c * P:c * P + P]
                    product3(ph[c][:], (w_at(0), w_at(1)),
                             [x[:, bass.ds(batch, 2), PAD:PAD + L] for x in (g.xt_hi, g.xt_lo)],
                             True, True, pe=nc.tensor).then_inc(hidden_ready, 1)

            def outputs(i, k):
                turn, e = i * 2 + k, i // PAIRS
                pe.wait_ge(added, turn + 1)
                pe.wait_ge(h_low, turn * 2 + 6)
                for m in range(GROUP):
                    cols = slice(m * P, m * P + P)
                    for c in range(FT):
                        last = product3(py[k][:, m * D:m * D + D], (h16[:, k, 0, c, cols], h16[:, k, 1, c, cols]),
                                        (w2h[:, 0, e, c, :], w2h[:, 1, e, c, :]), c == 0, c == FT - 1, pe=nc.tensor)
                last.then_inc(y_ready, 1)

            pe.wait_ge(added, 2)
            hidden(0, 0)
            pe.wait_ge(w2_low, 4)
            with pe.Fori(0, TURNS // 2 - 1) as i:
                hidden(i, 1)
                outputs(i, 0)
                hidden(i + 1, 0)
                outputs(i, 1)
            hidden(TURNS // 2 - 1, 1)
            outputs(TURNS // 2 - 1, 0)
            outputs(TURNS // 2 - 1, 1)


_INS = ["x", "ctx_768"] + ["L0_attn_" + n for n in (
    "q_w", "k_w", "v_w", "b_w", "q_cw", "k_cw", "v_cw", "mlp1_w", "mlp1_b", "mlp2_w", "mlp2_b", "logit_temp",
    "conv_res_logit", "norm_w", "o_w")] + ["L0_xattn_" + n for n in ("w_q", "w_k", "w_v", "w_out", "b_out")] + [
    "L0_ffn_" + n for n in ("gate_w", "w1", "b1", "w2", "b2")]


def decoder_layer(nc, w, out):
    with ExitStack() as ctx:
        g = Shared(nc, ctx)
        g.out = out
        with ExitStack() as attention:
            g.hold_attention(nc, attention)
            with ExitStack() as weights:
                g.hold_qkv_weights(nc, weights)
                load(nc, g, w)
                norm_and_transpose(nc, g)
                project(nc, g, w)
            delta_rule(nc, g)
            with ExitStack() as branches:
                g.hold_fir(nc, branches)
                g.hold_gate_weights(nc, branches)
                fir(nc, g, w)
                gate_and_add(nc, g, w)
        g.clear_semaphores(nc)
        norm_and_transpose(nc, g, "ln2")
        cross_attention(nc, g, w)
        norm_and_transpose(nc, g, "ln3")
        experts(nc, g, w)


def kernel(**inputs):
    import numpy as np
    import concourse.bacc as bacc
    from concourse.bass_utils import run_bass_kernel_spmd

    nc = bacc.Bacc("TRN2", target_bir_lowering=False, num_devices=1)
    laid_out = {n: inputs[n] for n in _INS}
    for n in ("short", "long"):
        laid_out["fir_" + n] = lay_out_fir(inputs[f"L0_attn_fir_{n}_w"])
    arrays, w = {}, {}
    for name, value in laid_out.items():
        a = np.ascontiguousarray(value)
        arrays[f"in_{name}"] = a
        w[name] = nc.dram_tensor(f"in_{name}", a.shape, mybir.dt.from_np(a.dtype), kind="ExternalInput").ap()
    out = nc.dram_tensor("out_x", (B, L, D), F32, kind="ExternalOutput").ap()
    decoder_layer(nc, w, out)
    r = run_bass_kernel_spmd(nc, [arrays], core_ids=[0])
    return r.results[0]["out_x"]
```
